# Optimizing a Trainium2 kernel written in Bass

```python
import numpy as np
import jax
import jax.numpy as jnp

def _softmax(x, axis=-1):
    return jax.nn.softmax(x, axis=axis)

def _gelu(x):
    return jax.nn.gelu(x, approximate=True)

def _silu(x):
    return jax.nn.silu(x)

def _sigmoid(x):
    return jax.nn.sigmoid(x)

def _layernorm(x, axis=-1, eps=1e-05):
    m = jnp.mean(x, axis=axis, keepdims=True)
    v = jnp.var(x, axis=axis, keepdims=True)
    return (x - m) / jnp.sqrt(v + eps)

def _scatter_add(tgt, idx, src, axis=0):
    return tgt.at[idx].add(src)

def _segment_sum(src, seg, n):
    return jax.ops.segment_sum(src, seg, n)
kernel_name = 'mk_seq_preln_d2_jaxref_r8_74182b'

def setup_inputs(seed: int=0):
    np.random.seed(seed)
    _w = jnp.asarray

    def _L0_attn_setup():
        import jax, jax.numpy as jnp
        import numpy as np
        B, L, D, H, F = (2, 128, 128, 16, 512)
        DH = D // H
        EPS = 1e-06

        def _layernorm(x, g, b, eps=1e-05):
            m = jnp.mean(x, axis=-1, keepdims=True)
            v = jnp.mean((x - m) ** 2, axis=-1, keepdims=True)
            return (x - m) / jnp.sqrt(v + eps) * g + b

        def _decoder_layer(inputs, Wq, bq, Wk, bk, Wv, bv, Wo, bo, ln1_g, ln1_b, W1, b1, W2, b2, ln2_g, ln2_b):
            Bn, Ln, Dn = inputs.shape

            def heads(W, b):
                return (inputs @ W + b).reshape(Bn, Ln, H, DH).transpose(0, 2, 1, 3)
            q = jax.nn.sigmoid(heads(Wq, bq))
            k = jax.nn.sigmoid(heads(Wk, bk))
            v = heads(Wv, bv)
            normal = (jnp.arange(Ln, dtype=jnp.float32) + 1.0)[None, None, :]
            sink_in = normal / jnp.einsum('bhld,bhld->bhl', q + EPS, jnp.cumsum(k, axis=2) + EPS)
            src_out = normal / jnp.einsum('bhld,bhld->bhl', k + EPS, jnp.cumsum(q, axis=2) + EPS)
            cons_sink = jnp.einsum('bhld,bhld->bhl', q + EPS, jnp.cumsum(k * src_out[..., None], axis=2) + EPS) / normal
            cons_src = jnp.einsum('bhld,bhld->bhl', k + EPS, jnp.cumsum(q * sink_in[..., None], axis=2) + EPS) / normal
            cons_src = jnp.clip(cons_src, -1.0, 1.0)
            sink_alloc = jax.nn.sigmoid(cons_sink)
            cons_src = jnp.exp(cons_src)
            src_comp = cons_src / jnp.cumsum(cons_src, axis=-1) * normal
            qs = q * (sink_in / normal)[..., None]
            vs = v * src_comp[..., None]
            kv = jnp.cumsum(jnp.einsum('bhld,bhlm->bhldm', k, vs), axis=2)
            x = jnp.einsum('bhld,bhldm->bhlm', qs, kv) * sink_alloc[..., None]
            x = x.transpose(0, 2, 1, 3).reshape(Bn, Ln, Dn)
            attn = x @ Wo + bo
            h = _layernorm(inputs + attn, ln1_g, ln1_b)
            ffn = jax.nn.gelu(h @ W1 + b1, approximate=False) @ W2 + b2
            return _layernorm(h + ffn, ln2_g, ln2_b)
        key = jax.random.key(seed)
        ks = jax.random.split(key, 12)

        def w(k, shape):
            return jax.random.normal(k, shape, dtype=jnp.float32) * 0.02
        return {'inputs': jax.random.normal(ks[0], (B, L, D), dtype=jnp.float32), 'attn_mask': jnp.zeros((L, L), dtype=jnp.bool_), 'Wq': w(ks[1], (D, D)), 'bq': jnp.zeros((D,), jnp.float32), 'Wk': w(ks[2], (D, D)), 'bk': jnp.zeros((D,), jnp.float32), 'Wv': w(ks[3], (D, D)), 'bv': jnp.zeros((D,), jnp.float32), 'Wo': w(ks[4], (D, D)), 'bo': jnp.zeros((D,), jnp.float32), 'ln1_g': jnp.ones((D,), jnp.float32), 'ln1_b': jnp.zeros((D,), jnp.float32), 'W1': w(ks[5], (D, F)), 'b1': jnp.zeros((F,), jnp.float32), 'W2': w(ks[6], (F, D)), 'b2': jnp.zeros((D,), jnp.float32), 'ln2_g': jnp.ones((D,), jnp.float32), 'ln2_b': jnp.zeros((D,), jnp.float32)}
    _L0_attn_in = _L0_attn_setup()

    def _L0_ffn_setup():
        import jax, jax.numpy as jnp
        import numpy as np
        B, T, DIM, H, DH, TOPK = (4, 256, 128, 8, 64, 3)
        key = jax.random.key(seed)
        ks = jax.random.split(key, 6)
        x = jax.random.normal(ks[0], (B, T, DIM), dtype=jnp.float32)
        sc = 1.0 / np.sqrt(DIM)
        Wq = jax.random.normal(ks[1], (DIM, H * DH), dtype=jnp.float32) * sc
        Wkv = jax.random.normal(ks[2], (DIM, 2 * H * DH), dtype=jnp.float32) * sc
        Ws = jax.random.normal(ks[3], (DIM, H), dtype=jnp.float32) * sc
        Wo = jax.random.normal(ks[4], (H, DH, DIM), dtype=jnp.float32) * (1.0 / np.sqrt(DH))
        bo = jax.random.normal(ks[5], (H, DIM), dtype=jnp.float32) * 0.01
        return {'x': x, 'Wq': Wq, 'Wkv': Wkv, 'Ws': Ws, 'Wo': Wo, 'bo': bo}
    _L0_ffn_in = _L0_ffn_setup()

    def _L1_attn_setup():
        import jax, jax.numpy as jnp
        import numpy as np
        B, S, E, H = (2, 256, 128, 16)
        D = E // H
        key = jax.random.key(seed)
        k1, k2, k3 = jax.random.split(key, 3)
        x = jax.random.normal(k1, (B, S, E), dtype=jnp.float32)
        lim_qkv = np.sqrt(6.0 / (E + 3 * E)).astype(np.float32)
        lim_out = np.sqrt(6.0 / (E + E)).astype(np.float32)
        w_qkv = jax.random.uniform(k2, (E, 3 * E), jnp.float32, -lim_qkv, lim_qkv)
        w_out = jax.random.uniform(k3, (E, E), jnp.float32, -lim_out, lim_out)
        return {'x': x, 'w_qkv': w_qkv, 'w_out': w_out}
    _L1_attn_in = _L1_attn_setup()

    def _L1_ffn_setup():
        import jax, jax.numpy as jnp
        import numpy as np
        H = 128
        I = 4 * H
        E = 8
        K = 2
        B, S = (2, 128)
        STD = 0.02 / np.sqrt(H)
        key = jax.random.key(seed)
        ks = jax.random.split(key, 8)
        x = jax.random.normal(ks[0], (B, S, H), dtype=jnp.float32)
        gate_w = jax.random.normal(ks[1], (H, E), dtype=jnp.float32) * STD
        bias = jnp.zeros((E,), dtype=jnp.float32)
        up_w = jax.random.normal(ks[2], (E, H, I), dtype=jnp.float32) * STD
        up_b = jnp.zeros((E, I), dtype=jnp.float32)
        down_w = jax.random.normal(ks[3], (E, I, H), dtype=jnp.float32) * STD
        down_b = jnp.zeros((E, H), dtype=jnp.float32)
        sw_up = jax.random.normal(ks[4], (H, I), dtype=jnp.float32) * STD
        sb_up = jnp.zeros((I,), dtype=jnp.float32)
        sw_down = jax.random.normal(ks[5], (I, H), dtype=jnp.float32) * STD
        sb_down = jnp.zeros((H,), dtype=jnp.float32)
        return {'x': x, 'gate_w': gate_w, 'bias': bias, 'up_w': up_w, 'up_b': up_b, 'down_w': down_w, 'down_b': down_b, 'sw_up': sw_up, 'sb_up': sb_up, 'sw_down': sw_down, 'sb_down': sb_down}
    _L1_ffn_in = _L1_ffn_setup()
    _d = {'L0_attn_inputs': _L0_attn_in['inputs'], 'L0_attn_attn_mask': _L0_attn_in['attn_mask'], 'L0_attn_Wq': _L0_attn_in['Wq'], 'L0_attn_bq': _L0_attn_in['bq'], 'L0_attn_Wk': _L0_attn_in['Wk'], 'L0_attn_bk': _L0_attn_in['bk'], 'L0_attn_Wv': _L0_attn_in['Wv'], 'L0_attn_bv': _L0_attn_in['bv'], 'L0_attn_Wo': _L0_attn_in['Wo'], 'L0_attn_bo': _L0_attn_in['bo'], 'L0_attn_ln1_g': _L0_attn_in['ln1_g'], 'L0_attn_ln1_b': _L0_attn_in['ln1_b'], 'L0_attn_W1': _L0_attn_in['W1'], 'L0_attn_b1': _L0_attn_in['b1'], 'L0_attn_W2': _L0_attn_in['W2'], 'L0_attn_b2': _L0_attn_in['b2'], 'L0_attn_ln2_g': _L0_attn_in['ln2_g'], 'L0_attn_ln2_b': _L0_attn_in['ln2_b'], 'L0_ffn_Wq': _L0_ffn_in['Wq'], 'L0_ffn_Wkv': _L0_ffn_in['Wkv'], 'L0_ffn_Ws': _L0_ffn_in['Ws'], 'L0_ffn_Wo': _L0_ffn_in['Wo'], 'L0_ffn_bo': _L0_ffn_in['bo'], 'L1_attn_w_qkv': _L1_attn_in['w_qkv'], 'L1_attn_w_out': _L1_attn_in['w_out'], 'L1_ffn_gate_w': _L1_ffn_in['gate_w'], 'L1_ffn_bias': _L1_ffn_in['bias'], 'L1_ffn_up_w': _L1_ffn_in['up_w'], 'L1_ffn_up_b': _L1_ffn_in['up_b'], 'L1_ffn_down_w': _L1_ffn_in['down_w'], 'L1_ffn_down_b': _L1_ffn_in['down_b'], 'L1_ffn_sw_up': _L1_ffn_in['sw_up'], 'L1_ffn_sb_up': _L1_ffn_in['sb_up'], 'L1_ffn_sw_down': _L1_ffn_in['sw_down'], 'L1_ffn_sb_down': _L1_ffn_in['sb_down']}
    _x0 = _d['L0_attn_inputs']
    _d['L0_attn_inputs'] = jax.random.normal(jax.random.fold_in(jax.random.key(seed), 1), (2, 1024, 128), dtype=_x0.dtype)
    del _x0
    return _d

def reference(L0_attn_inputs, L0_attn_attn_mask, L0_attn_Wq, L0_attn_bq, L0_attn_Wk, L0_attn_bk, L0_attn_Wv, L0_attn_bv, L0_attn_Wo, L0_attn_bo, L0_attn_ln1_g, L0_attn_ln1_b, L0_attn_W1, L0_attn_b1, L0_attn_W2, L0_attn_b2, L0_attn_ln2_g, L0_attn_ln2_b, L0_ffn_Wq, L0_ffn_Wkv, L0_ffn_Ws, L0_ffn_Wo, L0_ffn_bo, L1_attn_w_qkv, L1_attn_w_out, L1_ffn_gate_w, L1_ffn_bias, L1_ffn_up_w, L1_ffn_up_b, L1_ffn_down_w, L1_ffn_down_b, L1_ffn_sw_up, L1_ffn_sb_up, L1_ffn_sw_down, L1_ffn_sb_down):

    def _L0_attn_ref(inputs, attn_mask, Wq, bq, Wk, bk, Wv, bv, Wo, bo, ln1_g, ln1_b, W1, b1, W2, b2, ln2_g, ln2_b):
        import jax, jax.numpy as jnp
        import numpy as np
        B, L, D, H, F = (2, 128, 128, 16, 512)
        DH = D // H
        EPS = 1e-06

        def _layernorm(x, g, b, eps=1e-05):
            m = jnp.mean(x, axis=-1, keepdims=True)
            v = jnp.mean((x - m) ** 2, axis=-1, keepdims=True)
            return (x - m) / jnp.sqrt(v + eps) * g + b

        def _decoder_layer(inputs, Wq, bq, Wk, bk, Wv, bv, Wo, bo, ln1_g, ln1_b, W1, b1, W2, b2, ln2_g, ln2_b):
            Bn, Ln, Dn = inputs.shape

            def heads(W, b):
                return (inputs @ W + b).reshape(Bn, Ln, H, DH).transpose(0, 2, 1, 3)
            q = jax.nn.sigmoid(heads(Wq, bq))
            k = jax.nn.sigmoid(heads(Wk, bk))
            v = heads(Wv, bv)
            normal = (jnp.arange(Ln, dtype=jnp.float32) + 1.0)[None, None, :]
            sink_in = normal / jnp.einsum('bhld,bhld->bhl', q + EPS, jnp.cumsum(k, axis=2) + EPS)
            src_out = normal / jnp.einsum('bhld,bhld->bhl', k + EPS, jnp.cumsum(q, axis=2) + EPS)
            cons_sink = jnp.einsum('bhld,bhld->bhl', q + EPS, jnp.cumsum(k * src_out[..., None], axis=2) + EPS) / normal
            cons_src = jnp.einsum('bhld,bhld->bhl', k + EPS, jnp.cumsum(q * sink_in[..., None], axis=2) + EPS) / normal
            cons_src = jnp.clip(cons_src, -1.0, 1.0)
            sink_alloc = jax.nn.sigmoid(cons_sink)
            cons_src = jnp.exp(cons_src)
            src_comp = cons_src / jnp.cumsum(cons_src, axis=-1) * normal
            qs = q * (sink_in / normal)[..., None]
            vs = v * src_comp[..., None]
            kv = jnp.cumsum(jnp.einsum('bhld,bhlm->bhldm', k, vs), axis=2)
            x = jnp.einsum('bhld,bhldm->bhlm', qs, kv) * sink_alloc[..., None]
            x = x.transpose(0, 2, 1, 3).reshape(Bn, Ln, Dn)
            attn = x @ Wo + bo
            h = _layernorm(inputs + attn, ln1_g, ln1_b)
            ffn = jax.nn.gelu(h @ W1 + b1, approximate=False) @ W2 + b2
            return _layernorm(h + ffn, ln2_g, ln2_b)
        return _decoder_layer(inputs, Wq, bq, Wk, bk, Wv, bv, Wo, bo, ln1_g, ln1_b, W1, b1, W2, b2, ln2_g, ln2_b)

    def _L0_ffn_ref(x, Wq, Wkv, Ws, Wo, bo):
        import jax, jax.numpy as jnp
        import numpy as np
        B, T, DIM, H, DH, TOPK = (4, 256, 128, 8, 64, 3)
        b, t, _ = x.shape
        s = jax.nn.sigmoid(x @ Ws)
        vals, idx = jax.lax.top_k(s, TOPK)
        bi = jnp.arange(b)[:, None, None]
        ti = jnp.arange(t)[None, :, None]
        scores = jnp.zeros_like(s).at[bi, ti, idx].set(vals)
        q = (x @ Wq).reshape(b, t, H, DH).transpose(0, 2, 1, 3)
        kv = (x @ Wkv).reshape(b, t, 2, H, DH).transpose(2, 0, 3, 1, 4)
        k, v = (kv[0], kv[1])
        scale = DH ** (-0.5)
        attn = jax.nn.softmax(jnp.einsum('bhid,bhjd->bhij', q * scale, k), axis=-1)
        out = jnp.einsum('bhij,bhjd->bhid', attn, v)
        proj = jnp.einsum('bhtd,hde->bhte', out, Wo) + bo[None, :, None, :]
        return jnp.einsum('bhte,bth->bte', proj, scores)

    def _L1_attn_ref(x, w_qkv, w_out):
        import jax, jax.numpy as jnp
        import numpy as np
        B, S, E, H = (2, 256, 128, 16)
        D = E // H
        b, s, e = x.shape
        qkv = jnp.einsum('bse,ef->bsf', x, w_qkv)
        qkv = qkv.reshape(b, s, 3, H, D).transpose(2, 0, 3, 1, 4)
        q, k, v = (qkv[0], qkv[1], qkv[2])
        scale = 1.0 / np.sqrt(D).astype(np.float32)
        scores = jnp.einsum('bhsd,bhtd->bhst', q, k) * scale
        attn = jax.nn.softmax(scores, axis=-1)
        out = jnp.einsum('bhst,bhtd->bhsd', attn, v)
        out = out.transpose(0, 2, 1, 3).reshape(b, s, e)
        return jnp.einsum('bse,ef->bsf', out, w_out)

    def _L1_ffn_ref(x, gate_w, bias, up_w, up_b, down_w, down_b, sw_up, sb_up, sw_down, sb_down):
        import jax, jax.numpy as jnp
        import numpy as np
        H = 128
        I = 4 * H
        E = 8
        K = 2
        B, S = (2, 128)
        STD = 0.02 / np.sqrt(H)
        b, s, h = x.shape
        xf = x.reshape(-1, h)
        T = xf.shape[0]
        scores = jax.nn.sigmoid(xf @ gate_w + bias)
        top_scores, top_idx = jax.lax.top_k(scores, K)
        top_scores = top_scores / (jnp.sum(top_scores, axis=-1, keepdims=True) + 1e-06)
        w = jnp.zeros((T, E), dtype=xf.dtype).at[jnp.arange(T)[:, None], top_idx].add(top_scores)
        up = jnp.einsum('th,ehi->tei', xf, up_w) + up_b
        hact = jax.nn.gelu(up, approximate=False)
        eo = jnp.einsum('tei,eih->teh', hact, down_w) + down_b
        combined = jnp.einsum('teh,te->th', eo * 0.1, w)
        shared = (jax.nn.gelu(xf @ sw_up + sb_up, approximate=False) @ sw_down + sb_down) * 0.1
        out = (shared + combined).reshape(b, s, h)
        out = out / (jnp.max(jnp.abs(out), axis=-1, keepdims=True) + 1e-06)
        return out
    x = L0_attn_inputs
    x = x + _L0_attn_ref(_layernorm(x, axis=-1), L0_attn_attn_mask, L0_attn_Wq, L0_attn_bq, L0_attn_Wk, L0_attn_bk, L0_attn_Wv, L0_attn_bv, L0_attn_Wo, L0_attn_bo, L0_attn_ln1_g, L0_attn_ln1_b, L0_attn_W1, L0_attn_b1, L0_attn_W2, L0_attn_b2, L0_attn_ln2_g, L0_attn_ln2_b)
    x = x + _L0_ffn_ref(_layernorm(x, axis=-1), L0_ffn_Wq, L0_ffn_Wkv, L0_ffn_Ws, L0_ffn_Wo, L0_ffn_bo)
    x = x + _L1_attn_ref(_layernorm(x, axis=-1), L1_attn_w_qkv, L1_attn_w_out)
    x = x + _L1_ffn_ref(_layernorm(x, axis=-1), L1_ffn_gate_w, L1_ffn_bias, L1_ffn_up_w, L1_ffn_up_b, L1_ffn_down_w, L1_ffn_down_b, L1_ffn_sw_up, L1_ffn_sb_up, L1_ffn_sw_down, L1_ffn_sb_down)
    return x

_drawn_inputs = setup_inputs


def setup_inputs(seed=0):
    import zlib

    import numpy as np

    out = dict(_drawn_inputs(seed))
    spreads = {'L0_attn_bq': (0.0, 2.0),
     'L0_attn_bk': (0.0, 2.0),
     'L0_attn_bv': (0.0, 0.679),
     'L0_attn_bo': (0.0, 0.1),
     'L0_attn_ln1_g': (1.0, 0.2),
     'L0_attn_ln1_b': (0.0, 0.1),
     'L0_attn_b1': (0.0, 0.486),
     'L0_attn_b2': (0.0, 0.1),
     'L0_attn_ln2_g': (1.0, 0.2),
     'L0_attn_ln2_b': (0.0, 0.1),
     'L1_ffn_bias': (0.0, 0.1),
     'L1_ffn_up_b': (0.0, 0.8),
     'L1_ffn_down_b': (0.0, 0.1),
     'L1_ffn_sb_up': (0.0, 0.8),
     'L1_ffn_sb_down': (0.0, 0.1)}
    factors = {'L0_attn_Wq': 8.0,
     'L0_attn_Wk': 8.0,
     'L0_attn_Wv': 8.0,
     'L0_attn_Wo': 5.484,
     'L0_ffn_bo': 8.0,
     'L1_ffn_up_w': 23.785,
     'L1_ffn_down_w': 8.0,
     'L1_ffn_sw_up': 8.0,
     'L1_ffn_sw_down': 8.0}
    for name, (base, spread) in spreads.items():
        noise = np.random.default_rng([zlib.crc32(name.encode()), seed]).standard_normal(out[name].shape)
        drawn = base * np.exp(spread * noise) if base else spread * noise
        out[name] = jnp.asarray(drawn.astype(out[name].dtype))
    for name, factor in factors.items():
        out[name] = (out[name] * factor).astype(out[name].dtype)
    return out
```

```python
from contextlib import ExitStack

import concourse.bass as bass
from concourse import mybir

ALU = mybir.AluOpType
ACT = mybir.ActivationFunctionType
AX = mybir.AxisListType
F32 = mybir.dt.float32
F32R = mybir.dt.float32r
BF16 = mybir.dt.bfloat16

P = 128
BATCH = 2
SEQ = 1024
TOK = BATCH * SEQ
TILES = TOK // P
STILES = SEQ // P
D = 128
BANK = 512
QUARTERS = TOK // BANK
PER_Q = BANK // P
EPS_LN = 1e-5


class Phase:

    sems = None

    def __init__(self, nc, ctx, tag):
        self.nc, self.ctx, self.tag = nc, ctx, tag

    def sb(self, name, shape, dt=F32):
        return self.ctx.enter_context(self.nc.sbuf_tensor(f"{self.tag}_{name}", shape, dt))

    def sem(self, name):
        sem = self.nc.alloc_semaphore(f"{self.tag}_{name}")
        Phase.sems.append(sem)
        return sem


def clear_semaphores(nc):
    with nc.Block() as block:
        @block.gpsimd
        def _(pool):
            for sem in Phase.sems:
                pool.sem_clear(sem)
    for sem in Phase.sems:
        nc.release_semaphore(sem)
    Phase.sems = []


def f32(ap):
    return ap.bitcast(F32)


def quarter(q):
    return slice(q * BANK, (q + 1) * BANK)


def tile(t):
    return slice(t * P, (t + 1) * P)


def split_product(pe, out, a_hi, a_lo, b_hi, b_lo, start=True, stop=True):
    pe.matmul(out, a_hi, b_hi, start=start, stop=False, skip_group_check=True)
    pe.matmul(out, a_hi, b_lo, start=False, stop=False, skip_group_check=True)
    return pe.matmul(out, a_lo, b_hi, start=False, stop=stop, skip_group_check=True)


class Norm:

    def __init__(self, ph, name, src, dst, channels=None):
        self.src, self.dst, self.channels = src, dst, channels
        self.stats = ph.sb(f"{name}_stats", [P, TILES, 6])
        self.moments = ph.sb(f"{name}_moments", [P, TILES, 2])
        self.std = ph.sb(f"{name}_std", [P, TILES])
        self.rstd = ph.sb(f"{name}_rstd", [P, TILES])
        self.eps = ph.sb(f"{name}_eps", [P, 1])
        self.eps_ready = ph.sem(f"{name}_eps_ready")
        self.stats_ready = ph.sem(f"{name}_stats_ready")
        self.moments_ready = ph.sem(f"{name}_moments_ready")
        self.std_ready = ph.sem(f"{name}_std_ready")
        self.rstd_ready = ph.sem(f"{name}_rstd_ready")
        self.normed = ph.sem(f"{name}_normed")

    def vector(self, dve):
        dve.memset(self.eps[:, :], EPS_LN).then_inc(self.eps_ready, 1)
        for t in range(TILES):
            dve.bn_stats(self.stats[:, t, :], self.src[:, t, :]).then_inc(self.stats_ready, 1)
        for t in range(TILES):
            dve.wait_ge(self.stats_ready, t + 1)
            dve.bn_aggr(self.moments[:, t, :], self.stats[:, t, :]).then_inc(self.moments_ready, 1)
        for q in range(QUARTERS):
            dve.wait_ge(self.std_ready, q + 1)
            part = slice(q * PER_Q, (q + 1) * PER_Q)
            dve.reciprocal(self.rstd[:, part], self.std[:, part]).then_inc(self.rstd_ready, 1)
            dve.wait_ge(self.rstd_ready, q + 1)
            for t in range(q * PER_Q, (q + 1) * PER_Q):
                dve.tensor_scalar(self.dst[:, t, :], self.src[:, t, :], self.moments[:, t, 0:1],
                                  self.rstd[:, t:t + 1], ALU.subtract, ALU.mult).then_inc(self.normed, 1)

    def scalar(self, act):
        act.wait_ge(self.eps_ready, 1)
        for q in range(QUARTERS):
            part = slice(q * PER_Q, (q + 1) * PER_Q)
            act.wait_ge(self.moments_ready, (q + 1) * PER_Q)
            act.activation(self.std[:, part], self.moments[:, part, 1], ACT.Sqrt,
                           bias=self.eps[:, 0:1]).then_inc(self.std_ready, 1)


class Turn:

    def __init__(self, ph, name, psum, ident, view, hi, lo, ready, bank=0):
        self.psum, self.ident, self.view, self.hi, self.lo = psum, ident, view, hi, lo
        self.ready, self.bank = ready, bank
        self.turned = ph.sem(f"{name}_turned")
        self.hi_ready = ph.sem(f"{name}_hi_ready")
        self.lo_ready = ph.sem(f"{name}_lo_ready")

    def tensor(self, pe):
        for q in range(QUARTERS):
            self.ready(pe, q)
            for i in range(PER_Q):
                last = pe.transpose(self.psum[:, self.bank + q, tile(i)], self.view(q * PER_Q + i),
                                    self.ident)
            last.then_inc(self.turned, 1)

    def scalar(self, act):
        for q in range(QUARTERS):
            act.wait_ge(self.turned, q + 1)
            act.activation(self.hi[:, quarter(q)], self.psum[:, self.bank + q, :],
                           ACT.Copy).then_inc(self.hi_ready, 1)

    def vector(self, dve):
        for q in range(QUARTERS):
            dve.wait_ge(self.hi_ready, q + 1)
            dve.tensor_tensor(self.lo[:, quarter(q)], self.psum[:, self.bank + q, :],
                              f32(self.hi[:, quarter(q)]), ALU.subtract).then_inc(self.lo_ready, 1)


def split_weights(pool, pairs, loaded, hi_ready, lo_ready):
    for n, (raw, hi, lo, at) in enumerate(pairs):
        pool.wait_ge(loaded, at)
        pool.tensor_copy(hi, raw).then_inc(hi_ready, 1)
        pool.wait_ge(hi_ready, n + 1)
        pool.tensor_tensor(lo, raw, f32(hi), ALU.subtract).then_inc(lo_ready, 1)


def choose(dve, scores, beats, ties, rank, chosen, before, n, k, step):
    full = [P, TILES, n, n]
    mine = scores[:, :, :].unsqueeze(3).to_broadcast(full)
    other = scores[:, :, :].unsqueeze(2).to_broadcast(full)
    dve.tensor_tensor(beats[:, :, :, :], other, mine, ALU.is_gt).then_inc(step, 1)
    dve.tensor_tensor(ties[:, :, :, :], other, mine, ALU.is_equal).then_inc(step, 1)
    dve.wait_ge(step, 2)
    dve.tensor_tensor(ties[:, :, :, :], ties[:, :, :, :], before.unsqueeze(1).to_broadcast(full),
                      ALU.mult).then_inc(step, 1)
    dve.wait_ge(step, 3)
    dve.tensor_tensor(beats[:, :, :, :], beats[:, :, :, :], ties[:, :, :, :], ALU.add).then_inc(step, 1)
    dve.wait_ge(step, 4)
    dve.tensor_reduce(rank[:, :, :], beats[:, :, :, :], AX.X, ALU.add).then_inc(step, 1)
    dve.wait_ge(step, 5)
    dve.scalar_tensor_tensor(chosen[:, :, :], rank[:, :, :], float(k), scores[:, :, :],
                             ALU.is_lt, ALU.mult).then_inc(step, 1)


def project_and_add(nc, ctx, ph, psum, turn, X, factors, gather):
    gathered, attended, gathered_ready, G = gather
    out_done, added = ph.sem("out_done"), ph.sem("added")
    block = ctx.enter_context(nc.Block())
    per_batch = QUARTERS // BATCH

    @block.scalar
    def _(act):
        turn.scalar(act)

    @block.tensor
    def _(pe):
        turn.tensor(pe)
        for q in range(QUARTERS):
            pe.wait_ge(turn.lo_ready, q + 1)
            for i in range(PER_Q):
                t = q * PER_Q + i
                for n, (a_hi, a_lo, w_hi, w_lo) in enumerate(factors):
                    last = split_product(pe, psum[:, 4 + q, tile(i)], a_hi[:, tile(t)], a_lo[:, tile(t)], w_hi, w_lo,
                                         start=(n == 0), stop=(n == len(factors) - 1))
            last.then_inc(out_done, 1)

    @block.vector
    def _(dve):
        for q in range(QUARTERS):
            b, s0 = q // per_batch, q % per_batch * PER_Q
            for a in range(G):
                last = dve.tensor_copy(gathered[:, q * PER_Q:(q + 1) * PER_Q, a * D // G:(a + 1) * D // G],
                                       attended[:, b * G + a, s0:s0 + PER_Q, :])
            last.then_inc(gathered_ready, 1)
        turn.vector(dve)
        for q in range(QUARTERS):
            dve.wait_ge(out_done, q + 1)
            part = X[:, q * PER_Q:(q + 1) * PER_Q, :]
            dve.tensor_tensor(part, part, psum[:, 4 + q, :].rearrange("p (t d) -> p t d", d=D),
                              ALU.add).then_inc(added, 1)


def flow_phase(nc, psum, X, C, io, const):
    H, DH, EPS = 16, 8, 1e-6
    PARTS = ((0, 0), (0, 1), (0, 2), (1, 0), (1, 1), (2, 0))
    ROWS = len(PARTS) * DH
    NW = 4
    VW = D + DH
    HID = io["L0_attn_W1"].shape[1]
    FB = HID // P
    PERB = QUARTERS // BATCH
    parts_dram = nc.dram_tensor("flow_parts_scratch", [2, 3, P, TOK], BF16, kind="Internal").ap()

    with ExitStack() as ctx:
        ph = Phase(nc, ctx, "flow")
        U = ph.sb("U", [P, TILES, D])
        Y = ph.sb("Y", [P, TILES, D])
        wo_raw = ph.sb("wo_raw", [P, D])
        w1_raw, w1_hi, w1_lo = ph.sb("w1_raw", [P, HID]), ph.sb("w1_hi", [P, HID], F32R), ph.sb("w1_lo", [P, HID], F32R)
        w2_raw = ph.sb("w2_raw", [P, FB, D])
        columns = ph.sb("columns", [P, 4])
        b1 = ph.sb("b1", [P, FB])
        rows = ph.sb("rows", [P, 5, D])

        with ExitStack() as ctx_a:
            pa = Phase(nc, ctx_a, "flow_att")
            qT, kT, vT = (pa.sb(n, [P, TOK]) for n in ("qT", "kT", "vT"))
            FAC = pa.sb("FAC", [P, TOK])

            with ExitStack() as ctx1:
                p1 = Phase(nc, ctx1, "flow_in")
                UH, UL = p1.sb("UH", [P, TOK], F32R), p1.sb("UL", [P, TOK], F32R)
                w_raw, w_hi, w_lo = p1.sb("w_raw", [P, 3 * D]), p1.sb("w_hi", [P, 3 * D], F32R), p1.sb("w_lo", [P, 3 * D], F32R)
                part = p1.sb("part", [P, 2, 3, TOK], BF16)
                rest = p1.sb("rest", [P, 2, BANK])
                norm = Norm(p1, "norm", X, U)
                turn = Turn(p1, "turn", psum, C["ident"], lambda t: U[:, t, :], UH, UL,
                            lambda pe, q: pe.wait_ge(norm.normed, (q + 1) * PER_Q))
                w_loaded, rows_loaded = p1.sem("w_loaded"), p1.sem("rows_loaded")
                hi_ready, lo_ready = p1.sem("hi_ready"), p1.sem("lo_ready")
                projected, activated = p1.sem("projected"), p1.sem("activated")
                hi_taken, rest_ready, mid_taken, low_taken = (p1.sem(n) for n in ("hi_taken", "rest_ready", "mid_taken", "low_taken"))
                parts_stored = p1.sem("parts_stored")
                block = ctx1.enter_context(nc.Block())

                @block.sync
                def _(sp):
                    for n, name in enumerate(("Wq", "Wk", "Wv")):
                        sp.dma_start(w_raw[:, tile(n)], io[f"L0_attn_{name}"]).then_inc(w_loaded, 16)
                    sp.dma_start(w1_raw[:, :], io["L0_attn_W1"]).then_inc(w_loaded, 16)
                    with nc.allow_non_contiguous_dma(reason="bias columns"):
                        for n, name in enumerate(("bq", "bk", "bv", "b2")):
                            sp.dma_start(columns[:, n:n + 1], io[f"L0_attn_{name}"].rearrange("(p a) -> p a", a=1)).then_inc(rows_loaded, 16)
                        sp.dma_start(b1[:, :], io["L0_attn_b1"].rearrange("(a p) -> p a", p=P)).then_inc(rows_loaded, 16)
                    for n, name in enumerate(("bo", "ln1_g", "ln1_b", "ln2_g", "ln2_b")):
                        sp.dma_start(rows[:, n, :], io[f"L0_attn_{name}"].partition_broadcast(P)).then_inc(rows_loaded, 16)
                    sp.dma_start(wo_raw[:, :], io["L0_attn_Wo"]).then_inc(rows_loaded, 16)
                    sp.dma_start(w2_raw[:, :, :], io["L0_attn_W2"].rearrange("(a p) n -> p a n", p=P)).then_inc(rows_loaded, 16)
                    for m in range(2):
                        sp.wait_ge(low_taken, (m + 1) * QUARTERS)
                        sp.dma_start(parts_dram[m].rearrange("s p t -> p s t"), part[:, m, :, :]).then_inc(parts_stored, 16)
                    sp.wait_ge(parts_stored, 32)
                    sp.wait_ge(rows_loaded, 16 * 12)

                @block.gpsimd
                def _(pool):
                    split_weights(pool, [(w_raw[:, :], w_hi[:, :], w_lo[:, :], 64),
                                         (w1_raw[:, :], w1_hi[:, :], w1_lo[:, :], 64)], w_loaded, hi_ready, lo_ready)
                    for k in range(2 * QUARTERS):
                        m, q = k // QUARTERS, k % QUARTERS
                        pool.wait_ge(mid_taken, k + 1)
                        pool.tensor_tensor(part[:, m, 2, quarter(q)], rest[:, k % 2, :], part[:, m, 1, quarter(q)],
                                           ALU.subtract).then_inc(low_taken, 1)

                @block.tensor
                def _(pe):
                    turn.tensor(pe)
                    pe.wait_ge(lo_ready, 1)
                    pe.wait_ge(turn.lo_ready, QUARTERS)
                    for m in range(3):
                        for q in range(QUARTERS):
                            k = m * QUARTERS + q
                            if k >= 4:
                                pe.wait_ge(activated, k - 3)
                            split_product(pe, psum[:, 4 + k % 4, :], w_hi[:, tile(m)], w_lo[:, tile(m)],
                                          UH[:, quarter(q)], UL[:, quarter(q)]).then_inc(projected, 1)

                @block.scalar
                def _(act):
                    norm.scalar(act)
                    turn.scalar(act)
                    act.wait_ge(rows_loaded, 16 * 12)
                    for m, dst in enumerate((qT, kT, vT)):
                        for q in range(QUARTERS):
                            k = m * QUARTERS + q
                            act.wait_ge(projected, k + 1)
                            act.activation(dst[:, quarter(q)], psum[:, 4 + k % 4, :],
                                           ACT.Sigmoid if m < 2 else ACT.Identity,
                                           bias=columns[:, m:m + 1]).then_inc(activated, 1)
                    for k in range(2 * QUARTERS):
                        m, q = k // QUARTERS, k % QUARTERS
                        act.activation(part[:, m, 0, quarter(q)], (qT, kT)[m][:, quarter(q)], ACT.Copy).then_inc(hi_taken, 1)
                        act.wait_ge(rest_ready, k + 1)
                        act.activation(part[:, m, 1, quarter(q)], rest[:, k % 2, :], ACT.Copy).then_inc(mid_taken, 1)

                @block.vector
                def _(dve):
                    norm.vector(dve)
                    turn.vector(dve)
                    for k in range(2 * QUARTERS):
                        m, q = k // QUARTERS, k % QUARTERS
                        dve.wait_ge(hi_taken, k + 1)
                        if k >= 2:
                            dve.wait_ge(low_taken, k - 1)
                        dve.tensor_tensor(rest[:, k % 2, :], (qT, kT)[m][:, quarter(q)], part[:, m, 0, quarter(q)],
                                          ALU.subtract).then_inc(rest_ready, 1)

            qs = pa.sb("qs", [ROWS, 2, H, BANK], BF16)
            ks = pa.sb("ks", [ROWS, 2, H, BANK], BF16)
            stacked = [pa.sem(f"stacked{i}") for i in range(2)]

            def load_stacks(sp, q):
                for r, (qp, kp) in enumerate(PARTS):
                    for st, m, s in ((ks, 1, kp), (qs, 0, qp)):
                        sp.dma_start(st[r * DH:(r + 1) * DH, q % 2, :, :],
                                     parts_dram[m, s][:, quarter(q)].rearrange("(h d) t -> d h t", d=DH)).then_inc(stacked[q % 2], 16)

            with ExitStack() as ctx2:
                p2 = Phase(nc, ctx2, "flow_mass")
                cum = p2.sb("cum", [P, 2, SEQ])
                prod = p2.sb("prod", [P, TOK])
                sums_w = p2.sb("sums_w", [P, 32])
                spread = p2.sb("spread", [P, P])
                carry_w = p2.sb("carry_w", [P, P])
                normal, inv_normal = p2.sb("normal", [P, BANK]), p2.sb("inv_normal", [P, BANK])
                zeros = p2.sb("zeros", [P, 1])
                r_sink, sink, src = (p2.sb(n, [P, BANK]) for n in ("r_sink", "sink", "src"))
                scratch = p2.sb("scratch", [P, BANK])
                take, give = p2.sb("take", [P, BANK]), p2.sb("give", [P, BANK])
                cum_give = p2.sb("cum_give", [P, BANK])
                alloc = p2.sb("alloc", [P, BANK])
                c_loaded = p2.sem("c_loaded")
                step = p2.sem("step")
                summed, spreaded, act_step = p2.sem("summed"), p2.sem("spreaded"), p2.sem("act_step")
                block = ctx2.enter_context(nc.Block())

                AT = {}

                @block.sync
                def _(sp):
                    for name, dst in (("sums_w", sums_w), ("spread", spread), ("carry_w", carry_w),
                                      ("normal", normal), ("inv_normal", inv_normal)):
                        sp.dma_start(dst[:, :], const[name]).then_inc(c_loaded, 16)
                    for q in range(2):
                        load_stacks(sp, q)

                @block.vector
                def _(dve):
                    count = [0]

                    def done(ins, name=None):
                        count[0] += 1
                        ins.then_inc(step, 1)
                        dve.wait_ge(step, count[0])
                        if name:
                            AT[name] = count[0]

                    def flow(x, y, name, carried=None):
                        for b in range(BATCH):
                            cols = slice(b * SEQ, (b + 1) * SEQ)
                            done(dve.tensor_tensor_scan(cum[:, b, :], y[:, cols], y[:, cols], EPS, ALU.add, ALU.bypass))
                            if b == 0 and carried is not None:
                                dve.wait_ge(summed, carried)
                            done(dve.scalar_tensor_tensor(prod[:, cols], x[:, cols], EPS, cum[:, b, :], ALU.add, ALU.mult), name)

                    dve.wait_ge(c_loaded, 16 * 5)
                    flow(qT, kT, "p1")
                    flow(kT, qT, "p2", carried=1)
                    dve.wait_ge(summed, 1)
                    done(dve.reciprocal(r_sink[:, :], psum[:, 0, :]))
                    done(dve.tensor_tensor(sink[:, :], r_sink[:, :], normal[:, :], ALU.mult), "sink")
                    dve.wait_ge(summed, 2)
                    done(dve.reciprocal(src[:, :], psum[:, 1, :]))
                    done(dve.tensor_tensor(src[:, :], src[:, :], normal[:, :], ALU.mult), "src")
                    for n, (x, y) in enumerate(((kT, qT), (qT, kT))):
                        dve.wait_ge(spreaded, n + 1)
                        dve.wait_ge(summed, 2 + n)
                        for q in range(QUARTERS):
                            done(dve.tensor_tensor(prod[:, quarter(q)], x[:, quarter(q)], psum[:, 2 + q, :], ALU.mult), f"used{n}")
                        for b in range(BATCH):
                            cols = slice(b * SEQ, (b + 1) * SEQ)
                            done(dve.tensor_tensor_scan(cum[:, b, :], prod[:, cols], prod[:, cols], EPS, ALU.add, ALU.bypass))
                        for b in range(BATCH):
                            cols = slice(b * SEQ, (b + 1) * SEQ)
                            done(dve.scalar_tensor_tensor(prod[:, cols], y[:, cols], EPS, cum[:, b, :], ALU.add, ALU.mult), f"p{n + 3}")
                    dve.wait_ge(summed, 3)
                    done(dve.tensor_tensor(take[:, :], psum[:, 0, :], inv_normal[:, :], ALU.mult), "take")
                    dve.wait_ge(summed, 4)
                    done(dve.tensor_tensor(scratch[:, :], psum[:, 1, :], inv_normal[:, :], ALU.mult))
                    done(dve.tensor_scalar(give[:, :], scratch[:, :], 1.0, -1.0, ALU.min, ALU.max), "give")
                    dve.wait_ge(act_step, 2)
                    done(dve.tensor_tensor_scan(cum_give[:, :], give[:, :], give[:, :], 0.0, ALU.add, ALU.bypass), "cum_give")
                    dve.wait_ge(summed, 5)
                    done(dve.tensor_copy(zeros[:, :], psum[:, 0, 0:1]))
                    done(dve.tensor_scalar(scratch[:, :], cum_give[:, :], zeros[:, 0:1], None, ALU.add))
                    done(dve.reciprocal(cum_give[:, :], scratch[:, :]))
                    done(dve.tensor_tensor(scratch[:, :], give[:, :], cum_give[:, :], ALU.mult))
                    done(dve.tensor_tensor(give[:, :], scratch[:, :], normal[:, :], ALU.mult), "comp")
                    done(dve.tensor_tensor(r_sink[:, :], r_sink[:, :], alloc[:, :], ALU.mult), "fac")
                    dve.wait_ge(spreaded, 3)
                    for q in range(QUARTERS):
                        done(dve.tensor_tensor(vT[:, quarter(q)], vT[:, quarter(q)], psum[:, 2 + q, :], ALU.mult), "vs")
                    dve.wait_ge(spreaded, 4)
                    for q in range(QUARTERS):
                        done(dve.tensor_copy(FAC[:, quarter(q)], psum[:, 2 + q, :]))

                @block.tensor
                def _(pe):
                    pe.wait_ge(c_loaded, 16 * 5)

                    def head_sums(bank, name):
                        pe.wait_ge(step, AT[name])
                        for q in range(QUARTERS):
                            last = pe.matmul(psum[32 * q:32 * q + 32, bank, :], sums_w[:, :], prod[:, quarter(q)],
                                             start=True, stop=True, skip_group_check=True)
                        last.then_inc(summed, 1)

                    def to_channels(src_rows, name, free=None):
                        pe.wait_ge(step, AT[name])
                        if free:
                            pe.wait_ge(step, AT[free])
                        for q in range(QUARTERS):
                            rows_q = slice(32 * q, 32 * q + 32)
                            last = pe.matmul(psum[:, 2 + q, :], spread[rows_q, :], src_rows[rows_q, :],
                                             start=True, stop=True, skip_group_check=True)
                        last.then_inc(spreaded, 1)

                    head_sums(0, "p1")
                    head_sums(1, "p2")
                    to_channels(src, "src")
                    pe.wait_ge(step, AT["sink"])
                    head_sums(0, "p3")
                    to_channels(sink, "sink", "used0")
                    head_sums(1, "p4")
                    pe.wait_ge(step, AT["cum_give"])
                    pe.matmul(psum[:, 0, 0:1], carry_w[:, :], cum_give[:, BANK - 1:BANK], start=True, stop=True,
                              skip_group_check=True).then_inc(summed, 1)
                    to_channels(give, "comp")
                    to_channels(r_sink, "fac", "vs")

                @block.scalar
                def _(act):
                    act.wait_ge(step, AT["take"])
                    act.activation(alloc[:, :], take[:, :], ACT.Sigmoid).then_inc(act_step, 1)
                    act.wait_ge(step, AT["give"])
                    act.activation(give[:, :], give[:, :], ACT.Exp).then_inc(act_step, 1)

            with ExitStack() as ctx3:
                p3 = Phase(nc, ctx3, "flow_mix")
                k_tok = p3.sb("k_tok", [P, 2, PER_Q, D])
                v_tok = p3.sb("v_tok", [P, 2, PER_Q, D])
                v_one = p3.sb("v_one", [P, 2, NW * VW])
                causal = p3.sb("causal", [P, P])
                blocks = p3.sb("blocks", [P, P])
                masked = p3.sb("masked", [P, 2, H, P])
                state = p3.sb("state", [P, 2, P])
                mixed_t = p3.sb("mixed_t", [P, 2, P])
                c_loaded = p3.sem("c_loaded")
                v_zero, v_placed = p3.sem("v_zero"), p3.sem("v_placed")
                turned, tok_copied = p3.sem("turned"), p3.sem("tok_copied")
                scored, masked_ready = p3.sem("scored"), p3.sem("masked_ready")
                mixed, mixed_ready = p3.sem("mixed"), p3.sem("mixed_ready")
                stated, state_ready = p3.sem("stated"), p3.sem("state_ready")
                out_done, y_ready, u_ready = p3.sem("out_done"), p3.sem("y_ready"), p3.sem("u_ready")
                block = ctx3.enter_context(nc.Block())

                @block.sync
                def _(sp):
                    sp.dma_start(causal[:, :], const["causal"]).then_inc(c_loaded, 16)
                    sp.dma_start(blocks[:, :], const["blocks"]).then_inc(c_loaded, 16)
                    for q in range(2, QUARTERS):
                        sp.wait_ge(scored, 4 * PER_Q * (q - 1))
                        load_stacks(sp, q)

                @block.gpsimd
                def _(pool):
                    pool.memset(v_one[:, :, :], 0.0).then_inc(v_zero, 1)
                    pool.tensor_tensor(Y[:, :, :], U[:, :, :], rows[:, 0, :].unsqueeze(1).to_broadcast([P, TILES, D]),
                                       ALU.add).then_inc(u_ready, 1)
                    pool.wait_ge(v_zero, 1)
                    for t in range(TILES):
                        pool.wait_ge(tok_copied, 2 * (t // PER_Q + 1))
                        if t >= 2:
                            pool.wait_ge(mixed, t - 1)
                        pool.tensor_copy(
                            v_one[:, t % 2, :].rearrange("p (r x) -> p r x", x=VW)[:, :, 0:D]
                            .rearrange("p r (g y) -> p r g y", g=4)[:, :, :, 0:DH],
                            v_tok[:, t // PER_Q % 2, t % PER_Q, :].rearrange("p (g r d) -> p r g d", g=4, r=NW)
                        ).then_inc(v_placed, 1)

                @block.tensor
                def _(pe):
                    def turn_quarter(q):
                        if q >= 1:
                            pe.wait_ge(y_ready, q)
                            pe.wait_ge(state_ready, q * PER_Q)
                        if q >= 2:
                            pass
                        for n, src in enumerate((kT, vT)):
                            for i in range(PER_Q):
                                last = pe.transpose(psum[:, 6 + n, tile(i)], src[:, tile(q * PER_Q + i)], C["ident"])
                            last.then_inc(turned, 1)

                    def scores(t):
                        q, i = t // PER_Q, t % PER_Q
                        if i == 0:
                            pe.wait_ge(stacked[q % 2], 16 * 2 * len(PARTS) * (q // 2 + 1))
                        for g in range(4):
                            if t >= 1:
                                pe.wait_ge(masked_ready, (t - 1) * 4 + g + 1)
                            for r in range(4):
                                h = 4 * g + r
                                last = pe.matmul(psum[:, g, tile(r)], ks[:, q % 2, h, tile(i)], qs[:, q % 2, h, tile(i)],
                                                 start=True, stop=True, skip_group_check=True)
                            last.then_inc(scored, 1)

                    for q in range(QUARTERS):
                        turn_quarter(q)
                        if q == 0:
                            scores(0)
                        for i in range(PER_Q):
                            t = q * PER_Q + i
                            c = t % STILES
                            pe.wait_ge(tok_copied, 2 * (q + 1))
                            if c:
                                pe.wait_ge(state_ready, t)
                            if t >= 1:
                                pe.wait_ge(mixed_ready, t)
                            pe.wait_ge(v_placed, t + 1)
                            bank = 4
                            if c:
                                pe.matmul(psum[:, bank, 0:P], state[:, (t - 1) % 2, :], qT[:, tile(t)], start=True,
                                          stop=False, skip_group_check=True)
                            pe.wait_ge(masked_ready, 4 * (t + 1))
                            for r in range(NW):
                                for g in range(4):
                                    last = pe.matmul(psum[32 * g:32 * g + 32, bank, 0:P],
                                                     v_one[:, t % 2, r * D + 32 * g:r * D + 32 * g + 32],
                                                     masked[:, t % 2, 4 * g + r, :], start=(c == 0 and r == 0),
                                                     stop=(r == NW - 1), skip_group_check=True)
                            last.then_inc(mixed, 1)
                            if t + 1 < TILES:
                                scores(t + 1)
                            if t >= 1 and c == 0:
                                pe.wait_ge(state_ready, t)
                            pe.matmul(psum[:, 5, 0:P], k_tok[:, q % 2, i, :], v_tok[:, q % 2, i, :], start=(c == 0),
                                      stop=True, skip_group_check=True).then_inc(stated, 1)
                            pe.wait_ge(mixed_ready, t + 1)
                            if i == 0:
                                pe.wait_ge(tok_copied, 2 * (q + 1))
                            last = pe.matmul(psum[:, 7, tile(i)], mixed_t[:, t % 2, :], wo_raw[:, :], start=True,
                                             stop=True, skip_group_check=True)
                            last.then_inc(out_done, 1)

                @block.scalar
                def _(act):
                    for q in range(QUARTERS):
                        act.wait_ge(turned, 2 * q + 1)
                        if q >= 2:
                            act.wait_ge(stated, (q - 1) * PER_Q)
                            act.wait_ge(v_placed, (q - 1) * PER_Q)
                        act.activation(k_tok[:, q % 2, :, :], psum[:, 6, :].rearrange("p (t d) -> p t d", d=D), ACT.Copy).then_inc(tok_copied, 1)
                        act.wait_ge(turned, 2 * q + 2)
                        act.activation(v_tok[:, q % 2, :, :], psum[:, 7, :].rearrange("p (t d) -> p t d", d=D), ACT.Copy).then_inc(tok_copied, 1)

                @block.vector
                def _(dve):
                    dve.wait_ge(c_loaded, 32)

                    def mask(t):
                        for g in range(4):
                            dve.wait_ge(scored, 4 * t + g + 1)
                            if t >= 2:
                                dve.wait_ge(mixed, t - 1)
                            dve.tensor_tensor(masked[:, t % 2, 4 * g:4 * g + 4, :], psum[:, g, :].rearrange("p (r i) -> p r i", r=4),
                                              causal[:, :].unsqueeze(1).to_broadcast([P, 4, P]), ALU.mult).then_inc(masked_ready, 1)

                    mask(0)
                    for t in range(TILES):
                        if t + 1 < TILES:
                            mask_first = False
                        dve.wait_ge(mixed, t + 1)
                        if t >= 2:
                            dve.wait_ge(out_done, t - 1)
                        dve.tensor_tensor(mixed_t[:, t % 2, :], psum[:, 4, 0:P], FAC[:, tile(t)], ALU.mult).then_inc(mixed_ready, 1)
                        dve.wait_ge(stated, t + 1)
                        dve.tensor_tensor(state[:, t % 2, :], psum[:, 5, 0:P], blocks[:, :], ALU.mult).then_inc(state_ready, 1)
                        if t + 1 < TILES:
                            mask(t + 1)
                        if t % PER_Q == PER_Q - 1:
                            q = t // PER_Q
                            dve.wait_ge(out_done, t + 1)
                            dve.wait_ge(u_ready, 1)
                            part = Y[:, q * PER_Q:(q + 1) * PER_Q, :]
                            dve.tensor_tensor(part, part, psum[:, 7, :].rearrange("p (t d) -> p t d", d=D), ALU.add).then_inc(y_ready, 1)

        with ExitStack() as ctx4:
            p4 = Phase(nc, ctx4, "flow_ffn")
            HH, HL = p4.sb("HH", [P, TOK], F32R), p4.sb("HL", [P, TOK], F32R)
            h = p4.sb("h", [P, TILES, D])
            z = p4.sb("z", [P, TILES, D])
            hidden = p4.sb("hidden", [P, 2, FB, BANK])
            channels = p4.sb("channels", [P, 2, BANK])
            norm1 = Norm(p4, "norm1", Y, h)
            norm2 = Norm(p4, "norm2", z, Y)
            scaled, affine = p4.sem("scaled"), p4.sem("affine")
            turn = Turn(p4, "turn", psum, C["ident"], lambda t: h[:, t, :], HH, HL,
                        lambda pe, q: pe.wait_ge(affine, q + 1))
            up_done, hidden_ready, down_done = p4.sem("up_done"), p4.sem("hidden_ready"), p4.sem("down_done")
            channels_ready, back, z_ready = p4.sem("channels_ready"), p4.sem("back"), p4.sem("z_ready")
            scaled2, x_ready = p4.sem("scaled2"), p4.sem("x_ready")
            block = ctx4.enter_context(nc.Block())

            def affine_rows(dve, dst, q, g, b, first, second):
                part = dst[:, q * PER_Q:(q + 1) * PER_Q, :]
                full = [P, PER_Q, D]
                dve.tensor_tensor(part, part, rows[:, g, :].unsqueeze(1).to_broadcast(full), ALU.mult).then_inc(first, 1)
                dve.wait_ge(first, q + 1)
                return dve.tensor_tensor(part, part, rows[:, b, :].unsqueeze(1).to_broadcast(full), ALU.add)

            @block.tensor
            def _(pe):
                turn.tensor(pe)
                for q in range(QUARTERS):
                    pe.wait_ge(turn.lo_ready, QUARTERS)
                    for a in range(FB):
                        k = q * FB + a
                        if k >= 2:
                            pe.wait_ge(hidden_ready, k - 1)
                        split_product(pe, psum[:, 4 + k % 2, :], w1_hi[:, tile(a)], w1_lo[:, tile(a)],
                                      HH[:, quarter(q)], HL[:, quarter(q)]).then_inc(up_done, 1)
                    for a in range(FB):
                        pe.wait_ge(hidden_ready, q * FB + a + 1)
                        last = pe.matmul(psum[:, 6, :], w2_raw[:, a, :], hidden[:, q % 2, a, :], start=(a == 0),
                                         stop=(a == FB - 1), skip_group_check=True)
                    last.then_inc(down_done, 1)
                    pe.wait_ge(channels_ready, q + 1)
                    if q >= 1:
                        pe.wait_ge(z_ready, q)
                    for i in range(PER_Q):
                        last = pe.transpose(psum[:, 7, tile(i)], channels[:, q % 2, tile(i)], C["ident"])
                    last.then_inc(back, 1)

            @block.scalar
            def _(act):
                norm1.scalar(act)
                turn.scalar(act)
                for q in range(QUARTERS):
                    for a in range(FB):
                        k = q * FB + a
                        act.wait_ge(up_done, k + 1)
                        if a == 0 and q >= 2:
                            act.wait_ge(down_done, q - 1)
                        act.activation(hidden[:, q % 2, a, :], psum[:, 4 + k % 2, :], ACT.Gelu, bias=b1[:, a:a + 1]).then_inc(hidden_ready, 1)
                    act.wait_ge(down_done, q + 1)
                    if q >= 2:
                        act.wait_ge(back, q - 1)
                    act.activation(channels[:, q % 2, :], psum[:, 6, :], ACT.Identity, bias=columns[:, 3:4]).then_inc(channels_ready, 1)
                norm2.scalar(act)

            @block.vector
            def _(dve):
                norm1.vector(dve)
                for q in range(QUARTERS):
                    dve.wait_ge(norm1.normed, (q + 1) * PER_Q)
                    affine_rows(dve, h, q, 1, 2, scaled, affine).then_inc(affine, 1)
                turn.vector(dve)
                for q in range(QUARTERS):
                    dve.wait_ge(back, q + 1)
                    dve.wait_ge(affine, q + 1)
                    part = slice(q * PER_Q, (q + 1) * PER_Q)
                    dve.tensor_tensor(z[:, part, :], h[:, part, :], psum[:, 7, :].rearrange("p (t d) -> p t d", d=D),
                                      ALU.add).then_inc(z_ready, 1)
                dve.wait_ge(z_ready, QUARTERS)
                norm2.vector(dve)
                for q in range(QUARTERS):
                    dve.wait_ge(norm2.normed, (q + 1) * PER_Q)
                    affine_rows(dve, Y, q, 3, 4, scaled2, x_ready).then_inc(x_ready, 1)
                for q in range(QUARTERS):
                    part = slice(q * PER_Q, (q + 1) * PER_Q)
                    dve.wait_ge(x_ready, q + 1)
                    dve.tensor_tensor(X[:, part, :], X[:, part, :], Y[:, part, :], ALU.add).then_inc(x_ready, 1)


def gated_attention_phase(nc, psum, X, C, io):
    H, DH, TOPK, G = 8, 64, 3, 2
    PAIRS = H // G
    GROUPS = BATCH * PAIRS
    SCALE = float(DH) ** -0.5
    STEPS = STILES * G
    HD = H * DH
    QB = HD // D
    with ExitStack() as ctx:
        ph = Phase(nc, ctx, "gated")
        attended = ph.sb("attended", [P, TILES, HD])
        values = ph.sb("values", [P, TILES, HD])
        UH, UL = ph.sb("UH", [P, TOK], F32R), ph.sb("UL", [P, TOK], F32R)
        gates = ph.sb("gates", [P, TILES, H])
        wo_raw = ph.sb("wo_raw", [P, QB, D])
        wo_loaded = ph.sem("wo_loaded")
        wqk_hi = ph.sb("wqk_hi", [P, 2, HD], F32R)
        wqk_lo = ph.sb("wqk_lo", [P, 2, HD], F32R)
        max_dram = nc.dram_tensor("gated_max_scratch", [GROUPS, STEPS, P], F32, kind="Internal").ap()

        with ExitStack() as ctx1:
            ph1 = Phase(nc, ctx1, "gated_in")
            U = ph1.sb("U", [P, TILES, D])
            w_raw = ph1.sb("w_raw", [P, 3 * HD])
            wv_hi, wv_lo = ph1.sb("wv_hi", [P, HD], F32R), ph1.sb("wv_lo", [P, HD], F32R)
            ws_raw = ph1.sb("ws_raw", [P, H])
            ws_hi, ws_lo = ph1.sb("ws_hi", [P, H], F32R), ph1.sb("ws_lo", [P, H], F32R)
            scores = ph1.sb("scores", [P, TILES, H])
            beats = ph1.sb("beats", [P, TILES, H, H])
            ties = ph1.sb("ties", [P, TILES, H, H])
            rank = ph1.sb("rank", [P, TILES, H])
            norm = Norm(ph1, "norm", X, U)
            turn = Turn(ph1, "turn", psum, C["ident"], lambda t: U[:, t, :], UH, UL,
                        lambda pe, q: pe.wait_ge(norm.normed, (q + 1) * PER_Q))
            w_loaded, hi_ready, lo_ready = ph1.sem("w_loaded"), ph1.sem("hi_ready"), ph1.sem("lo_ready")
            logits_done, scores_ready = ph1.sem("logits_done"), ph1.sem("scores_ready")
            gate_step = ph1.sem("gate_step")
            v_done, v_copied = ph1.sem("v_done"), ph1.sem("v_copied")
            block = ctx1.enter_context(nc.Block())

            @block.sync
            def _(sp):
                sp.dma_start(ws_raw[:, :], io["L0_ffn_Ws"]).then_inc(w_loaded, 16)
                sp.dma_start(w_raw[:, 2 * HD:], io["L0_ffn_Wkv"][:, HD:]).then_inc(w_loaded, 16)
                sp.dma_start(w_raw[:, 0:HD], io["L0_ffn_Wq"]).then_inc(w_loaded, 16)
                sp.dma_start(w_raw[:, HD:2 * HD], io["L0_ffn_Wkv"][:, 0:HD]).then_inc(w_loaded, 16)
                sp.dma_start(wo_raw[:, :, :], io["L0_ffn_Wo"].rearrange("(a g) d e -> (g d) a e", g=2)).then_inc(wo_loaded, 16)
                sp.wait_ge(wo_loaded, 16)

            @block.gpsimd
            def _(pool):
                split_weights(pool, [(ws_raw[:, :], ws_hi[:, :], ws_lo[:, :], 64),
                                     (w_raw[:, 2 * HD:], wv_hi[:, :], wv_lo[:, :], 64),
                                     (w_raw[:, 0:HD], wqk_hi[:, 0, :], wqk_lo[:, 0, :], 64),
                                     (w_raw[:, HD:2 * HD], wqk_hi[:, 1, :], wqk_lo[:, 1, :], 64)],
                              w_loaded, hi_ready, lo_ready)

            @block.tensor
            def _(pe):
                turn.tensor(pe)
                pe.wait_ge(lo_ready, 1)
                pe.wait_ge(turn.lo_ready, QUARTERS)
                for t in range(TILES):
                    last = split_product(pe, psum[:, 4, t * H:(t + 1) * H], UH[:, tile(t)], UL[:, tile(t)],
                                         ws_hi[:, :], ws_lo[:, :])
                last.then_inc(logits_done, 1)
                pe.wait_ge(lo_ready, 2)
                for t in range(TILES):
                    if t >= 2:
                        pe.wait_ge(v_copied, t - 1)
                    split_product(pe, psum[:, 5 + t % 2, :], UH[:, tile(t)], UL[:, tile(t)],
                                  wv_hi[:, :], wv_lo[:, :]).then_inc(v_done, 1)

            @block.scalar
            def _(act):
                norm.scalar(act)
                turn.scalar(act)
                act.wait_ge(logits_done, 1)
                act.activation(scores[:, :, :], psum[:, 4, 0:TILES * H].rearrange("p (t h) -> p t h", h=H),
                               ACT.Sigmoid).then_inc(scores_ready, 1)
                for t in range(TILES):
                    act.wait_ge(v_done, t + 1)
                    act.activation(values[:, t, :], psum[:, 5 + t % 2, :], ACT.Copy).then_inc(v_copied, 1)

            @block.vector
            def _(dve):
                norm.vector(dve)
                turn.vector(dve)
                dve.wait_ge(scores_ready, 1)
                choose(dve, scores, beats, ties, rank, gates, C["before"], H, TOPK, gate_step)

        with ExitStack() as ctx2:
            ph2 = Phase(nc, ctx2, "gated_att")
            q2 = ph2.sb("q2", [P, 2, G, SEQ], F32R)
            ql = ph2.sb("ql", [DH + 1, 2, G, SEQ], F32R)
            k2 = ph2.sb("k2", [P, 2, G, SEQ], F32R)
            k1 = ph2.sb("k1", [DH + 1, 2, G, SEQ], F32R)
            w2_hi = ph2.sb("w2_hi", [P, 2, 2, G, 2, DH], F32R)
            w2_lo = ph2.sb("w2_lo", [P, 2, 2, G, 2, DH], F32R)
            probs = ph2.sb("probs", [P, 2, G, SEQ])
            ones = ph2.sb("ones", [P, 32])
            maxima = ph2.sb("maxima", [P, 2, STEPS])
            top = ph2.sb("top", [P, STEPS])
            shift_t = ph2.sb("shift_t", [STEPS, P], F32R)
            inv = ph2.sb("inv", [P, STILES, G])
            sums = ph2.sb("sums", [P, SEQ])
            dens = ph2.sb("dens", [P, BANK])
            w2_ready = ph2.sem("w2_ready")
            ones_ready = ph2.sem("ones_ready")
            chunk_done = ph2.sem("chunk_done")
            chunk_used = ph2.sem("chunk_used")
            parts_hi = ph2.sem("parts_hi")
            parts_ready = ph2.sem("parts_ready")
            top_ready = ph2.sem("top_ready")
            shift_ready = ph2.sem("shift_ready")
            shift_copied = ph2.sem("shift_copied")
            shift_stored = ph2.sem("shift_stored")
            shift_loaded = ph2.sem("shift_loaded")
            scored = ph2.sem("scored")
            exped = ph2.sem("exped")
            mixed = ph2.sem("mixed")
            sums_copied = ph2.sem("sums_copied")
            inv_ready = ph2.sem("inv_ready")
            block = ctx2.enter_context(nc.Block())

            def proj_of(g):
                return [("proj", g, j, m, x) for j in range(G) for m in range(2) for x in range(2)]

            def rows_of(g):
                return [("max", g, s, x) for s in range(STEPS) for x in range(2)]

            lead = proj_of(0) + rows_of(0) + [("shift", 0)]
            UNITS = 2 * STEPS
            EARLY = 6
            plan = []
            for n in range(GROUPS):
                ahead = proj_of(n + 1) + rows_of(n + 1) + [("shift", n + 1)] if n + 1 < GROUPS else []
                for u in range(UNITS):
                    now = []
                    if n >= 1 and u in (8, 10, 12):
                        now += [[("den", n - 1)], [("out", n - 1, 0)], [("out", n - 1, 1)]][u // 2 - 4]
                    a, b = (len(ahead) * min(i, UNITS - EARLY) // (UNITS - EARLY) for i in (u, u + 1))
                    plan.append(now + ahead[a:b])
            tail = [("den", GROUPS - 1), ("out", GROUPS - 1, 0), ("out", GROUPS - 1, 1)]
            order = lead + [c for now in plan for c in now] + tail
            number = {c: i for i, c in enumerate(order)}

            @block.sync
            def _(sp):
                for g in range(GROUPS):
                    sp.wait_ge(shift_copied, g + 1)
                    sp.dma_start(max_dram[g], f32(shift_t[:, :])).then_inc(shift_stored, 16)
                    sp.wait_ge(shift_stored, 16 * (g + 1))
                    sp.dma_start(f32(ql[DH:DH + 1, g % 2, :, :].rearrange("r j t -> r (j t)")),
                                 max_dram[g:g + 1].rearrange("r x y -> r (x y)")).then_inc(shift_loaded, 16)

            @block.gpsimd
            def _(pool):
                for g in range(GROUPS):
                    p0 = g % PAIRS * G * DH
                    if g >= 2:
                        pool.wait_ge(chunk_done, number[proj_of(g - 2)[-1]] + 1)
                    for n, (dst, src) in enumerate(((w2_hi, wqk_hi), (w2_lo, wqk_lo))):
                        for c in range(2):
                            pool.tensor_copy(dst[:, g % 2, :, :, c, :],
                                             src[:, :, p0:p0 + G * DH].rearrange("p m (j d) -> p m j d", j=G)
                                             ).then_inc(w2_ready, 1)

            def bank_of(i):
                return 6 + i % 2

            @block.tensor
            def _(pe):
                def chunk(c):
                    i = number[c]
                    bank = bank_of(i)
                    if i >= 2:
                        pe.wait_ge(chunk_used, i - 1)
                    if c[0] == "proj":
                        _, g, j, m, x = c
                        if j == m == x == 0:
                            pe.wait_ge(w2_ready, 4 * (g + 1))
                        at = g // PAIRS * SEQ + x * BANK
                        w = [t[:, g % 2, m, j, :, :].rearrange("p c d -> p (c d)") for t in (w2_hi, w2_lo)]
                        last = split_product(pe, psum[:, bank, :], *w, UH[:, at:at + BANK], UL[:, at:at + BANK])
                    elif c[0] == "max":
                        _, g, s, x = c
                        if s == x == 0:
                            pe.wait_ge(parts_ready, (g + 1) * 4 * G)
                        j, qt = s // STILES, s % STILES
                        last = pe.matmul(psum[:, bank, :], q2[:, g % 2, j, tile(qt)],
                                         k2[:, g % 2, j, x * BANK:(x + 1) * BANK], start=True, stop=True,
                                         skip_group_check=True)
                    elif c[0] == "shift":
                        pe.wait_ge(shift_ready, c[1] + 1)
                        last = pe.transpose(psum[0:STEPS, bank, 0:P], top[:, :], C["ident"])
                    elif c[0] == "out":
                        _, g, x = c
                        pe.wait_ge(sums_copied, 2 * (g + 1))
                        for i2 in range(4):
                            last = pe.transpose(psum[:, bank, tile(i2)], sums[:, tile(4 * x + i2)], C["ident"])
                    else:
                        pe.wait_ge(sums_copied, 2 * (c[1] + 1))
                        for i2 in range(4):
                            last = pe.transpose(psum[:, bank, tile(i2)], dens[:, tile(i2)], C["ident"])
                    last.then_inc(chunk_done, 1)

                def mix(n, kt, piece):
                    if piece == 0:
                        pe.wait_ge(exped, 2 * (n * STEPS + (kt + 1) * G))
                        if kt == 0 and n >= 1:
                            pe.wait_ge(sums_copied, 2 * n)
                    t = n // PAIRS * STILES + kt
                    flags = dict(start=(kt == 0), stop=(kt == STILES - 1), skip_group_check=True)
                    if piece < 2:
                        for j in range(G):
                            c0 = (n % PAIRS * G + j) * DH
                            last = pe.matmul(psum[DH * j:DH * j + DH, 3 + piece, :], values[:, t, c0:c0 + DH],
                                             probs[:, kt % 2, j, piece * BANK:(piece + 1) * BANK], **flags)
                    else:
                        for x in range(2):
                            for j in range(G):
                                at = 32 * (2 * x + j)
                                last = pe.matmul(psum[at:at + 32, 5, :], ones[:, :],
                                                 probs[:, kt % 2, j, x * BANK:(x + 1) * BANK], **flags)
                    last.then_inc(mixed, 1)

                pe.wait_ge(ones_ready, 1)
                for c in lead:
                    chunk(c)
                for n in range(GROUPS):
                    for u in range(UNITS):
                        k = n * UNITS + u
                        kt, j, x = u // (2 * G), u // 2 % G, u % 2
                        if u == 0:
                            pe.wait_ge(shift_loaded, 16 * (n + 1))
                        if k >= 3:
                            pe.wait_ge(exped, k - 2)
                        cols = slice(x * BANK, (x + 1) * BANK)
                        o = psum[:, k % 3, :]
                        pe.matmul(o, k2[:, n % 2, j, tile(kt)], q2[:, n % 2, j, cols], start=True, stop=False,
                                  skip_group_check=True)
                        pe.matmul(o, k1[:, n % 2, j, tile(kt)], ql[:, n % 2, j, cols], start=False,
                                  stop=True, skip_group_check=True).then_inc(scored, 1)
                        for c in plan[k]:
                            chunk(c)
                        if u % (2 * G) and k >= 2 * G:
                            before = (k - 2 * G) // (2 * G)
                            mix(before // STILES, before % STILES, u % (2 * G) - 1)
                for piece in range(3):
                    mix(GROUPS - 1, STILES - 1, piece)
                for c in tail:
                    chunk(c)

            @block.scalar
            def _(act):
                def proj(c):
                    _, g, j, m, x = c
                    cols = slice(x * BANK, (x + 1) * BANK)
                    act.wait_ge(chunk_done, number[c] + 1)
                    if m == 0:
                        act.activation(q2[:, g % 2, j, cols], psum[:, bank_of(number[c]), :], ACT.Copy).then_inc(parts_hi, 1)
                    else:
                        act.activation(k2[:, g % 2, j, cols], psum[:, bank_of(number[c]), :], ACT.Copy)
                        act.activation(k1[0:DH, g % 2, j, cols], psum[0:DH, bank_of(number[c]), :], ACT.Copy).then_inc(parts_hi, 1)

                def evacuate(n):
                    act.wait_ge(mixed, 3 * STILES * (n + 1))
                    if n >= 1:
                        act.wait_ge(chunk_done, number[("out", n - 1, 1)] + 1)
                    act.activation(sums[:, :], psum[:, 3:5, :].rearrange("p a b -> p (a b)"), ACT.Copy).then_inc(sums_copied, 1)
                    act.activation(dens[:, :], psum[:, 5, :], ACT.Copy).then_inc(sums_copied, 1)

                for c in proj_of(0):
                    proj(c)
                for n in range(GROUPS):
                    for u in range(UNITS):
                        k = n * UNITS + u
                        kt, j, x = u // (2 * G), u // 2 % G, u % 2
                        act.wait_ge(scored, k + 1)
                        if n * STILES + kt >= 2 and j == x == 0:
                            act.wait_ge(mixed, 3 * (n * STILES + kt - 1))
                        act.activation(probs[:, kt % 2, j, x * BANK:(x + 1) * BANK], psum[:, k % 3, :],
                                       ACT.Exp, scale=SCALE).then_inc(exped, 1)
                        if u == 4 and n >= 1:
                            evacuate(n - 1)
                        for c in plan[k]:
                            if c[0] == "proj":
                                proj(c)
                evacuate(GROUPS - 1)

            @block.vector
            def _(dve):
                dve.memset(ones[:, :], 1.0)
                dve.memset(f32(k1[DH:DH + 1, :, :, :]), 1.0).then_inc(ones_ready, 1)
                parts = 0
                for i, c in enumerate(order):
                    bank = bank_of(i)
                    if c[0] == "proj":
                        _, g, j, m, x = c
                        parts += 1
                        cols = slice(x * BANK, (x + 1) * BANK)
                        dve.wait_ge(parts_hi, parts)
                        if m == 0:
                            ins = dve.tensor_tensor(ql[0:DH, g % 2, j, cols], psum[0:DH, bank, :],
                                                    f32(q2[0:DH, g % 2, j, cols]), ALU.subtract)
                        else:
                            ins = dve.tensor_tensor(k2[DH:P, g % 2, j, cols], psum[DH:P, bank, :],
                                                    f32(k2[DH:P, g % 2, j, cols]), ALU.subtract)
                        ins.then_inc(chunk_used, 1)
                        dve.wait_ge(chunk_used, i + 1)
                        dve.sem_inc(parts_ready, 1)
                        continue
                    dve.wait_ge(chunk_done, i + 1)
                    if c[0] == "max":
                        _, g, s, x = c
                        if s == 0 and x == 0 and g >= 1:
                            dve.wait_ge(top_ready, g)
                        dve.tensor_reduce(maxima[:, x, s:s + 1], psum[:, bank, :], AX.X, ALU.max).then_inc(chunk_used, 1)
                        if s == STEPS - 1 and x == 1:
                            dve.wait_ge(chunk_used, i + 1)
                            if g >= 1:
                                dve.wait_ge(chunk_done, number[("shift", g - 1)] + 1)
                            dve.tensor_tensor(top[:, :], maxima[:, 0, :], maxima[:, 1, :], ALU.max).then_inc(top_ready, 1)
                            dve.wait_ge(top_ready, g + 1)
                            dve.sem_inc(shift_ready, 1)
                    elif c[0] == "shift":
                        g = c[1]
                        if g >= 1:
                            dve.wait_ge(shift_stored, 16 * g)
                        dve.tensor_scalar(shift_t[:, :], psum[0:STEPS, bank, 0:P], -1.0, None, ALU.mult).then_inc(chunk_used, 1)
                        dve.wait_ge(chunk_used, i + 1)
                        dve.sem_inc(shift_copied, 1)
                    elif c[0] == "den":
                        g = c[1]
                        b, h0 = g // PAIRS, g % PAIRS * G
                        view = psum[:, bank, :].rearrange("p (t x j r) -> p x t j r", t=4, x=2, j=G)
                        if g >= 1:
                            dve.wait_ge(chunk_used, number[("out", g - 1, 1)] + 1)
                        for x in range(2):
                            ins = dve.reciprocal(inv[:, 4 * x:4 * x + 4, :], view[:, x, :, :, 0])
                        ins.then_inc(inv_ready, 1)
                        dve.wait_ge(inv_ready, 2 * g + 1)
                        dve.tensor_tensor(inv[:, :, :], inv[:, :, :], gates[:, b * STILES:(b + 1) * STILES, h0:h0 + G],
                                          ALU.mult).then_inc(inv_ready, 1)
                        dve.wait_ge(inv_ready, 2 * g + 2)
                        dve.sem_inc(chunk_used, 1)
                    else:
                        _, g, x = c
                        b, h0 = g // PAIRS, g % PAIRS * G
                        t0 = b * STILES + 4 * x
                        dve.tensor_tensor(attended[:, t0:t0 + 4, h0 * DH:(h0 + G) * DH].rearrange("p t (j d) -> p t j d", d=DH),
                                          psum[:, bank, :].rearrange("p (t j d) -> p t j d", t=4, j=G),
                                          inv[:, 4 * x:4 * x + 4, :].unsqueeze(3).to_broadcast([P, 4, G, DH]),
                                          ALU.mult).then_inc(chunk_used, 1)

        with ExitStack() as ctx3:
            ph3 = Phase(nc, ctx3, "gated_out")
            att_t = ph3.sb("att_t", [P, 2, QB, BANK])
            bo = ph3.sb("bo", [H, D])
            gates_t = ph3.sb("gates_t", [H, TOK])
            channels = ph3.sb("channels", [P, 2, BANK])
            bo_loaded, gates_turned, gates_copied = ph3.sem("bo_loaded"), ph3.sem("gates_turned"), ph3.sem("gates_copied")
            turned, copied, product, product_copied = ph3.sem("turned"), ph3.sem("copied"), ph3.sem("product"), ph3.sem("product_copied")
            back, added = ph3.sem("back"), ph3.sem("added")
            block = ctx3.enter_context(nc.Block())

            @block.sync
            def _(sp):
                sp.dma_start(bo[:, :], io["L0_ffn_bo"]).then_inc(bo_loaded, 16)

            @block.tensor
            def _(pe):
                for q in range(QUARTERS):
                    if q >= 1:
                        pe.wait_ge(gates_copied, q)
                    for i in range(PER_Q):
                        last = pe.transpose(psum[0:H, 7, tile(i)], gates[:, q * PER_Q + i, :], C["ident"])
                    last.then_inc(gates_turned, 1)
                pe.wait_ge(bo_loaded, 16)

                def finish(q):
                    pe.wait_ge(product_copied, q + 1)
                    if q >= 1:
                        pe.wait_ge(added, q)
                    for i in range(PER_Q):
                        last = pe.transpose(psum[:, 6, tile(i)], channels[:, q % 2, tile(i)], C["ident"])
                    last.then_inc(back, 1)

                for q in range(QUARTERS):
                    for a in range(QB):
                        k = q * QB + a
                        if k >= 2:
                            pe.wait_ge(copied, k - 1)
                        for i in range(PER_Q):
                            last = pe.transpose(psum[:, k % 2, tile(i)],
                                                attended[:, q * PER_Q + i, a * D:(a + 1) * D], C["ident"])
                        last.then_inc(turned, 1)
                    if q >= 1:
                        finish(q - 1)
                    pe.wait_ge(copied, (q + 1) * QB)
                    if q == 0:
                        pe.wait_ge(gates_copied, QUARTERS)
                    for a in range(QB):
                        pe.matmul(psum[:, 4 + q % 2, :], wo_raw[:, a, :], att_t[:, q % 2, a, :],
                                  start=(a == 0), stop=False, skip_group_check=True)
                    pe.matmul(psum[:, 4 + q % 2, :], bo[:, :], gates_t[:, quarter(q)], start=False, stop=True,
                              skip_group_check=True).then_inc(product, 1)
                finish(QUARTERS - 1)

            @block.scalar
            def _(act):
                for q in range(QUARTERS):
                    act.wait_ge(gates_turned, q + 1)
                    act.activation(gates_t[:, quarter(q)], psum[0:H, 7, :], ACT.Copy).then_inc(gates_copied, 1)
                for k in range(QUARTERS * QB):
                    act.wait_ge(turned, k + 1)
                    if k >= 2 * QB and k % QB == 0:
                        act.wait_ge(product, k // QB - 1)
                    act.activation(att_t[:, k // QB % 2, k % QB, :], psum[:, k % 2, :], ACT.Copy).then_inc(copied, 1)

            @block.vector
            def _(dve):
                for q in range(QUARTERS):
                    dve.wait_ge(product, q + 1)
                    if q >= 2:
                        dve.wait_ge(back, q - 1)
                    dve.tensor_copy(channels[:, q % 2, :], psum[:, 4 + q % 2, :]).then_inc(product_copied, 1)
                    dve.wait_ge(back, q + 1)
                    part = X[:, q * PER_Q:(q + 1) * PER_Q, :]
                    dve.tensor_tensor(part, part, psum[:, 6, :].rearrange("p (t d) -> p t d", d=D),
                                      ALU.add).then_inc(added, 1)


def narrow_attention_phase(nc, psum, X, C, io):
    H, DH, G = 16, 8, 4
    GROUPS = BATCH * H // G
    PARTS = ((0, 0), (0, 1), (0, 2), (1, 0), (1, 1), (2, 0))
    NR = len(PARTS)
    ROWS = NR * DH
    SCALE = float(DH) ** -0.5
    STEPS = STILES * G
    HALF_S = STEPS // 2
    w_v = io["L1_attn_w_qkv"]
    with ExitStack() as ctx:
        ph = Phase(nc, ctx, "narrow")
        attended = ph.sb("attended", [P, GROUPS, STILES, G * DH])
        w_raw = ph.sb("w_raw", [P, 4 * D])
        w_hi = ph.sb("w_hi", [P, 4 * D], F32R)
        w_lo = ph.sb("w_lo", [P, 4 * D], F32R)
        w_loaded, w_hi_ready, w_ready = ph.sem("w_loaded"), ph.sem("w_hi_ready"), ph.sem("w_ready")
        values = ph.sb("values", [P, GROUPS, STILES, G, DH])

        K_ROWS = 96
        qs = ph.sb("qs", [K_ROWS, BATCH * H * SEQ], BF16)
        ks = ph.sb("ks", [K_ROWS, BATCH * H * SEQ], BF16)
        stacks_cleared = ph.sem("stacks_cleared")

        parts_dram = nc.dram_tensor("narrow_parts_scratch", [2, 3, P, TOK], BF16, kind="Internal").ap()
        max_dram = nc.dram_tensor("narrow_max_scratch", [GROUPS, 2 * G * STILES, P], BF16, kind="Internal").ap()
        ones_row = ph.sb("ones_row", [2, SEQ], BF16)

        with ExitStack() as ctx1:
            ph1 = Phase(nc, ctx1, "narrow_in")
            U = attended[:, :, :, :].rearrange("p a t d -> p (a t d)").rearrange("p (t d) -> p t d", d=D)
            UH, UL = ph1.sb("UH", [P, TOK], F32R), ph1.sb("UL", [P, TOK], F32R)
            part = ph1.sb("part", [P, 2, 3, TOK], BF16)
            rest = ph1.sb("rest", [P, 2, BANK])
            norm = Norm(ph1, "norm", X, U)
            turn = Turn(ph1, "turn", psum, C["ident"], lambda t: U[:, t, :], UH, UL,
                        lambda pe, q: pe.wait_ge(norm.normed, (q + 1) * PER_Q))
            projected = ph1.sem("projected")
            hi_taken = ph1.sem("hi_taken")
            rest_ready = ph1.sem("rest_ready")
            mid_taken = ph1.sem("mid_taken")
            low_taken = ph1.sem("low_taken")
            v_done = ph1.sem("v_done")
            v_copied = ph1.sem("v_copied")
            parts_stored = ph1.sem("parts_stored")
            block = ctx1.enter_context(nc.Block())

            @block.sync
            def _(sp):
                sp.dma_start(w_raw[:, 0:3 * D], w_v).then_inc(w_loaded, 16)
                sp.dma_start(w_raw[:, 3 * D:], io["L1_attn_w_out"]).then_inc(w_loaded, 16)
                for m in range(2):
                    sp.wait_ge(low_taken, (m + 1) * QUARTERS)
                    sp.dma_start(parts_dram[m].rearrange("s p t -> p s t"), part[:, m, :, :]).then_inc(parts_stored, 16)
                sp.wait_ge(parts_stored, 32)

            @block.gpsimd
            def _(pool):
                split_weights(pool, [(w_raw[:, :], w_hi[:, :], w_lo[:, :], 32)], w_loaded, w_hi_ready, w_ready)
                pool.memset(ones_row[:, :], 1.0).then_inc(stacks_cleared, 1)
                pool.wait_ge(stacks_cleared, 1)
                pool.wait_ge(w_ready, 1)
                for i, st in enumerate((qs, ks)):
                    if i:
                        pool.wait_ge(stacks_cleared, K_ROWS // 32)
                    for r in range(32, K_ROWS, 32):
                        pool.memset(st[r:r + 32, :].bitcast(mybir.dt.uint32), 0).then_inc(stacks_cleared, 1)

            @block.tensor
            def _(pe):
                turn.tensor(pe)
                pe.wait_ge(w_ready, 1)
                pe.wait_ge(turn.lo_ready, QUARTERS)
                for m in range(2):
                    for q in range(QUARTERS):
                        k = m * QUARTERS + q
                        if k >= 4:
                            pe.wait_ge(rest_ready, k - 3)
                        split_product(pe, psum[:, 4 + k % 4, :], w_hi[:, tile(m)], w_lo[:, tile(m)],
                                      UH[:, quarter(q)], UL[:, quarter(q)]).then_inc(projected, 1)
                for q in range(QUARTERS):
                    for i in range(PER_Q):
                        t = q * PER_Q + i
                        last = split_product(pe, psum[:, q, tile(i)], UH[:, tile(t)], UL[:, tile(t)],
                                             w_hi[:, tile(2)], w_lo[:, tile(2)])
                    last.then_inc(v_done, 1)

            @block.scalar
            def _(act):
                norm.scalar(act)
                turn.scalar(act)
                for m in range(2):
                    for q in range(QUARTERS):
                        k = m * QUARTERS + q
                        act.wait_ge(projected, k + 1)
                        act.activation(part[:, m, 0, quarter(q)], psum[:, 4 + k % 4, :], ACT.Copy).then_inc(hi_taken, 1)
                        act.wait_ge(rest_ready, k + 1)
                        act.activation(part[:, m, 1, quarter(q)], rest[:, k % 2, :], ACT.Copy).then_inc(mid_taken, 1)
                for q in range(QUARTERS):
                    act.wait_ge(v_done, q + 1)
                    b, s0 = q * PER_Q // STILES, q * PER_Q % STILES
                    last = None
                    for i in range(PER_Q):
                        last = act.activation(values[:, b * G:(b + 1) * G, s0 + i, :, :],
                                              psum[:, q, tile(i)].rearrange("p (a g d) -> p a g d", a=G, g=G),
                                              ACT.Copy)
                    last.then_inc(v_copied, 1)

            @block.vector
            def _(dve):
                norm.vector(dve)
                turn.vector(dve)
                for m in range(2):
                    for q in range(QUARTERS):
                        k = m * QUARTERS + q
                        dve.wait_ge(hi_taken, k + 1)
                        if k >= 2:
                            dve.wait_ge(mid_taken, k - 1)
                            dve.wait_ge(low_taken, k - 1)
                        dve.tensor_tensor(rest[:, k % 2, :], psum[:, 4 + k % 4, :], part[:, m, 0, quarter(q)],
                                          ALU.subtract).then_inc(rest_ready, 1)
                        dve.wait_ge(mid_taken, k + 1)
                        dve.tensor_tensor(part[:, m, 2, quarter(q)], rest[:, k % 2, :], part[:, m, 1, quarter(q)],
                                          ALU.subtract).then_inc(low_taken, 1)

        with ExitStack() as ctx2:
            ph2 = Phase(nc, ctx2, "narrow_att")
            probs = ph2.sb("probs", [P, 2, G, SEQ])
            v_ones = ph2.sb("v_ones", [P, 2, STILES, G, 32])
            maxima = ph2.sb("maxima", [P, 2, 2, STEPS])
            top = ph2.sb("top", [P, STEPS])
            shift = ph2.sb("shift", [P, 2 * STEPS], BF16)
            shift_t = ph2.sb("shift_t", [2 * STEPS, P], BF16)
            sums = ph2.sb("sums", [P, SEQ])
            inv = ph2.sb("inv", [P, 4 * G])
            stacked = [ph2.sem(f"stacked{m}") for m in range(BATCH)]
            v_zero = ph2.sem("v_zero")
            v_base = ph2.sem("v_base")
            v_ready = ph2.sem("v_ready")
            chunk_done = ph2.sem("chunk_done")
            chunk_used = ph2.sem("chunk_used")
            top_ready = ph2.sem("top_ready")
            shift_hi = ph2.sem("shift_hi")
            shift_ready = ph2.sem("shift_ready")
            shift_copied = ph2.sem("shift_copied")
            shift_stored = ph2.sem("shift_stored")
            shift_loaded = ph2.sem("shift_loaded")
            scored = ph2.sem("scored")
            exped = ph2.sem("exped")
            mixed = ph2.sem("mixed")
            sums_copied = ph2.sem("sums_copied")
            inv_ready = ph2.sem("inv_ready")
            block = ctx2.enter_context(nc.Block())

            UNITS = 2 * STEPS
            EARLY = 12
            queue = []
            for g in range(GROUPS):
                queue += [("max", g, s, x) for s in range(STEPS) for x in range(2)] + [("shift", g)]
            n_lead = UNITS + 1 + EARLY
            lead, queue = queue[:n_lead], queue[n_lead:]
            plan = []
            for k in range(GROUPS * UNITS):
                n, u = k // UNITS, k % UNITS
                now = [("out", n - 1, (u - 16) // 4)] if n >= 1 and u in (16, 20) else []
                a, b = (min(len(queue), i * (UNITS + 1) // UNITS) for i in (k, k + 1))
                plan.append(now + queue[a:b])
            tail = [("out", GROUPS - 1, 0), ("out", GROUPS - 1, 1)]
            order = lead + [c for now in plan for c in now] + tail
            number = {c: i for i, c in enumerate(order)}

            def head_tok(g, s):
                return (g * G + s % G) * SEQ

            @block.sync
            def _(sp):
                half = H * SEQ
                for b in range(BATCH):
                    for r, (qp, kp) in enumerate(PARTS):
                        for st, m, s in ((ks, 1, kp), (qs, 0, qp)):
                            sp.dma_start(st[r * DH:(r + 1) * DH, b * half:(b + 1) * half].rearrange("d (h t) -> d h t", t=SEQ),
                                         parts_dram[m, s][:, b * SEQ:(b + 1) * SEQ].rearrange("(h d) t -> d h t", d=DH)
                                         ).then_inc(stacked[b], 16)
                    sp.dma_start(ks[ROWS:ROWS + 2, b * half:(b + 1) * half].rearrange("r (h t) -> r h t", t=SEQ),
                                 ones_row[:, :].unsqueeze(1).to_broadcast([2, H, SEQ])).then_inc(stacked[b], 16)
                for g in range(GROUPS):
                    sp.wait_ge(shift_copied, g + 1)
                    sp.dma_start(max_dram[g], shift_t[:, :]).then_inc(shift_stored, 16)
                    sp.wait_ge(shift_stored, 16 * (g + 1))
                    sp.dma_start(qs[ROWS:ROWS + 2, g * G * SEQ:(g + 1) * G * SEQ],
                                 max_dram[g].rearrange("(r x) y -> r (x y)", r=2)).then_inc(shift_loaded, 16)

            @block.gpsimd
            def _(pool):
                pool.memset(v_ones[:, :, :, :, :], 0.0).then_inc(v_zero, 1)
                pool.wait_ge(v_zero, 1)
                pool.memset(v_ones[:, :, :, :, DH:DH + 1], 1.0).then_inc(v_base, 1)
                pool.wait_ge(v_base, 1)
                for n in range(GROUPS):
                    if n >= 2:
                        pool.wait_ge(mixed, (n - 1) * STILES * 2)
                    pool.tensor_copy(v_ones[:, n % 2, :, :, 0:DH], values[:, n, :, :, :]).then_inc(v_ready, 1)

            @block.tensor
            def _(pe):
                def chunk(c):
                    i = number[c]
                    bank = 5 + i % 3
                    if i >= 3:
                        pe.wait_ge(chunk_used, i - 2)
                    if c[0] == "max":
                        _, g, s, x = c
                        if s == 0 and x == 0 and g in (0, GROUPS // BATCH):
                            pe.wait_ge(stacked[g * BATCH // GROUPS], 16 * (2 * NR + 1))
                        at = head_tok(g, s)
                        last = pe.matmul(psum[:, bank, :], qs[:, at + s // G * P:at + s // G * P + P],
                                         ks[:, at + x * BANK:at + (x + 1) * BANK], start=True, stop=True,
                                         skip_group_check=True)
                    elif c[0] == "shift":
                        pe.wait_ge(shift_ready, c[1] + 1)
                        last = pe.transpose(psum[:, bank, :].bitcast(BF16)[0:2 * STEPS, 0:P], shift[:, :], C["ident_bf"])
                    else:
                        _, g, x = c
                        pe.wait_ge(sums_copied, g + 1)
                        for i2 in range(4):
                            last = pe.transpose(psum[:, bank, tile(i2)], sums[:, tile(4 * x + i2)], C["ident"])
                    last.then_inc(chunk_done, 1)

                def mix(n, kt, x):
                    if x == 0:
                        pe.wait_ge(exped, 2 * (n * STEPS + (kt + 1) * G))
                        if kt == 0:
                            pe.wait_ge(v_ready, n + 1)
                            if n >= 1:
                                pe.wait_ge(sums_copied, n)
                    for j in range(G):
                        last = pe.matmul(psum[32 * j:32 * j + 32, 3 + x, :], v_ones[:, n % 2, kt, j, :],
                                         probs[:, kt % 2, j, x * BANK:(x + 1) * BANK],
                                         start=(kt == 0), stop=(kt == STILES - 1), skip_group_check=True)
                    last.then_inc(mixed, 1)

                for c in lead:
                    chunk(c)
                for n in range(GROUPS):
                    for u in range(UNITS):
                        k = n * UNITS + u
                        kt, j, x = u // (2 * G), u // 2 % G, u % 2
                        if u == 0:
                            pe.wait_ge(shift_loaded, 16 * (n + 1))
                        if k >= 3:
                            pe.wait_ge(exped, k - 2)
                        at = head_tok(n, j)
                        pe.matmul(psum[:, k % 3, :], ks[:, at + kt * P:at + kt * P + P],
                                  qs[:, at + x * BANK:at + (x + 1) * BANK], start=True, stop=True,
                                  skip_group_check=True).then_inc(scored, 1)
                        for c in plan[k]:
                            chunk(c)
                        if u % (2 * G) in (2, 6) and k >= 2 * G:
                            before = (k - 2 * G) // (2 * G)
                            mix(before // STILES, before % STILES, u % (2 * G) // 4)
                mix(GROUPS - 1, STILES - 1, 0)
                mix(GROUPS - 1, STILES - 1, 1)
                for c in tail:
                    chunk(c)

            def evacuate(act, n):
                act.wait_ge(mixed, 2 * STILES * (n + 1))
                if n >= 1:
                    act.wait_ge(chunk_done, number[("out", n - 1, 1)] + 1)
                act.activation(sums[:, :], psum[:, 3:5, :].rearrange("p a b -> p (a b)"), ACT.Copy).then_inc(sums_copied, 1)

            @block.scalar
            def _(act):
                for n in range(GROUPS):
                    for u in range(UNITS):
                        k = n * UNITS + u
                        kt, j, x = u // (2 * G), u // 2 % G, u % 2
                        act.wait_ge(scored, k + 1)
                        if n * STILES + kt >= 2 and j == x == 0:
                            act.wait_ge(mixed, 2 * (n * STILES + kt - 1))
                        act.activation(probs[:, kt % 2, j, x * BANK:(x + 1) * BANK], psum[:, k % 3, :],
                                       ACT.Exp, scale=SCALE).then_inc(exped, 1)
                        if u == 8 and n >= 1:
                            evacuate(act, n - 1)
                evacuate(act, GROUPS - 1)

            @block.vector
            def _(dve):
                shifts = 0
                for i, c in enumerate(order):
                    bank = 5 + i % 3
                    if c[0] == "max":
                        _, g, s, x = c
                        dve.wait_ge(chunk_done, i + 1)
                        if s == 0 and x == 0 and g >= 2:
                            dve.wait_ge(top_ready, g - 1)
                        dve.tensor_reduce(maxima[:, g % 2, x, (s % G) * STILES + s // G:(s % G) * STILES + s // G + 1],
                                          psum[:, bank, :], AX.X, ALU.max).then_inc(chunk_used, 1)
                        if s == STEPS - 1 and x == 1:
                            dve.wait_ge(chunk_used, i + 1)
                            dve.tensor_tensor(top[:, :], maxima[:, g % 2, 0, :], maxima[:, g % 2, 1, :], ALU.max).then_inc(top_ready, 1)
                            dve.wait_ge(top_ready, g + 1)
                            if g >= 1:
                                dve.wait_ge(chunk_done, number[("shift", g - 1)] + 1)
                            dve.tensor_scalar(shift[:, 0:STEPS], top[:, :], -1.0, None, ALU.mult).then_inc(shift_hi, 1)
                            dve.wait_ge(shift_hi, g + 1)
                            dve.scalar_tensor_tensor(shift[:, STEPS:], top[:, :], -1.0, shift[:, 0:STEPS],
                                                     ALU.mult, ALU.subtract).then_inc(shift_ready, 1)
                    elif c[0] == "shift":
                        g = c[1]
                        dve.wait_ge(chunk_done, i + 1)
                        if g >= 1:
                            dve.wait_ge(shift_stored, 16 * g)
                        dve.tensor_copy(shift_t[:, :], psum[:, bank, :].bitcast(BF16)[0:2 * STEPS, 0:P]).then_inc(chunk_used, 1)
                        dve.wait_ge(chunk_used, i + 1)
                        dve.sem_inc(shift_copied, 1)
                    else:
                        _, g, x = c
                        dve.wait_ge(chunk_done, i + 1)
                        dve.wait_ge(chunk_used, i)
                        view = psum[:, bank, :].rearrange("p (t j d) -> p t j d", t=4, j=G)
                        dve.reciprocal(inv[:, :].rearrange("p (t j) -> p t j", j=G), view[:, :, :, DH]).then_inc(inv_ready, 1)
                        dve.wait_ge(inv_ready, 2 * g + x + 1)
                        dve.tensor_tensor(attended[:, g, 4 * x:4 * x + 4, :].rearrange("p t (j d) -> p t j d", d=DH),
                                          view[:, :, :, 0:DH],
                                          inv[:, :].rearrange("p (t j) -> p t j", j=G).unsqueeze(3).to_broadcast([P, 4, G, DH]),
                                          ALU.mult).then_inc(chunk_used, 1)

        with ExitStack() as ctx3:
            ph3 = Phase(nc, ctx3, "narrow_out")
            UH, UL = ph3.sb("AH", [P, TOK], F32R), ph3.sb("AL", [P, TOK], F32R)
            gathered = ph3.sb("gathered", [P, TILES, D])
            gathered_ready = ph3.sem("gathered_ready")
            turn = Turn(ph3, "turn", psum, C["ident"], lambda t: gathered[:, t, :], UH, UL,
                        lambda pe, q: pe.wait_ge(gathered_ready, q + 1))
            project_and_add(nc, ctx3, ph3, psum, turn, X, [(UH, UL, w_hi[:, tile(3)], w_lo[:, tile(3)])],
                            gather=(gathered, attended, gathered_ready, G))


def experts_phase(nc, psum, X, C, io, out, stored):
    E, TOPK, HID = 8, 2, io["L1_ffn_up_w"].shape[2]
    FB = HID // P
    ALLE = E + 1
    with ExitStack() as ctx:
        ph = Phase(nc, ctx, "moe")
        U = ph.sb("U", [P, TILES, D])
        UH, UL = ph.sb("UH", [P, TOK], F32R), ph.sb("UL", [P, TOK], F32R)
        raw_up = ph.sb("raw_up", [P, 2, HID])
        raw_down = ph.sb("raw_down", [P, 2, FB, D])
        up_hi = ph.sb("up_hi", [P, 2, HID], F32R)
        up_lo = ph.sb("up_lo", [P, 2, HID], F32R)
        up_bias = ph.sb("up_bias", [P, ALLE, FB])
        down_bias = ph.sb("down_bias", [P, ALLE])
        gate_raw = ph.sb("gate_raw", [P, E])
        gate_hi = ph.sb("gate_hi", [P, E], F32R)
        gate_lo = ph.sb("gate_lo", [P, E], F32R)
        gate_bias = ph.sb("gate_bias", [P, E])
        logits = ph.sb("logits", [P, TILES, E])
        scores = ph.sb("scores", [P, TILES, E])
        rank = ph.sb("rank", [P, TILES, E])
        beats = ph.sb("beats", [P, TILES, E, E])
        ties = ph.sb("ties", [P, TILES, E, E])
        chosen = ph.sb("chosen", [P, TILES, E])
        total = ph.sb("total", [P, TILES])
        share = ph.sb("share", [P, TILES])
        mixw = ph.sb("mixw", [P, TILES, E])
        mixw_t = ph.sb("mixw_t", [P, P])
        mixb = ph.sb("mixb", [P, 2, TOK])
        hidden = ph.sb("hidden", [P, 2, FB, BANK])
        term = ph.sb("term", [P, 2, BANK])
        acc = ph.sb("acc", [P, TOK])
        least = ph.sb("least", [P, TILES])
        peak = ph.sb("peak", [P, TILES])
        peak_eps = ph.sb("peak_eps", [P, TILES])
        inv_peak = ph.sb("inv_peak", [P, TILES])
        scr = nc.dram_tensor("moe_mix_scratch", [P, P], F32, kind="Internal").ap()

        norm = Norm(ph, "norm", X, U)
        turn = Turn(ph, "turn", psum, C["ident"], lambda t: U[:, t, :], UH, UL,
                    lambda pe, q: pe.wait_ge(norm.normed, (q + 1) * PER_Q))
        small_loaded = ph.sem("small_loaded")
        up_loaded = [ph.sem(f"up_loaded{i}") for i in range(2)]
        down_loaded = [ph.sem(f"down_loaded{i}") for i in range(2)]
        gate_hi_ready = ph.sem("gate_hi_ready")
        gate_ready = ph.sem("gate_ready")
        up_hi_ready = ph.sem("up_hi_ready")
        up_ready = ph.sem("up_ready")
        logits_done = ph.sem("logits_done")
        logits_ready = ph.sem("logits_ready")
        scores_ready = ph.sem("scores_ready")
        gate_step = ph.sem("gate_step")
        mix_turned = ph.sem("mix_turned")
        mix_copied = ph.sem("mix_copied")
        mix_stored = ph.sem("mix_stored")
        mixb_loaded = [ph.sem(f"mixb_loaded{i}") for i in range(2)]
        up_done = ph.sem("up_done")
        hidden_ready = ph.sem("hidden_ready")
        down_done = ph.sem("down_done")
        term_ready = ph.sem("term_ready")
        acc_ready = ph.sem("acc_ready")
        acc_turned = ph.sem("acc_turned")
        peak_step = ph.sem("peak_step")
        result_ready = ph.sem("result_ready")
        GATE_STEPS = 10

        def up_src(e):
            return io["L1_ffn_up_w"][e] if e < E else io["L1_ffn_sw_up"]

        def down_src(e):
            w = io["L1_ffn_down_w"][e] if e < E else io["L1_ffn_sw_down"]
            return w.rearrange("(a p) n -> p a n", p=P)

        out_v = out.rearrange("b (t p) d -> p (b t) d", p=P)
        block = ctx.enter_context(nc.Block())

        def mixb_load(sp, n):
            if n >= 3:
                sp.wait_ge(term_ready, (n - 1) * QUARTERS)
            src = scr.rearrange("(t e) p -> e t p", e=E)[n - 1]
            sp.dma_start(mixb[:, n % 2, :].rearrange("p (t k) -> p t k", k=P),
                         src.partition_broadcast(P)).then_inc(mixb_loaded[n % 2], 16)

        @block.sync
        def _(sp):
            with nc.allow_non_contiguous_dma(reason="small bias columns"):
                sp.dma_start(gate_raw[:, :], io["L1_ffn_gate_w"]).then_inc(small_loaded, 16)
                sp.dma_start(gate_bias[:, :], io["L1_ffn_bias"].partition_broadcast(P)).then_inc(small_loaded, 16)
                sp.dma_start(up_bias[:, 0:E, :], io["L1_ffn_up_b"].rearrange("e (a p) -> p e a", p=P)).then_inc(small_loaded, 16)
                sp.dma_start(up_bias[:, E, :], io["L1_ffn_sb_up"].rearrange("(a p) -> p a", p=P)).then_inc(small_loaded, 16)
                sp.dma_start(down_bias[:, 0:E], io["L1_ffn_down_b"].rearrange("e p -> p e")).then_inc(small_loaded, 16)
                sp.dma_start(down_bias[:, E:E + 1], io["L1_ffn_sb_down"].rearrange("(p a) -> p a", a=1)).then_inc(small_loaded, 16)
            for n in range(ALLE):
                e = (n + E) % ALLE
                if n >= 2:
                    sp.wait_ge(up_ready, n - 1)
                    sp.wait_ge(down_done, (n - 1) * QUARTERS)
                sp.dma_start(raw_up[:, n % 2, :], up_src(e)).then_inc(up_loaded[n % 2], 16)
                sp.dma_start(raw_down[:, n % 2, :, :], down_src(e)).then_inc(down_loaded[n % 2], 16)
                if n == 1:
                    sp.wait_ge(mix_copied, 1)
                    sp.dma_start(scr, mixw_t[:, :]).then_inc(mix_stored, 16)
                    sp.wait_ge(mix_stored, 16)
                if n >= 1:
                    mixb_load(sp, n)
            for q in range(QUARTERS):
                sp.wait_ge(result_ready, q + 1)
                sp.dma_start(out_v[:, q * PER_Q:(q + 1) * PER_Q, :],
                             X[:, q * PER_Q:(q + 1) * PER_Q, :]).then_inc(stored, 16)
            sp.wait_ge(stored, 16 * QUARTERS)

        @block.gpsimd
        def _(pool):
            pool.wait_ge(small_loaded, 16 * 6)
            pool.tensor_copy(gate_hi[:, :], gate_raw[:, :]).then_inc(gate_hi_ready, 1)
            pool.wait_ge(gate_hi_ready, 1)
            pool.tensor_tensor(gate_lo[:, :], gate_raw[:, :], f32(gate_hi[:, :]), ALU.subtract).then_inc(gate_ready, 1)
            for n in range(ALLE):
                pool.wait_ge(up_loaded[n % 2], 16 * (n // 2 + 1))
                if n >= 2:
                    pool.wait_ge(up_done, (n - 1) * QUARTERS * FB)
                pool.tensor_copy(up_hi[:, n % 2, :], raw_up[:, n % 2, :]).then_inc(up_hi_ready, 1)
                pool.wait_ge(up_hi_ready, n + 1)
                pool.tensor_tensor(up_lo[:, n % 2, :], raw_up[:, n % 2, :], f32(up_hi[:, n % 2, :]),
                                   ALU.subtract).then_inc(up_ready, 1)

        @block.tensor
        def _(pe):
            turn.tensor(pe)
            pe.wait_ge(gate_ready, 1)
            pe.wait_ge(turn.lo_ready, QUARTERS)
            for t in range(TILES):
                last = split_product(pe, psum[:, 4, t * E:(t + 1) * E], UH[:, tile(t)], UL[:, tile(t)],
                                     gate_hi[:, :], gate_lo[:, :])
            last.then_inc(logits_done, 1)

            def up(n, q):
                if q == 0:
                    pe.wait_ge(up_ready, n + 1)
                for a in range(FB):
                    k = (n * QUARTERS + q) * FB + a
                    if k >= 4:
                        pe.wait_ge(hidden_ready, k - 3)
                    split_product(pe, psum[:, a, :], up_hi[:, n % 2, tile(a)], up_lo[:, n % 2, tile(a)],
                                  UH[:, quarter(q)], UL[:, quarter(q)]).then_inc(up_done, 1)

            def down(n, q):
                k = n * QUARTERS + q
                if q == 0:
                    pe.wait_ge(down_loaded[n % 2], 16 * (n // 2 + 1))
                if k == 0:
                    pe.wait_ge(mix_copied, 1)
                if k >= 2:
                    pe.wait_ge(term_ready, k - 1)
                for a in range(FB):
                    pe.wait_ge(hidden_ready, k * FB + a + 1)
                    last = pe.matmul(psum[:, 6 + k % 2, :], raw_down[:, n % 2, a, :], hidden[:, k % 2, a, :],
                                     start=(a == 0), stop=(a == FB - 1), skip_group_check=True)
                last.then_inc(down_done, 1)

            steps = [(n, q) for n in range(ALLE) for q in range(QUARTERS)]
            for k, (n, q) in enumerate(steps):
                up(n, q)
                if k == 0:
                    pe.wait_ge(gate_step, GATE_STEPS)
                    pe.transpose(psum[:, 5, 0:P], mixw[:, :, :].rearrange("p t e -> p (t e)"),
                                 C["ident"]).then_inc(mix_turned, 1)
                if k >= 1:
                    down(*steps[k - 1])
            down(*steps[-1])
            for q in range(QUARTERS):
                pe.wait_ge(acc_ready, (ALLE - 2) * QUARTERS + q + 1)
                if q == 0:
                    pe.wait_ge(hidden_ready, ALLE * QUARTERS * FB)
                for i in range(PER_Q):
                    last = pe.transpose(psum[:, q, tile(i)], acc[:, tile(q * PER_Q + i)], C["ident"])
                last.then_inc(acc_turned, 1)

        @block.scalar
        def _(act):
            norm.scalar(act)
            turn.scalar(act)
            act.wait_ge(logits_ready, 1)
            act.activation(scores[:, :, :], logits[:, :, :], ACT.Sigmoid).then_inc(scores_ready, 1)
            for n in range(ALLE):
                e = (n + E) % ALLE
                for q in range(QUARTERS):
                    k = n * QUARTERS + q
                    if k >= 2:
                        act.wait_ge(down_done, k - 1)
                    for a in range(FB):
                        act.wait_ge(up_done, k * FB + a + 1)
                        act.activation(hidden[:, k % 2, a, :], psum[:, a, :], ACT.Gelu,
                                       bias=up_bias[:, e, a:a + 1]).then_inc(hidden_ready, 1)
                    if k == 0:
                        act.wait_ge(mix_turned, 1)
                        act.activation(mixw_t[:, :], psum[:, 5, 0:P], ACT.Copy).then_inc(mix_copied, 1)

        @block.vector
        def _(dve):
            norm.vector(dve)
            turn.vector(dve)
            dve.wait_ge(small_loaded, 16 * 6)
            dve.wait_ge(logits_done, 1)
            dve.tensor_tensor(logits[:, :, :], psum[:, 4, 0:TILES * E].rearrange("p (t e) -> p t e", e=E),
                              gate_bias[:, :].unsqueeze(1).to_broadcast([P, TILES, E]),
                              ALU.add).then_inc(logits_ready, 1)
            dve.wait_ge(scores_ready, 1)
            choose(dve, scores, beats, ties, rank, chosen, C["before"], E, TOPK, gate_step)
            dve.wait_ge(gate_step, 6)
            dve.tensor_reduce(total[:, :], chosen[:, :, :], AX.X, ALU.add).then_inc(gate_step, 1)
            dve.wait_ge(gate_step, 7)
            dve.tensor_scalar(share[:, :], total[:, :], 1e-6, 10.0, ALU.add, ALU.mult).then_inc(gate_step, 1)
            dve.wait_ge(gate_step, 8)
            dve.reciprocal(total[:, :], share[:, :]).then_inc(gate_step, 1)
            dve.wait_ge(gate_step, 9)
            dve.tensor_tensor(mixw[:, :, :], chosen[:, :, :],
                              total[:, :].unsqueeze(2).to_broadcast([P, TILES, E]), ALU.mult).then_inc(gate_step, 1)
            for n in range(ALLE):
                e = (n + E) % ALLE
                for q in range(QUARTERS):
                    k = n * QUARTERS + q
                    dve.wait_ge(down_done, k + 1)
                    if n == 0:
                        dve.tensor_scalar(acc[:, quarter(q)], psum[:, 6 + k % 2, :], down_bias[:, e:e + 1],
                                          0.1, ALU.add, ALU.mult).then_inc(term_ready, 1)
                        continue
                    if q == 0:
                        dve.wait_ge(mixb_loaded[n % 2], 16 * ((n + 1) // 2))
                    if n >= 2:
                        dve.wait_ge(acc_ready, (n - 2) * QUARTERS + q + 1)
                    dve.scalar_tensor_tensor(term[:, k % 2, :], psum[:, 6 + k % 2, :], down_bias[:, e:e + 1],
                                             mixb[:, n % 2, quarter(q)], ALU.add, ALU.mult).then_inc(term_ready, 1)
                    dve.wait_ge(term_ready, k + 1)
                    dve.tensor_tensor(acc[:, quarter(q)], acc[:, quarter(q)], term[:, k % 2, :],
                                      ALU.add).then_inc(acc_ready, 1)
            for q in range(QUARTERS):
                part = slice(q * PER_Q, (q + 1) * PER_Q)
                dve.wait_ge(acc_turned, q + 1)
                turned = psum[:, q, :].rearrange("p (t d) -> p t d", d=D)
                dve.tensor_reduce(peak[:, part], turned, AX.X, ALU.max).then_inc(peak_step, 1)
                dve.tensor_reduce(least[:, part], turned, AX.X, ALU.min).then_inc(peak_step, 1)
                dve.wait_ge(peak_step, 5 * q + 2)
                dve.scalar_tensor_tensor(peak_eps[:, part], least[:, part], -1.0, peak[:, part], ALU.mult,
                                         ALU.max).then_inc(peak_step, 1)
                dve.wait_ge(peak_step, 5 * q + 3)
                dve.tensor_scalar(peak[:, part], peak_eps[:, part], 1e-6, None, ALU.add).then_inc(peak_step, 1)
                dve.wait_ge(peak_step, 5 * q + 4)
                dve.reciprocal(inv_peak[:, part], peak[:, part]).then_inc(peak_step, 1)
                dve.wait_ge(peak_step, 5 * q + 5)
                for i in range(PER_Q):
                    t = q * PER_Q + i
                    last = dve.scalar_tensor_tensor(X[:, t, :], psum[:, q, tile(i)], inv_peak[:, t:t + 1],
                                                    X[:, t, :], ALU.mult, ALU.add)
                last.then_inc(result_ready, 1)


def program(nc, io, const, out, phases="ABCD"):
    with ExitStack() as ctx:
        Phase.sems = []

        def sb(name, shape, dt=F32):
            return ctx.enter_context(nc.sbuf_tensor(name, shape, dt))

        psum = ctx.enter_context(nc.psum_tensor("psum", [P, 8, BANK], F32))
        X = sb("X", [P, TILES, D])
        ident = sb("ident", [P, P])
        ident_bf = sb("ident_bf", [P, P], BF16)
        before = sb("before", [P, 8, 8])
        C = {"ident": ident[:, :], "ident_bf": ident_bf[:, :], "before": before[:, :, :]}
        stored = ctx.enter_context(nc.semaphore("stored"))
        loaded = ctx.enter_context(nc.semaphore("loaded"))
        with nc.Block() as block:
            @block.sync
            def _(sp):
                src = io["L0_attn_inputs"].rearrange("b (t p) d -> p (b t) d", p=P)
                for q in range(QUARTERS):
                    sp.dma_start(X[:, q * PER_Q:(q + 1) * PER_Q, :], src[:, q * PER_Q:(q + 1) * PER_Q, :]).then_inc(loaded, 16)
                sp.dma_start(ident[:, :], const["ident"]).then_inc(loaded, 16)
                sp.dma_start(before[:, :, :], const["before"].partition_broadcast(P)).then_inc(loaded, 16)
                sp.wait_ge(loaded, 16 * 6)

            @block.vector
            def _(dve):
                dve.wait_ge(loaded, 16 * 6)
                dve.tensor_copy(ident_bf[:, :], ident[:, :])
        if "A" in phases:
            flow_phase(nc, psum, X, C, io, const)
            clear_semaphores(nc)
        if "B" in phases:
            gated_attention_phase(nc, psum, X, C, io)
            clear_semaphores(nc)
        if "C" in phases:
            narrow_attention_phase(nc, psum, X, C, io)
            clear_semaphores(nc)
        if "D" in phases:
            experts_phase(nc, psum, X, C, io, out, stored)
        else:
            s = ctx.enter_context(nc.semaphore("dbg"))
            with nc.Block() as block:
                @block.sync
                def _(sp):
                    sp.dma_start(out.rearrange("b (t p) d -> p (b t) d", p=P), X[:, :, :]).then_inc(s, 16)
                    sp.wait_ge(s, 16)


def constants():
    import numpy as np
    eye = np.eye(P, dtype=np.float32)
    row, col = np.arange(P)[:, None], np.arange(P)[None, :]
    row_head = np.where(row % 32 < 16, row % 32, -1)
    token = (row // 32) % 2 * BANK + np.arange(BANK)[None, :] + 1.0
    return {
        "sums_w": (row // 8 == np.arange(32)[None, :] % 16).astype(np.float32),
        "spread": (row_head == col // 8).astype(np.float32),
        "carry_w": ((row + 32 == col) & (row // 32 % 2 == 0)).astype(np.float32),
        "normal": token.astype(np.float32),
        "inv_normal": (1.0 / token).astype(np.float32),
        "causal": (row <= col).astype(np.float32),
        "blocks": (row // 8 == col // 8).astype(np.float32),
        "ident": eye,
        "before": np.tril(np.ones((8, 8), np.float32), -1),
    }


def kernel(**inputs):
    import numpy as _np
    import concourse.bacc as _bacc
    from concourse import mybir as _mybir
    from concourse.bass_utils import run_bass_kernel_spmd as _run

    nc = _bacc.Bacc("TRN2", target_bir_lowering=False, num_devices=1)
    arrays, io, const = {}, {}, {}
    for name, a in inputs.items():
        if name == "L0_attn_attn_mask":
            continue
        a = _np.ascontiguousarray(a)
        arrays[f"in_{name}"] = a
        io[name] = nc.dram_tensor(f"in_{name}", a.shape, _mybir.dt.from_np(a.dtype), kind="ExternalInput").ap()
    for name, a in constants().items():
        arrays[f"const_{name}"] = a
        const[name] = nc.dram_tensor(f"const_{name}", a.shape, _mybir.dt.from_np(a.dtype), kind="ExternalInput").ap()
    out = nc.dram_tensor("out_0", (BATCH, SEQ, D), _mybir.dt.float32, kind="ExternalOutput").ap()
    program(nc, io, const, out)
    r = _run(nc, [arrays], core_ids=[0])
    return r.results[0]["out_0"]
```

```python
from contextlib import ExitStack

import concourse.bass as bass
from concourse import mybir

ALU = mybir.AluOpType
ACT = mybir.ActivationFunctionType
AX = mybir.AxisListType
F32 = mybir.dt.float32
F32R = mybir.dt.float32r
BF16 = mybir.dt.bfloat16

P = 128
BATCH = 2
SEQ = 1024
TOK = BATCH * SEQ
TILES = TOK // P
STILES = SEQ // P
D = 128
BANK = 512
QUARTERS = TOK // BANK
PER_Q = BANK // P
EPS_LN = 1e-5


class Phase:

    sems = None

    def __init__(self, nc, ctx, tag):
        self.nc, self.ctx, self.tag = nc, ctx, tag

    def sb(self, name, shape, dt=F32):
        return self.ctx.enter_context(self.nc.sbuf_tensor(f"{self.tag}_{name}", shape, dt))

    def sem(self, name):
        sem = self.nc.alloc_semaphore(f"{self.tag}_{name}")
        Phase.sems.append(sem)
        return sem


def clear_semaphores(nc):
    with nc.Block() as block:
        @block.gpsimd
        def _(pool):
            for sem in Phase.sems:
                pool.sem_clear(sem)
    for sem in Phase.sems:
        nc.release_semaphore(sem)
    Phase.sems = []


def f32(ap):
    return ap.bitcast(F32)


def quarter(q):
    return slice(q * BANK, (q + 1) * BANK)


def tile(t):
    return slice(t * P, (t + 1) * P)


def split_product(pe, out, a_hi, a_lo, b_hi, b_lo, start=True, stop=True):
    pe.matmul(out, a_hi, b_hi, start=start, stop=False, skip_group_check=True)
    pe.matmul(out, a_hi, b_lo, start=False, stop=False, skip_group_check=True)
    return pe.matmul(out, a_lo, b_hi, start=False, stop=stop, skip_group_check=True)


class Norm:

    def __init__(self, ph, name, src, dst):
        self.src, self.dst = src, dst
        self.stats = ph.sb(f"{name}_stats", [P, TILES, 6])
        self.moments = ph.sb(f"{name}_moments", [P, TILES, 2])
        self.std = ph.sb(f"{name}_std", [P, TILES])
        self.rstd = ph.sb(f"{name}_rstd", [P, TILES])
        self.eps = ph.sb(f"{name}_eps", [P, 1])
        self.eps_ready = ph.sem(f"{name}_eps_ready")
        self.stats_ready = ph.sem(f"{name}_stats_ready")
        self.moments_ready = ph.sem(f"{name}_moments_ready")
        self.std_ready = ph.sem(f"{name}_std_ready")
        self.rstd_ready = ph.sem(f"{name}_rstd_ready")
        self.normed = ph.sem(f"{name}_normed")

    def set_eps(self, dve):
        dve.memset(self.eps[:, :], EPS_LN).then_inc(self.eps_ready, 1)

    def quarter_stats(self, dve, q):
        for t in range(q * PER_Q, (q + 1) * PER_Q):
            dve.bn_stats(self.stats[:, t, :], self.src[:, t, :]).then_inc(self.stats_ready, 1)
        for t in range(q * PER_Q, (q + 1) * PER_Q):
            dve.wait_ge(self.stats_ready, t + 1)
            dve.bn_aggr(self.moments[:, t, :], self.stats[:, t, :]).then_inc(self.moments_ready, 1)

    def quarter_root(self, act, q):
        part = slice(q * PER_Q, (q + 1) * PER_Q)
        if q == 0:
            act.wait_ge(self.eps_ready, 1)
        act.wait_ge(self.moments_ready, (q + 1) * PER_Q)
        act.activation(self.std[:, part], self.moments[:, part, 1], ACT.Sqrt,
                       bias=self.eps[:, 0:1]).then_inc(self.std_ready, 1)

    def quarter_norm(self, dve, q):
        part = slice(q * PER_Q, (q + 1) * PER_Q)
        dve.wait_ge(self.std_ready, q + 1)
        dve.reciprocal(self.rstd[:, part], self.std[:, part]).then_inc(self.rstd_ready, 1)
        dve.wait_ge(self.rstd_ready, q + 1)
        for t in range(q * PER_Q, (q + 1) * PER_Q):
            dve.tensor_scalar(self.dst[:, t, :], self.src[:, t, :], self.moments[:, t, 0:1],
                              self.rstd[:, t:t + 1], ALU.subtract, ALU.mult).then_inc(self.normed, 1)


class Turn:

    def __init__(self, ph, name, psum, ident, view, hi, lo, ready, bank=0):
        self.psum, self.ident, self.view, self.hi, self.lo = psum, ident, view, hi, lo
        self.ready, self.bank = ready, bank
        self.turned = ph.sem(f"{name}_turned")
        self.hi_ready = ph.sem(f"{name}_hi_ready")
        self.lo_ready = ph.sem(f"{name}_lo_ready")

    def tensor(self, pe, products=None):
        for q in range(QUARTERS):
            self.ready(pe, q)
            for i in range(PER_Q):
                last = pe.transpose(self.psum[:, self.bank + q, tile(i)], self.view(q * PER_Q + i),
                                    self.ident)
            last.then_inc(self.turned, 1)
            if products and q >= 1:
                pe.wait_ge(self.lo_ready, q)
                products(q - 1)
        if products:
            pe.wait_ge(self.lo_ready, QUARTERS)
            products(QUARTERS - 1)

    def quarter_high(self, act, q):
        act.wait_ge(self.turned, q + 1)
        act.activation(self.hi[:, quarter(q)], self.psum[:, self.bank + q, :], ACT.Copy).then_inc(self.hi_ready, 1)

    def quarter_low(self, dve, q):
        dve.wait_ge(self.hi_ready, q + 1)
        dve.tensor_tensor(self.lo[:, quarter(q)], self.psum[:, self.bank + q, :],
                          f32(self.hi[:, quarter(q)]), ALU.subtract).then_inc(self.lo_ready, 1)


def norm_and_turn_vector(dve, norm, turn, arrived=None, scale=None):
    norm.set_eps(dve)
    for q in range(QUARTERS + 1):
        if q < QUARTERS:
            if arrived:
                arrived(q)
            norm.quarter_stats(dve, q)
        if q >= 1:
            norm.quarter_norm(dve, q - 1)
            if scale:
                scale(q - 1)
        if q >= 2:
            turn.quarter_low(dve, q - 2)
    turn.quarter_low(dve, QUARTERS - 1)


def norm_and_turn_scalar(act, norm, turn):
    for q in range(QUARTERS + 1):
        if q < QUARTERS:
            norm.quarter_root(act, q)
        if q >= 1:
            turn.quarter_high(act, q - 1)


def split_weights(pool, pairs, loaded, hi_ready, lo_ready):
    for n, (raw, hi, lo, at) in enumerate(pairs):
        pool.wait_ge(loaded, at)
        pool.tensor_copy(hi, raw).then_inc(hi_ready, 1)
        pool.wait_ge(hi_ready, n + 1)
        pool.tensor_tensor(lo, raw, f32(hi), ALU.subtract).then_inc(lo_ready, 1)


def choose(dve, scores, beats, ties, rank, chosen, before, n, k, step):
    full = [P, TILES, n, n]
    mine = scores[:, :, :].unsqueeze(3).to_broadcast(full)
    other = scores[:, :, :].unsqueeze(2).to_broadcast(full)
    dve.tensor_tensor(beats[:, :, :, :], other, mine, ALU.is_gt).then_inc(step, 1)
    dve.tensor_tensor(ties[:, :, :, :], other, mine, ALU.is_equal).then_inc(step, 1)
    dve.wait_ge(step, 2)
    dve.tensor_tensor(ties[:, :, :, :], ties[:, :, :, :], before.unsqueeze(1).to_broadcast(full),
                      ALU.mult).then_inc(step, 1)
    dve.wait_ge(step, 3)
    dve.tensor_tensor(beats[:, :, :, :], beats[:, :, :, :], ties[:, :, :, :], ALU.add).then_inc(step, 1)
    dve.wait_ge(step, 4)
    dve.tensor_reduce(rank[:, :, :], beats[:, :, :, :], AX.X, ALU.add).then_inc(step, 1)
    dve.wait_ge(step, 5)
    dve.scalar_tensor_tensor(chosen[:, :, :], rank[:, :, :], float(k), scores[:, :, :],
                             ALU.is_lt, ALU.mult).then_inc(step, 1)


def project_and_add(nc, ctx, ph, psum, turn, X, factors, gather):
    gathered, attended, gathered_ready, G = gather
    out_done, added = ph.sem("out_done"), ph.sem("added")
    block = ctx.enter_context(nc.Block())
    per_batch = QUARTERS // BATCH

    @block.scalar
    def _(act):
        for q in range(QUARTERS):
            turn.quarter_high(act, q)

    @block.tensor
    def _(pe):
        turn.tensor(pe)
        for q in range(QUARTERS):
            pe.wait_ge(turn.lo_ready, q + 1)
            for i in range(PER_Q):
                t = q * PER_Q + i
                for n, (a_hi, a_lo, w_hi, w_lo) in enumerate(factors):
                    last = split_product(pe, psum[:, 4 + q, tile(i)], a_hi[:, tile(t)], a_lo[:, tile(t)], w_hi, w_lo,
                                         start=(n == 0), stop=(n == len(factors) - 1))
            last.then_inc(out_done, 1)

    @block.vector
    def _(dve):
        for q in range(QUARTERS):
            b, s0 = q // per_batch, q % per_batch * PER_Q
            for a in range(G):
                last = dve.tensor_copy(gathered[:, q * PER_Q:(q + 1) * PER_Q, a * D // G:(a + 1) * D // G],
                                       attended[:, b * G + a, s0:s0 + PER_Q, :])
            last.then_inc(gathered_ready, 1)
        for q in range(QUARTERS):
            turn.quarter_low(dve, q)
        for q in range(QUARTERS):
            dve.wait_ge(out_done, q + 1)
            part = X[:, q * PER_Q:(q + 1) * PER_Q, :]
            dve.tensor_tensor(part, part, psum[:, 4 + q, :].rearrange("p (t d) -> p t d", d=D),
                              ALU.add).then_inc(added, 1)


def flow_phase(nc, psum, X, C, io, const):
    H, DH, EPS = 16, 8, 1e-6
    PARTS = ((0, 0), (0, 1), (0, 2), (1, 0), (1, 1), (2, 0))
    K_ROWS = 96
    NW = 4
    VW = D + DH
    HID = io["L0_attn_W1"].shape[1]
    FB = HID // P
    PERB = QUARTERS // BATCH
    parts_dram = nc.dram_tensor("flow_parts_scratch", [2, 3, P, TOK], BF16, kind="Internal").ap()

    with ExitStack() as ctx:
        ph = Phase(nc, ctx, "flow")
        U = ph.sb("U", [P, TILES, D])
        Y = ph.sb("Y", [P, TILES, D])
        wo_raw = ph.sb("wo_raw", [P, D])
        w1_raw, w1_hi, w1_lo = ph.sb("w1_raw", [P, HID]), ph.sb("w1_hi", [P, HID], F32R), ph.sb("w1_lo", [P, HID], F32R)
        w2_raw = ph.sb("w2_raw", [P, FB, D])
        columns = ph.sb("columns", [P, 4])
        b1 = ph.sb("b1", [P, FB])
        rows = ph.sb("rows", [P, 5, D])

        with ExitStack() as ctx_a:
            pa = Phase(nc, ctx_a, "flow_att")
            qT, kT, vT = (pa.sb(n, [P, TOK]) for n in ("qT", "kT", "vT"))
            FAC = pa.sb("FAC", [P, TOK])
            sums_w = pa.sb("sums_w", [P, 32])
            spread = pa.sb("spread", [P, P])
            carry_w = pa.sb("carry_w", [P, P])
            normal, inv_normal = pa.sb("normal", [P, BANK]), pa.sb("inv_normal", [P, BANK])
            causal, blocks = pa.sb("causal", [P, P]), pa.sb("blocks", [P, P])
            qs = pa.sb("qs", [K_ROWS, 2, H, BANK], BF16)
            ks = pa.sb("ks", [K_ROWS, 2, H, BANK], BF16)
            stacked = [pa.sem(f"stacked{i}") for i in range(2)]
            stacks_cleared = pa.sem("stacks_cleared")

            with ExitStack() as ctx1:
                p1 = Phase(nc, ctx1, "flow_in")
                UH, UL = p1.sb("UH", [P, TOK], F32R), p1.sb("UL", [P, TOK], F32R)
                w_raw, w_hi, w_lo = p1.sb("w_raw", [P, 3 * D]), p1.sb("w_hi", [P, 3 * D], F32R), p1.sb("w_lo", [P, 3 * D], F32R)
                norm = Norm(p1, "norm", X, U)
                turn = Turn(p1, "turn", psum, C["ident"], lambda t: U[:, t, :], UH, UL,
                            lambda pe, q: pe.wait_ge(norm.normed, (q + 1) * PER_Q))
                w_loaded, rows_loaded, c_loaded = p1.sem("w_loaded"), p1.sem("rows_loaded"), p1.sem("c_loaded")
                hi_ready, lo_ready = p1.sem("hi_ready"), p1.sem("lo_ready")
                projected, activated = p1.sem("projected"), p1.sem("activated")
                block = ctx1.enter_context(nc.Block())

                @block.sync
                def _(sp):
                    for n, name in enumerate(("Wq", "Wk", "Wv")):
                        sp.dma_start(w_raw[:, tile(n)], io[f"L0_attn_{name}"]).then_inc(w_loaded, 16)
                    sp.dma_start(w1_raw[:, :], io["L0_attn_W1"]).then_inc(w_loaded, 16)
                    with nc.allow_non_contiguous_dma(reason="bias columns"):
                        for n, name in enumerate(("bq", "bk", "bv", "b2")):
                            sp.dma_start(columns[:, n:n + 1], io[f"L0_attn_{name}"].rearrange("(p a) -> p a", a=1)).then_inc(rows_loaded, 16)
                        sp.dma_start(b1[:, :], io["L0_attn_b1"].rearrange("(a p) -> p a", p=P)).then_inc(rows_loaded, 16)
                    for n, name in enumerate(("bo", "ln1_g", "ln1_b", "ln2_g", "ln2_b")):
                        sp.dma_start(rows[:, n, :], io[f"L0_attn_{name}"].partition_broadcast(P)).then_inc(rows_loaded, 16)
                    sp.dma_start(wo_raw[:, :], io["L0_attn_Wo"]).then_inc(rows_loaded, 16)
                    sp.dma_start(w2_raw[:, :, :], io["L0_attn_W2"].rearrange("(a p) n -> p a n", p=P)).then_inc(rows_loaded, 16)
                    for name, dst in (("sums_w", sums_w), ("spread", spread), ("carry_w", carry_w), ("normal", normal),
                                      ("inv_normal", inv_normal), ("causal", causal), ("blocks", blocks)):
                        sp.dma_start(dst[:, :], const[name]).then_inc(c_loaded, 16)
                    sp.wait_ge(rows_loaded, 16 * 12)
                    sp.wait_ge(c_loaded, 16 * 7)

                @block.gpsimd
                def _(pool):
                    pool.memset(qs[:, :, :, :].rearrange("p a h t -> p (a h t)").bitcast(F32), 0.0).then_inc(stacks_cleared, 1)
                    split_weights(pool, [(w_raw[:, :], w_hi[:, :], w_lo[:, :], 64),
                                         (w1_raw[:, :], w1_hi[:, :], w1_lo[:, :], 64)], w_loaded, hi_ready, lo_ready)

                @block.tensor
                def _(pe):
                    turn.tensor(pe)
                    pe.wait_ge(lo_ready, 1)
                    for m in range(3):
                        for q in range(QUARTERS):
                            pe.wait_ge(turn.lo_ready, q + 1)
                            k = m * QUARTERS + q
                            if k >= 4:
                                pe.wait_ge(activated, k - 3)
                            split_product(pe, psum[:, 4 + k % 4, :], w_hi[:, tile(m)], w_lo[:, tile(m)],
                                          UH[:, quarter(q)], UL[:, quarter(q)]).then_inc(projected, 1)

                @block.scalar
                def _(act):
                    norm_and_turn_scalar(act, norm, turn)
                    act.wait_ge(rows_loaded, 16 * 12)
                    for m, dst in enumerate((qT, kT, vT)):
                        for q in range(QUARTERS):
                            k = m * QUARTERS + q
                            act.wait_ge(projected, k + 1)
                            act.activation(dst[:, quarter(q)], psum[:, 4 + k % 4, :],
                                           ACT.Sigmoid if m < 2 else ACT.Identity,
                                           bias=columns[:, m:m + 1]).then_inc(activated, 1)

                @block.vector
                def _(dve):
                    norm_and_turn_vector(dve, norm, turn)

            def load_stacks(sp, q):
                for r, (qp, kp) in enumerate(PARTS):
                    for st, m, s in ((ks, 1, kp), (qs, 0, qp)):
                        sp.dma_start(st[r * DH:(r + 1) * DH, q % 2, :, :],
                                     parts_dram[m, s][:, quarter(q)].rearrange("(h d) t -> d h t", d=DH)).then_inc(stacked[q % 2], 16)

            with ExitStack() as ctx2:
                p2 = Phase(nc, ctx2, "flow_mass")
                cum = p2.sb("cum", [P, 2, SEQ])
                prod = p2.sb("prod", [P, TOK])
                carried = p2.sb("carried", [P, 1])
                part = p2.sb("part", [P, 2, 3, TOK], BF16)
                rest = p2.sb("rest", [P, 2, BANK])
                hi_taken, rest_ready, mid_taken, low_taken = (p2.sem(n) for n in ("hi_taken", "rest_ready", "mid_taken", "low_taken"))
                parts_stored, fac_copied = p2.sem("parts_stored"), p2.sem("fac_copied")
                r_sink, sink, src = (p2.sb(n, [P, BANK]) for n in ("r_sink", "sink", "src"))
                scratch = p2.sb("scratch", [P, BANK])
                take, give = p2.sb("take", [P, BANK]), p2.sb("give", [P, BANK])
                cum_give = p2.sb("cum_give", [P, BANK])
                alloc = p2.sb("alloc", [P, BANK])
                step = p2.sem("step")
                summed, spreaded, act_step = p2.sem("summed"), p2.sem("spreaded"), p2.sem("act_step")
                block = ctx2.enter_context(nc.Block())

                AT = {}

                @block.sync
                def _(sp):
                    for m in range(2):
                        sp.wait_ge(low_taken, (m + 1) * QUARTERS)
                        sp.dma_start(parts_dram[m].rearrange("s p t -> p s t"), part[:, m, :, :]).then_inc(parts_stored, 16)
                    sp.wait_ge(parts_stored, 32)
                    sp.wait_ge(stacks_cleared, 2)
                    for q in range(2):
                        load_stacks(sp, q)

                @block.gpsimd
                def _(pool):
                    pool.memset(ks[:, :, :, :].rearrange("p a h t -> p (a h t)").bitcast(F32), 0.0).then_inc(stacks_cleared, 1)
                    for k in range(2 * QUARTERS + 1):
                        if k < 2 * QUARTERS:
                            m, q = k // QUARTERS, k % QUARTERS
                            pool.wait_ge(hi_taken, k + 1)
                            if k >= 2:
                                pool.wait_ge(mid_taken, k - 1)
                                pool.wait_ge(low_taken, k - 1)
                            pool.tensor_tensor(rest[:, k % 2, :], (qT, kT)[m][:, quarter(q)], part[:, m, 0, quarter(q)],
                                               ALU.subtract).then_inc(rest_ready, 1)
                        if k >= 1:
                            m, q = (k - 1) // QUARTERS, (k - 1) % QUARTERS
                            pool.wait_ge(mid_taken, k)
                            pool.tensor_tensor(part[:, m, 2, quarter(q)], rest[:, (k - 1) % 2, :],
                                               part[:, m, 1, quarter(q)], ALU.subtract).then_inc(low_taken, 1)

                @block.vector
                def _(dve):
                    count = [0]

                    def done(ins, name=None):
                        count[0] += 1
                        ins.then_inc(step, 1)
                        dve.wait_ge(step, count[0])
                        if name:
                            AT[name] = count[0]

                    def cumulate(x, src, b, name, free=None):
                        cols = slice(b * SEQ, (b + 1) * SEQ)
                        done(dve.tensor_tensor_scan(cum[:, b, :], src[:, cols], src[:, cols], EPS, ALU.add, ALU.bypass))
                        if free:
                            dve.wait_ge(summed, free)
                        done(dve.scalar_tensor_tensor(prod[:, cols], x[:, cols], EPS, cum[:, b, :], ALU.add, ALU.mult), f"{name}{b}")

                    for b in range(BATCH):
                        cumulate(qT, kT, b, "p1_")
                    for b in range(BATCH):
                        cumulate(kT, qT, b, "p2_", free=b + 1)
                    dve.wait_ge(summed, 2 * BATCH)
                    done(dve.reciprocal(src[:, :], psum[:, 1, :]))
                    done(dve.tensor_tensor(src[:, :], src[:, :], normal[:, :], ALU.mult), "src")
                    done(dve.reciprocal(r_sink[:, :], psum[:, 0, :]))
                    done(dve.tensor_tensor(sink[:, :], r_sink[:, :], normal[:, :], ALU.mult), "sink")
                    for n, (x, y) in enumerate(((kT, qT), (qT, kT))):
                        for b in range(BATCH):
                            dve.wait_ge(summed, (n + 1) * BATCH + b + 1)
                            for q in range(b * PERB, (b + 1) * PERB):
                                dve.wait_ge(spreaded, n * QUARTERS + q + 1)
                                done(dve.tensor_tensor(prod[:, quarter(q)], x[:, quarter(q)], psum[:, 2 + q, :], ALU.mult), f"used{n}_{q}")
                            cumulate(y, prod, b, f"p{n + 3}_")
                    done(dve.tensor_tensor(take[:, :], psum[:, 0, :], inv_normal[:, :], ALU.mult), "take")
                    dve.wait_ge(summed, 4 * BATCH)
                    done(dve.tensor_tensor(scratch[:, :], psum[:, 1, :], inv_normal[:, :], ALU.mult))
                    done(dve.tensor_scalar(give[:, :], scratch[:, :], 1.0, -1.0, ALU.min, ALU.max), "give")
                    dve.wait_ge(act_step, 1)
                    done(dve.tensor_tensor(r_sink[:, :], r_sink[:, :], alloc[:, :], ALU.mult), "fac")
                    dve.wait_ge(act_step, 2)
                    done(dve.tensor_tensor_scan(cum_give[:, :], give[:, :], give[:, :], 0.0, ALU.add, ALU.bypass), "cum_give")
                    done(dve.tensor_tensor(give[:, :], give[:, :], normal[:, :], ALU.mult))
                    dve.wait_ge(summed, 4 * BATCH + 1)
                    done(dve.tensor_copy(carried[:, :], psum[:, 0, 0:1]))
                    done(dve.tensor_scalar(scratch[:, :], cum_give[:, :], carried[:, 0:1], None, ALU.add))
                    done(dve.reciprocal(cum_give[:, :], scratch[:, :]))
                    done(dve.tensor_tensor(give[:, :], give[:, :], cum_give[:, :], ALU.mult), "comp")
                    for q in range(QUARTERS):
                        dve.wait_ge(spreaded, 3 * QUARTERS + q + 1)
                        done(dve.tensor_tensor(vT[:, quarter(q)], vT[:, quarter(q)], psum[:, 2 + q, :], ALU.mult))

                @block.tensor
                def _(pe):
                    def head_sums(bank, name, b):
                        pe.wait_ge(step, AT[f"{name}_{b}"])
                        for q in range(b * PERB, (b + 1) * PERB):
                            last = pe.matmul(psum[32 * q:32 * q + 32, bank, :], sums_w[:, :], prod[:, quarter(q)],
                                             start=True, stop=True, skip_group_check=True)
                        last.then_inc(summed, 1)

                    def to_channels(src_rows, name, q):
                        pe.wait_ge(step, AT[name])
                        rows_q = slice(32 * q, 32 * q + 32)
                        pe.matmul(psum[:, 2 + q, :], spread[rows_q, :], src_rows[rows_q, :],
                                  start=True, stop=True, skip_group_check=True).then_inc(spreaded, 1)

                    for n in range(2):
                        for b in range(BATCH):
                            head_sums(n, f"p{n + 1}", b)
                    for q in range(QUARTERS):
                        to_channels(src, "src", q)
                    pe.wait_ge(step, AT["sink"])
                    for b in range(BATCH):
                        head_sums(0, "p3", b)
                        for q in range(b * PERB, (b + 1) * PERB):
                            to_channels(sink, f"used0_{q}", q)
                    for b in range(BATCH):
                        head_sums(1, "p4", b)
                    for q in range(QUARTERS):
                        to_channels(r_sink, "fac", q)
                    pe.wait_ge(step, AT["cum_give"])
                    pe.matmul(psum[:, 0, 0:1], carry_w[:, :], cum_give[:, BANK - 1:BANK], start=True, stop=True,
                              skip_group_check=True).then_inc(summed, 1)
                    for q in range(QUARTERS):
                        pe.wait_ge(fac_copied, q + 1)
                        to_channels(give, "comp", q)

                @block.scalar
                def _(act):
                    for k in range(2 * QUARTERS + 1):
                        if k < 2 * QUARTERS:
                            m, q = k // QUARTERS, k % QUARTERS
                            act.activation(part[:, m, 0, quarter(q)], (qT, kT)[m][:, quarter(q)], ACT.Copy).then_inc(hi_taken, 1)
                        if k >= 1:
                            m, q = (k - 1) // QUARTERS, (k - 1) % QUARTERS
                            act.wait_ge(rest_ready, k)
                            act.activation(part[:, m, 1, quarter(q)], rest[:, (k - 1) % 2, :], ACT.Copy).then_inc(mid_taken, 1)
                    act.wait_ge(step, AT["take"])
                    act.activation(alloc[:, :], take[:, :], ACT.Sigmoid).then_inc(act_step, 1)
                    act.wait_ge(step, AT["give"])
                    act.activation(give[:, :], give[:, :], ACT.Exp).then_inc(act_step, 1)
                    for q in range(QUARTERS):
                        act.wait_ge(spreaded, 2 * QUARTERS + q + 1)
                        act.activation(FAC[:, quarter(q)], psum[:, 2 + q, :], ACT.Copy).then_inc(fac_copied, 1)

            with ExitStack() as ctx3:
                p3 = Phase(nc, ctx3, "flow_mix")
                k_tok = p3.sb("k_tok", [P, 2, PER_Q, D])
                v_tok = p3.sb("v_tok", [P, 2, PER_Q, D])
                v_one = p3.sb("v_one", [P, 2, NW * VW])
                masked = p3.sb("masked", [P, 2, H, P])
                state = p3.sb("state", [P, 2, P])
                mixed_t = p3.sb("mixed_t", [P, 2, P])
                v_zero, v_placed = p3.sem("v_zero"), p3.sem("v_placed")
                turned, tok_copied = p3.sem("turned"), p3.sem("tok_copied")
                scored, masked_ready = p3.sem("scored"), p3.sem("masked_ready")
                mixed, mixed_ready = p3.sem("mixed"), p3.sem("mixed_ready")
                stated, state_ready = p3.sem("stated"), p3.sem("state_ready")
                out_done, y_ready, u_ready = p3.sem("out_done"), p3.sem("y_ready"), p3.sem("u_ready")
                block = ctx3.enter_context(nc.Block())

                @block.sync
                def _(sp):
                    for q in range(2, QUARTERS):
                        sp.wait_ge(scored, 4 * PER_Q * (q - 1))
                        load_stacks(sp, q)

                @block.gpsimd
                def _(pool):
                    pool.memset(v_one[:, :, :], 0.0).then_inc(v_zero, 1)
                    pool.tensor_tensor(Y[:, :, :], U[:, :, :], rows[:, 0, :].unsqueeze(1).to_broadcast([P, TILES, D]),
                                       ALU.add).then_inc(u_ready, 1)
                    pool.wait_ge(v_zero, 1)
                    for t in range(TILES):
                        pool.wait_ge(tok_copied, 2 * (t // PER_Q + 1))
                        if t >= 2:
                            pool.wait_ge(mixed, t - 1)
                        pool.tensor_copy(
                            v_one[:, t % 2, :].rearrange("p (r x) -> p r x", x=VW)[:, :, 0:D]
                            .rearrange("p r (g y) -> p r g y", g=4)[:, :, :, 0:DH],
                            v_tok[:, t // PER_Q % 2, t % PER_Q, :].rearrange("p (g r d) -> p r g d", g=4, r=NW)
                        ).then_inc(v_placed, 1)

                @block.tensor
                def _(pe):
                    def turn(q, n):
                        k = 2 * q + n
                        if k >= 1:
                            pe.wait_ge(tok_copied, k)
                        for i in range(PER_Q):
                            last = pe.transpose(psum[:, 6, tile(i)], (kT, vT)[n][:, tile(q * PER_Q + i)], C["ident"])
                        last.then_inc(turned, 1)

                    def scores(t):
                        q, i = t // PER_Q, t % PER_Q
                        if i == 0:
                            pe.wait_ge(stacked[q % 2], 16 * 2 * len(PARTS) * (q // 2 + 1))
                        for g in range(4):
                            if t >= 1:
                                pe.wait_ge(masked_ready, (t - 1) * 4 + g + 1)
                            for r in range(4):
                                h = 4 * g + r
                                last = pe.matmul(psum[:, g, tile(r)], ks[:, q % 2, h, tile(i)], qs[:, q % 2, h, tile(i)],
                                                 start=True, stop=True, skip_group_check=True)
                            last.then_inc(scored, 1)

                    def project(t):
                        pe.wait_ge(mixed_ready, t + 1)
                        if t and t % PER_Q == 0:
                            pe.wait_ge(y_ready, t // PER_Q)
                        pe.matmul(psum[:, 7, tile(t % PER_Q)], mixed_t[:, t % 2, :], wo_raw[:, :], start=True,
                                  stop=True, skip_group_check=True).then_inc(out_done, 1)

                    turn(0, 0)
                    turn(0, 1)
                    scores(0)
                    for t in range(TILES):
                        q, i = t // PER_Q, t % PER_Q
                        c = t % STILES
                        if t + 1 < TILES:
                            scores(t + 1)
                        if t >= 1:
                            pe.wait_ge(state_ready, t)
                            pe.wait_ge(mixed_ready, t)
                        if c:
                            pe.matmul(psum[:, 4, 0:P], state[:, (t - 1) % 2, :], qT[:, tile(t)], start=True,
                                      stop=False, skip_group_check=True)
                        pe.wait_ge(v_placed, t + 1)
                        pe.wait_ge(masked_ready, 4 * (t + 1))
                        for r in range(NW):
                            for g in range(4):
                                last = pe.matmul(psum[32 * g:32 * g + 32, 4, 0:P],
                                                 v_one[:, t % 2, r * D + 32 * g:r * D + 32 * g + 32],
                                                 masked[:, t % 2, 4 * g + r, :], start=(c == 0 and r == 0),
                                                 stop=(r == NW - 1), skip_group_check=True)
                        last.then_inc(mixed, 1)
                        pe.matmul(psum[:, 5, 0:P], k_tok[:, q % 2, i, :], v_tok[:, q % 2, i, :], start=(c == 0),
                                  stop=True, skip_group_check=True).then_inc(stated, 1)
                        if t >= 1:
                            project(t - 1)
                        if i in (0, 1) and q + 1 < QUARTERS:
                            turn(q + 1, i)
                    project(TILES - 1)

                @block.scalar
                def _(act):
                    for k in range(2 * QUARTERS):
                        q, n = k // 2, k % 2
                        act.wait_ge(turned, k + 1)
                        if q >= 2 and n == 0:
                            act.wait_ge(stated, (q - 1) * PER_Q)
                            act.wait_ge(v_placed, (q - 1) * PER_Q)
                        act.activation((k_tok, v_tok)[n][:, q % 2, :, :], psum[:, 6, :].rearrange("p (t d) -> p t d", d=D),
                                       ACT.Copy).then_inc(tok_copied, 1)

                @block.vector
                def _(dve):

                    def mask(t):
                        for g in range(4):
                            dve.wait_ge(scored, 4 * t + g + 1)
                            if t >= 2:
                                dve.wait_ge(mixed, t - 1)
                            dve.tensor_tensor(masked[:, t % 2, 4 * g:4 * g + 4, :], psum[:, g, :].rearrange("p (r i) -> p r i", r=4),
                                              causal[:, :].unsqueeze(1).to_broadcast([P, 4, P]), ALU.mult).then_inc(masked_ready, 1)

                    def add_to_y(q):
                        dve.wait_ge(out_done, (q + 1) * PER_Q)
                        if q == 0:
                            dve.wait_ge(u_ready, 1)
                        part = Y[:, q * PER_Q:(q + 1) * PER_Q, :]
                        dve.tensor_tensor(part, part, psum[:, 7, :].rearrange("p (t d) -> p t d", d=D), ALU.add).then_inc(y_ready, 1)

                    mask(0)
                    for t in range(TILES):
                        if t + 1 < TILES:
                            mask(t + 1)
                        dve.wait_ge(mixed, t + 1)
                        if t >= 2:
                            dve.wait_ge(out_done, t - 1)
                        dve.tensor_tensor(mixed_t[:, t % 2, :], psum[:, 4, 0:P], FAC[:, tile(t)], ALU.mult).then_inc(mixed_ready, 1)
                        dve.wait_ge(stated, t + 1)
                        dve.tensor_tensor(state[:, t % 2, :], psum[:, 5, 0:P], blocks[:, :], ALU.mult).then_inc(state_ready, 1)
                        if t and t % PER_Q == 0:
                            add_to_y(t // PER_Q - 1)
                    add_to_y(QUARTERS - 1)

        with ExitStack() as ctx4:
            p4 = Phase(nc, ctx4, "flow_ffn")
            HH, HL = p4.sb("HH", [P, TOK], F32R), p4.sb("HL", [P, TOK], F32R)
            h = p4.sb("h", [P, TILES, D])
            z = p4.sb("z", [P, TILES, D])
            hidden = p4.sb("hidden", [P, 2, FB, BANK])
            channels = p4.sb("channels", [P, 2, BANK])
            norm1 = Norm(p4, "norm1", Y, h)
            norm2 = Norm(p4, "norm2", z, Y)
            scaled, affine = p4.sem("scaled"), p4.sem("affine")
            turn = Turn(p4, "turn", psum, C["ident"], lambda t: h[:, t, :], HH, HL,
                        lambda pe, q: pe.wait_ge(affine, q + 1))
            up_done, hidden_ready, down_done = p4.sem("up_done"), p4.sem("hidden_ready"), p4.sem("down_done")
            channels_ready, back, z_ready = p4.sem("channels_ready"), p4.sem("back"), p4.sem("z_ready")
            scaled2, y_ready, x_ready = (p4.sem(n) for n in ("scaled2", "y_ready", "x_ready"))
            block = ctx4.enter_context(nc.Block())

            up_banks = (4, 5, 0, 1)

            def affine_rows(dve, dst, q, g, b, first, second):
                part = dst[:, q * PER_Q:(q + 1) * PER_Q, :]
                full = [P, PER_Q, D]
                dve.tensor_tensor(part, part, rows[:, g, :].unsqueeze(1).to_broadcast(full), ALU.mult).then_inc(first, 1)
                dve.wait_ge(first, q + 1)
                return dve.tensor_tensor(part, part, rows[:, b, :].unsqueeze(1).to_broadcast(full), ALU.add)

            @block.tensor
            def _(pe):
                def up(q):
                    pe.wait_ge(turn.lo_ready, q + 1)
                    for a in range(FB):
                        k = q * FB + a
                        if k == 3:
                            pe.wait_ge(turn.lo_ready, 2)
                        if k >= 4:
                            pe.wait_ge(hidden_ready, k - 3)
                        split_product(pe, psum[:, up_banks[k % 4], :], w1_hi[:, tile(a)], w1_lo[:, tile(a)],
                                      HH[:, quarter(q)], HL[:, quarter(q)]).then_inc(up_done, 1)

                def down(q):
                    if q >= 1:
                        pe.wait_ge(channels_ready, q)
                    for a in range(FB):
                        pe.wait_ge(hidden_ready, q * FB + a + 1)
                        last = pe.matmul(psum[:, 6, :], w2_raw[:, a, :], hidden[:, q % 2, a, :], start=(a == 0),
                                         stop=(a == FB - 1), skip_group_check=True)
                    last.then_inc(down_done, 1)

                def turn_back(q):
                    pe.wait_ge(channels_ready, q + 1)
                    if q >= 1:
                        pe.wait_ge(z_ready, q)
                    for i in range(PER_Q):
                        last = pe.transpose(psum[:, 7, tile(i)], channels[:, q % 2, tile(i)], C["ident"])
                    last.then_inc(back, 1)

                turn.tensor(pe)
                for s in range(QUARTERS + 2):
                    if s < QUARTERS:
                        up(s)
                    if 1 <= s <= QUARTERS:
                        down(s - 1)
                    if s >= 2:
                        turn_back(s - 2)

            @block.scalar
            def _(act):
                norm_and_turn_scalar(act, norm1, turn)
                for s in range(QUARTERS + 3):
                    if s < QUARTERS:
                        if s >= 2:
                            act.wait_ge(down_done, s - 1)
                        for a in range(FB):
                            k = s * FB + a
                            act.wait_ge(up_done, k + 1)
                            act.activation(hidden[:, s % 2, a, :], psum[:, up_banks[k % 4], :], ACT.Gelu, bias=b1[:, a:a + 1]).then_inc(hidden_ready, 1)
                    if 1 <= s <= QUARTERS:
                        act.wait_ge(down_done, s)
                        if s >= 3:
                            act.wait_ge(back, s - 2)
                        act.activation(channels[:, (s - 1) % 2, :], psum[:, 6, :], ACT.Identity, bias=columns[:, 3:4]).then_inc(channels_ready, 1)
                    if s >= 3:
                        norm2.quarter_root(act, s - 3)

            @block.vector
            def _(dve):
                def scale(q):
                    dve.wait_ge(norm1.normed, (q + 1) * PER_Q)
                    affine_rows(dve, h, q, 1, 2, scaled, affine).then_inc(affine, 1)

                def finish(q):
                    norm2.quarter_norm(dve, q)
                    dve.wait_ge(norm2.normed, (q + 1) * PER_Q)
                    affine_rows(dve, Y, q, 3, 4, scaled2, y_ready).then_inc(y_ready, 1)
                    dve.wait_ge(y_ready, q + 1)
                    part = slice(q * PER_Q, (q + 1) * PER_Q)
                    dve.tensor_tensor(X[:, part, :], X[:, part, :], Y[:, part, :], ALU.add).then_inc(x_ready, 1)

                norm_and_turn_vector(dve, norm1, turn, scale=scale)
                norm2.set_eps(dve)
                for q in range(QUARTERS):
                    dve.wait_ge(back, q + 1)
                    part = slice(q * PER_Q, (q + 1) * PER_Q)
                    dve.tensor_tensor(z[:, part, :], h[:, part, :], psum[:, 7, :].rearrange("p (t d) -> p t d", d=D),
                                      ALU.add).then_inc(z_ready, 1)
                    dve.wait_ge(z_ready, q + 1)
                    norm2.quarter_stats(dve, q)
                    if q >= 1:
                        finish(q - 1)
                finish(QUARTERS - 1)


def gated_attention_phase(nc, psum, X, C, io):
    H, DH, TOPK, G = 8, 64, 3, 2
    PAIRS = H // G
    GROUPS = BATCH * PAIRS
    SCALE = float(DH) ** -0.5
    STEPS = STILES * G
    HD = H * DH
    QB = HD // D
    with ExitStack() as ctx:
        ph = Phase(nc, ctx, "gated")
        attended = ph.sb("attended", [P, TILES, HD])
        values = ph.sb("values", [P, TILES, HD])
        UH, UL = ph.sb("UH", [P, TOK], F32R), ph.sb("UL", [P, TOK], F32R)
        gates = ph.sb("gates", [P, TILES, H])
        wqk_hi = ph.sb("wqk_hi", [P, 2, HD], F32R)
        wqk_lo = ph.sb("wqk_lo", [P, 2, HD], F32R)
        max_dram = nc.dram_tensor("gated_max_scratch", [GROUPS, STEPS, P], F32, kind="Internal").ap()

        with ExitStack() as ctx1:
            ph1 = Phase(nc, ctx1, "gated_in")
            U = ph1.sb("U", [P, TILES, D])
            w_raw = ph1.sb("w_raw", [P, 3 * HD])
            wv_hi, wv_lo = ph1.sb("wv_hi", [P, HD], F32R), ph1.sb("wv_lo", [P, HD], F32R)
            ws_raw = ph1.sb("ws_raw", [P, H])
            ws_hi, ws_lo = ph1.sb("ws_hi", [P, H], F32R), ph1.sb("ws_lo", [P, H], F32R)
            scores = ph1.sb("scores", [P, TILES, H])
            beats = ph1.sb("beats", [P, TILES, H, H])
            ties = ph1.sb("ties", [P, TILES, H, H])
            rank = ph1.sb("rank", [P, TILES, H])
            norm = Norm(ph1, "norm", X, U)
            turn = Turn(ph1, "turn", psum, C["ident"], lambda t: U[:, t, :], UH, UL,
                        lambda pe, q: pe.wait_ge(norm.normed, (q + 1) * PER_Q))
            w_loaded, hi_ready, lo_ready = ph1.sem("w_loaded"), ph1.sem("hi_ready"), ph1.sem("lo_ready")
            logits_done, scores_ready = ph1.sem("logits_done"), ph1.sem("scores_ready")
            gate_step = ph1.sem("gate_step")
            v_done, v_copied = ph1.sem("v_done"), ph1.sem("v_copied")
            block = ctx1.enter_context(nc.Block())

            @block.sync
            def _(sp):
                sp.dma_start(ws_raw[:, :], io["L0_ffn_Ws"]).then_inc(w_loaded, 16)
                sp.dma_start(w_raw[:, 2 * HD:], io["L0_ffn_Wkv"][:, HD:]).then_inc(w_loaded, 16)
                sp.dma_start(w_raw[:, 0:HD], io["L0_ffn_Wq"]).then_inc(w_loaded, 16)
                sp.dma_start(w_raw[:, HD:2 * HD], io["L0_ffn_Wkv"][:, 0:HD]).then_inc(w_loaded, 16)

            @block.gpsimd
            def _(pool):
                split_weights(pool, [(ws_raw[:, :], ws_hi[:, :], ws_lo[:, :], 64),
                                     (w_raw[:, 2 * HD:], wv_hi[:, :], wv_lo[:, :], 64),
                                     (w_raw[:, 0:HD], wqk_hi[:, 0, :], wqk_lo[:, 0, :], 64),
                                     (w_raw[:, HD:2 * HD], wqk_hi[:, 1, :], wqk_lo[:, 1, :], 64)],
                              w_loaded, hi_ready, lo_ready)

            @block.tensor
            def _(pe):
                def logits(q):
                    if q == 0:
                        pe.wait_ge(lo_ready, 1)
                    for t in range(q * PER_Q, (q + 1) * PER_Q):
                        last = split_product(pe, psum[:, 4, t * H:(t + 1) * H], UH[:, tile(t)], UL[:, tile(t)],
                                             ws_hi[:, :], ws_lo[:, :])
                    last.then_inc(logits_done, 1)

                turn.tensor(pe, logits)
                pe.wait_ge(lo_ready, 2)
                for t in range(TILES):
                    if t >= 2:
                        pe.wait_ge(v_copied, t - 1)
                    split_product(pe, psum[:, 5 + t % 2, :], UH[:, tile(t)], UL[:, tile(t)],
                                  wv_hi[:, :], wv_lo[:, :]).then_inc(v_done, 1)

            @block.scalar
            def _(act):
                norm_and_turn_scalar(act, norm, turn)
                act.wait_ge(logits_done, QUARTERS)
                act.activation(scores[:, :, :], psum[:, 4, 0:TILES * H].rearrange("p (t h) -> p t h", h=H),
                               ACT.Sigmoid).then_inc(scores_ready, 1)
                for t in range(TILES):
                    act.wait_ge(v_done, t + 1)
                    act.activation(values[:, t, :], psum[:, 5 + t % 2, :], ACT.Copy).then_inc(v_copied, 1)

            @block.vector
            def _(dve):
                norm_and_turn_vector(dve, norm, turn)
                dve.wait_ge(scores_ready, 1)
                choose(dve, scores, beats, ties, rank, gates, C["before"], H, TOPK, gate_step)

        with ExitStack() as ctx2:
            ph2 = Phase(nc, ctx2, "gated_att")
            q2 = ph2.sb("q2", [P, 2, G, SEQ], F32R)
            ql = ph2.sb("ql", [DH + 1, 2, G, SEQ], F32R)
            k2 = ph2.sb("k2", [P, 2, G, SEQ], F32R)
            k1 = ph2.sb("k1", [DH + 1, 2, G, SEQ], F32R)
            w2_hi = ph2.sb("w2_hi", [P, 2, 2, G, 2, DH], F32R)
            w2_lo = ph2.sb("w2_lo", [P, 2, 2, G, 2, DH], F32R)
            probs = ph2.sb("probs", [P, 2, G, SEQ])
            tally = ph2.sb("tally", [P, 2, G, SEQ])
            zero = ph2.sb("zero", [P, 1])
            ones = ph2.sb("ones", [P, 32])
            maxima = ph2.sb("maxima", [P, 2, STEPS])
            top = ph2.sb("top", [P, STEPS])
            shift_t = ph2.sb("shift_t", [STEPS, P], F32R)
            inv = ph2.sb("inv", [P, STILES, G])
            sums = ph2.sb("sums", [P, SEQ])
            w2_ready = ph2.sem("w2_ready")
            ones_ready = ph2.sem("ones_ready")
            chunk_done = ph2.sem("chunk_done")
            chunk_used = ph2.sem("chunk_used")
            parts_hi = ph2.sem("parts_hi")
            parts_ready = ph2.sem("parts_ready")
            top_ready = ph2.sem("top_ready")
            shift_ready = ph2.sem("shift_ready")
            shift_copied = ph2.sem("shift_copied")
            shift_stored = ph2.sem("shift_stored")
            shift_loaded = ph2.sem("shift_loaded")
            scored = ph2.sem("scored")
            exped = ph2.sem("exped")
            mixed = ph2.sem("mixed")
            tallied = ph2.sem("tallied")
            sums_copied = ph2.sem("sums_copied")
            dens_copied = ph2.sem("dens_copied")
            inv_ready = ph2.sem("inv_ready")
            block = ctx2.enter_context(nc.Block())

            def proj_of(g):
                return [("proj", g, j, m, x) for j in range(G) for m in range(2) for x in range(2)]

            def rows_of(g):
                return [("max", g, s, x) for s in range(STEPS) for x in range(2)]

            def queue_of(g):
                proj, rows = proj_of(g), rows_of(g)
                mixed_in = proj[:5]
                for p, c in zip(proj[5:], rows):
                    mixed_in += [c, p]
                return mixed_in + rows[len(proj) - 5:] + [("shift", g)]

            def outs_of(g):
                return [("sum", g), ("den", g), ("out", g, 0), ("out", g, 1)]

            lead = queue_of(0)
            UNITS = 2 * STEPS
            EARLY = 4
            plan = []
            for n in range(GROUPS):
                ahead = queue_of(n + 1) if n + 1 < GROUPS else []
                for u in range(UNITS):
                    now = []
                    if n >= 1 and u in (8, 10, 12, 14):
                        now.append(outs_of(n - 1)[u // 2 - 4])
                    a, b = (len(ahead) * min(i, UNITS - EARLY) // (UNITS - EARLY) for i in (u, u + 1))
                    plan.append(now + ahead[a:b])
            tail = outs_of(GROUPS - 1)
            order = lead + [c for now in plan for c in now] + tail
            number = {c: i for i, c in enumerate(order)}

            @block.sync
            def _(sp):
                for g in range(GROUPS):
                    sp.wait_ge(shift_copied, g + 1)
                    sp.dma_start(max_dram[g], f32(shift_t[:, :])).then_inc(shift_stored, 16)
                    sp.wait_ge(shift_stored, 16 * (g + 1))
                    sp.dma_start(f32(ql[DH:DH + 1, g % 2, :, :].rearrange("r j t -> r (j t)")),
                                 max_dram[g:g + 1].rearrange("r x y -> r (x y)")).then_inc(shift_loaded, 16)

            @block.gpsimd
            def _(pool):
                pool.memset(ones[:, :], 1.0).then_inc(ones_ready, 1)
                pool.memset(zero[:, :], 0.0).then_inc(ones_ready, 1)
                pool.wait_ge(ones_ready, 2)
                pool.memset(f32(k1[DH:DH + 1, :, :, :]), 1.0).then_inc(ones_ready, 1)
                pool.wait_ge(ones_ready, 3)
                for n in range(GROUPS):
                    for kt in range(STILES):
                        for j in range(G):
                            pool.wait_ge(exped, 2 * (n * STEPS + kt * G + j + 1))
                            if kt == 0 and j == 0 and n >= 2:
                                pool.wait_ge(chunk_done, number[("den", n - 2)] + 1)
                            if kt:
                                pool.wait_ge(tallied, n * STEPS + (kt - 1) * G + j + 1)
                            so_far = tally[:, n % 2, j, :] if kt else zero[:, :].to_broadcast([P, SEQ])
                            pool.tensor_tensor(tally[:, n % 2, j, :], probs[:, kt % 2, j, :], so_far,
                                               ALU.add).then_inc(tallied, 1)

            def dens_of(g):
                return tally[:, g % 2, 0, 0:BANK]

            def bank_of(i):
                return 5 + i % 3

            @block.tensor
            def _(pe):
                def chunk(c):
                    i = number[c]
                    bank = bank_of(i)
                    if i >= 3:
                        pe.wait_ge(chunk_used, i - 2)
                    if c[0] == "proj":
                        _, g, j, m, x = c
                        if j == m == x == 0:
                            pe.wait_ge(w2_ready, 4 * (g + 1))
                        at = g // PAIRS * SEQ + x * BANK
                        w = [t[:, g % 2, m, j, :, :].rearrange("p c d -> p (c d)") for t in (w2_hi, w2_lo)]
                        last = split_product(pe, psum[:, bank, :], *w, UH[:, at:at + BANK], UL[:, at:at + BANK])
                    elif c[0] == "max":
                        _, g, s, x = c
                        if s == x == 0:
                            pe.wait_ge(parts_ready, g * 4 * G + 4)
                        if s == STILES and x == 0:
                            pe.wait_ge(parts_ready, (g + 1) * 4 * G)
                        j, qt = s // STILES, s % STILES
                        last = pe.matmul(psum[:, bank, :], q2[:, g % 2, j, tile(qt)],
                                         k2[:, g % 2, j, x * BANK:(x + 1) * BANK], start=True, stop=True,
                                         skip_group_check=True)
                    elif c[0] == "shift":
                        pe.wait_ge(shift_ready, c[1] + 1)
                        last = pe.transpose(psum[0:STEPS, bank, 0:P], top[:, :], C["ident"])
                    elif c[0] == "out":
                        _, g, x = c
                        pe.wait_ge(sums_copied, g + 1)
                        for i2 in range(4):
                            last = pe.transpose(psum[:, bank, tile(i2)], sums[:, tile(4 * x + i2)], C["ident"])
                    else:
                        g = c[1]
                        if c[0] == "sum":
                            pe.wait_ge(tallied, (g + 1) * STEPS)
                            for x in range(2):
                                for j in range(G):
                                    at = 32 * (2 * x + j)
                                    last = pe.matmul(psum[at:at + 32, bank, :], ones[:, :],
                                                     tally[:, g % 2, j, x * BANK:(x + 1) * BANK], start=True,
                                                     stop=True, skip_group_check=True)
                        else:
                            pe.wait_ge(dens_copied, g + 1)
                            for i2 in range(4):
                                last = pe.transpose(psum[:, bank, tile(i2)], dens_of(g)[:, tile(i2)], C["ident"])
                    last.then_inc(chunk_done, 1)

                def mix(n, kt, piece):
                    if piece == 0:
                        pe.wait_ge(exped, 2 * (n * STEPS + (kt + 1) * G))
                        if kt == 0 and n >= 1:
                            pe.wait_ge(sums_copied, n)
                    t = n // PAIRS * STILES + kt
                    flags = dict(start=(kt == 0), stop=(kt == STILES - 1), skip_group_check=True)
                    for j in range(G):
                        c0 = (n % PAIRS * G + j) * DH
                        last = pe.matmul(psum[DH * j:DH * j + DH, 3 + piece, :], values[:, t, c0:c0 + DH],
                                         probs[:, kt % 2, j, piece * BANK:(piece + 1) * BANK], **flags)
                    last.then_inc(mixed, 1)

                for c in lead:
                    chunk(c)
                pe.wait_ge(ones_ready, 3)
                for n in range(GROUPS):
                    for u in range(UNITS):
                        k = n * UNITS + u
                        kt, j, x = u // (2 * G), u // 2 % G, u % 2
                        if u == 0:
                            pe.wait_ge(shift_loaded, 16 * (n + 1))
                        if k >= 3:
                            pe.wait_ge(exped, k - 2)
                        cols = slice(x * BANK, (x + 1) * BANK)
                        o = psum[:, k % 3, :]
                        pe.matmul(o, k2[:, n % 2, j, tile(kt)], q2[:, n % 2, j, cols], start=True, stop=False,
                                  skip_group_check=True)
                        pe.matmul(o, k1[:, n % 2, j, tile(kt)], ql[:, n % 2, j, cols], start=False,
                                  stop=True, skip_group_check=True).then_inc(scored, 1)
                        for c in plan[k]:
                            chunk(c)
                        if u % (2 * G) in (1, 3) and k >= 2 * G:
                            before = (k - 2 * G) // (2 * G)
                            mix(before // STILES, before % STILES, u % (2 * G) // 2)
                for piece in range(2):
                    mix(GROUPS - 1, STILES - 1, piece)
                for c in tail:
                    chunk(c)

            @block.scalar
            def _(act):
                def proj(c):
                    _, g, j, m, x = c
                    cols = slice(x * BANK, (x + 1) * BANK)
                    act.wait_ge(chunk_done, number[c] + 1)
                    if m == 0:
                        act.activation(q2[:, g % 2, j, cols], psum[:, bank_of(number[c]), :], ACT.Copy).then_inc(parts_hi, 1)
                    else:
                        act.activation(k2[:, g % 2, j, cols], psum[:, bank_of(number[c]), :], ACT.Copy)
                        act.activation(k1[0:DH, g % 2, j, cols], psum[0:DH, bank_of(number[c]), :], ACT.Copy).then_inc(parts_hi, 1)

                def evacuate(n):
                    act.wait_ge(mixed, 2 * STILES * (n + 1))
                    if n >= 1:
                        act.wait_ge(chunk_done, number[("out", n - 1, 1)] + 1)
                    act.activation(sums[:, :], psum[:, 3:5, :].rearrange("p a b -> p (a b)"), ACT.Copy).then_inc(sums_copied, 1)

                def form_weights(g):
                    p0 = g % PAIRS * G * DH
                    if g >= 2:
                        act.wait_ge(chunk_done, number[proj_of(g - 2)[-1]] + 1)
                    for n, (dst, src) in enumerate(((w2_hi, wqk_hi), (w2_lo, wqk_lo))):
                        for c in range(2):
                            act.activation(dst[:, g % 2, :, :, c, :],
                                             src[:, :, p0:p0 + G * DH].rearrange("p m (j d) -> p m j d", j=G), ACT.Copy
                                             ).then_inc(w2_ready, 1)

                form_weights(0)
                form_weights(1)
                for c in lead:
                    if c[0] == "proj":
                        proj(c)
                for n in range(GROUPS):
                    for u in range(UNITS):
                        k = n * UNITS + u
                        kt, j, x = u // (2 * G), u // 2 % G, u % 2
                        act.wait_ge(scored, k + 1)
                        if n * STILES + kt >= 2 and x == 0:
                            act.wait_ge(mixed, 2 * (n * STILES + kt - 1))
                            act.wait_ge(tallied, (n * STILES + kt - 2) * G + j + 1)
                        act.activation(probs[:, kt % 2, j, x * BANK:(x + 1) * BANK], psum[:, k % 3, :],
                                       ACT.Exp, scale=SCALE).then_inc(exped, 1)
                        if u == 4 and n >= 1:
                            evacuate(n - 1)
                        if u == UNITS // 2 and n + 2 < GROUPS:
                            form_weights(n + 2)
                        for c in plan[k]:
                            if c[0] == "proj":
                                proj(c)
                evacuate(GROUPS - 1)

            @block.vector
            def _(dve):
                parts = 0
                for i, c in enumerate(order):
                    bank = bank_of(i)
                    if c[0] == "proj":
                        _, g, j, m, x = c
                        parts += 1
                        cols = slice(x * BANK, (x + 1) * BANK)
                        dve.wait_ge(parts_hi, parts)
                        if m == 0:
                            ins = dve.tensor_tensor(ql[0:DH, g % 2, j, cols], psum[0:DH, bank, :],
                                                    f32(q2[0:DH, g % 2, j, cols]), ALU.subtract)
                        else:
                            ins = dve.tensor_tensor(k2[DH:P, g % 2, j, cols], psum[DH:P, bank, :],
                                                    f32(k2[DH:P, g % 2, j, cols]), ALU.subtract)
                        ins.then_inc(chunk_used, 1)
                        dve.wait_ge(chunk_used, i + 1)
                        dve.sem_inc(parts_ready, 1)
                        continue
                    dve.wait_ge(chunk_done, i + 1)
                    if c[0] == "max":
                        _, g, s, x = c
                        if s == 0 and x == 0 and g >= 1:
                            dve.wait_ge(top_ready, g)
                        dve.tensor_reduce(maxima[:, x, s:s + 1], psum[:, bank, :], AX.X, ALU.max).then_inc(chunk_used, 1)
                        if s == STEPS - 1 and x == 1:
                            dve.wait_ge(chunk_used, i + 1)
                            if g >= 1:
                                dve.wait_ge(chunk_done, number[("shift", g - 1)] + 1)
                            dve.tensor_tensor(top[:, :], maxima[:, 0, :], maxima[:, 1, :], ALU.max).then_inc(top_ready, 1)
                            dve.wait_ge(top_ready, g + 1)
                            dve.sem_inc(shift_ready, 1)
                    elif c[0] == "shift":
                        g = c[1]
                        if g >= 1:
                            dve.wait_ge(shift_stored, 16 * g)
                        dve.tensor_scalar(shift_t[:, :], psum[0:STEPS, bank, 0:P], -1.0, None, ALU.mult).then_inc(chunk_used, 1)
                        dve.wait_ge(chunk_used, i + 1)
                        dve.sem_inc(shift_copied, 1)
                    elif c[0] == "sum":
                        g = c[1]
                        dve.tensor_copy(dens_of(g), psum[:, bank, :]).then_inc(chunk_used, 1)
                        dve.wait_ge(chunk_used, i + 1)
                        dve.sem_inc(dens_copied, 1)
                    elif c[0] == "den":
                        g = c[1]
                        b, h0 = g // PAIRS, g % PAIRS * G
                        if g >= 1:
                            dve.wait_ge(chunk_used, number[("out", g - 1, 1)] + 1)
                        view = psum[:, bank, :].rearrange("p (t x j r) -> p x t j r", t=4, x=2, j=G)
                        for x in range(2):
                            ins = dve.reciprocal(inv[:, 4 * x:4 * x + 4, :], view[:, x, :, :, 0])
                        ins.then_inc(inv_ready, 1)
                        dve.wait_ge(inv_ready, 2 * g + 1)
                        dve.tensor_tensor(inv[:, :, :], inv[:, :, :], gates[:, b * STILES:(b + 1) * STILES, h0:h0 + G],
                                          ALU.mult).then_inc(inv_ready, 1)
                        dve.wait_ge(inv_ready, 2 * g + 2)
                        dve.sem_inc(chunk_used, 1)
                    else:
                        _, g, x = c
                        b, h0 = g // PAIRS, g % PAIRS * G
                        t0 = b * STILES + 4 * x
                        dve.tensor_tensor(attended[:, t0:t0 + 4, h0 * DH:(h0 + G) * DH].rearrange("p t (j d) -> p t j d", d=DH),
                                          psum[:, bank, :].rearrange("p (t j d) -> p t j d", t=4, j=G),
                                          inv[:, 4 * x:4 * x + 4, :].unsqueeze(3).to_broadcast([P, 4, G, DH]),
                                          ALU.mult).then_inc(chunk_used, 1)

        with ExitStack() as ctx3:
            ph3 = Phase(nc, ctx3, "gated_out")
            att_t = ph3.sb("att_t", [P, 2, QB, BANK])
            bo = ph3.sb("bo", [H, D])
            wo_raw = ph3.sb("wo_raw", [P, QB, D])
            gates_t = ph3.sb("gates_t", [H, TOK])
            channels = ph3.sb("channels", [P, 2, BANK])
            w_loaded, gates_turned, gates_copied = ph3.sem("w_loaded"), ph3.sem("gates_turned"), ph3.sem("gates_copied")
            copied = [ph3.sem("copied_even"), ph3.sem("copied_odd")]
            turned, product, product_copied = ph3.sem("turned"), ph3.sem("product"), ph3.sem("product_copied")
            back, added = ph3.sem("back"), ph3.sem("added")
            block = ctx3.enter_context(nc.Block())

            def copy_turned(engine, odd, q):
                for a in range(odd, QB, 2):
                    k = q * QB + a
                    engine.wait_ge(turned, k + 1)
                    if q >= 2:
                        engine.wait_ge(product, q - 1)
                    dst, src = att_t[:, q % 2, a, :], psum[:, k % 4, :]
                    ins = engine.tensor_copy(dst, src) if odd else engine.activation(dst, src, ACT.Copy)
                    ins.then_inc(copied[odd], 1)

            @block.sync
            def _(sp):
                sp.dma_start(bo[:, :], io["L0_ffn_bo"]).then_inc(w_loaded, 16)
                sp.dma_start(wo_raw[:, :, :], io["L0_ffn_Wo"].rearrange("(a g) d e -> (g d) a e", g=2)).then_inc(w_loaded, 16)

            @block.tensor
            def _(pe):
                for q in range(QUARTERS):
                    if q >= 1:
                        pe.wait_ge(gates_copied, q)
                    for i in range(PER_Q):
                        last = pe.transpose(psum[0:H, 7, tile(i)], gates[:, q * PER_Q + i, :], C["ident"])
                    last.then_inc(gates_turned, 1)
                pe.wait_ge(w_loaded, 32)

                def finish(q):
                    pe.wait_ge(product_copied, q + 1)
                    if q >= 1:
                        pe.wait_ge(added, q)
                    for i in range(PER_Q):
                        last = pe.transpose(psum[:, 6, tile(i)], channels[:, q % 2, tile(i)], C["ident"])
                    last.then_inc(back, 1)

                for q in range(QUARTERS):
                    for a in range(QB):
                        k = q * QB + a
                        if k >= 4:
                            pe.wait_ge(copied[k % 2], k // 2 - 1)
                        for i in range(PER_Q):
                            last = pe.transpose(psum[:, k % 4, tile(i)],
                                                attended[:, q * PER_Q + i, a * D:(a + 1) * D], C["ident"])
                        last.then_inc(turned, 1)
                    if q >= 1:
                        finish(q - 1)
                    for engine in range(2):
                        pe.wait_ge(copied[engine], (q + 1) * QB // 2)
                    if q == 0:
                        pe.wait_ge(gates_copied, QUARTERS)
                    for a in range(QB):
                        pe.matmul(psum[:, 4 + q % 2, :], wo_raw[:, a, :], att_t[:, q % 2, a, :],
                                  start=(a == 0), stop=False, skip_group_check=True)
                    pe.matmul(psum[:, 4 + q % 2, :], bo[:, :], gates_t[:, quarter(q)], start=False, stop=True,
                              skip_group_check=True).then_inc(product, 1)
                finish(QUARTERS - 1)

            @block.scalar
            def _(act):
                for q in range(QUARTERS):
                    act.wait_ge(gates_turned, q + 1)
                    act.activation(gates_t[:, quarter(q)], psum[0:H, 7, :], ACT.Copy).then_inc(gates_copied, 1)
                for q in range(QUARTERS):
                    copy_turned(act, 0, q)

            @block.vector
            def _(dve):
                def add(q):
                    dve.wait_ge(back, q + 1)
                    part = X[:, q * PER_Q:(q + 1) * PER_Q, :]
                    dve.tensor_tensor(part, part, psum[:, 6, :].rearrange("p (t d) -> p t d", d=D),
                                      ALU.add).then_inc(added, 1)

                for q in range(QUARTERS):
                    copy_turned(dve, 1, q)
                    if q >= 1:
                        add(q - 1)
                    dve.wait_ge(product, q + 1)
                    dve.tensor_copy(channels[:, q % 2, :], psum[:, 4 + q % 2, :]).then_inc(product_copied, 1)
                add(QUARTERS - 1)


def narrow_attention_phase(nc, psum, X, C, io):
    H, DH, G = 16, 8, 4
    GROUPS = BATCH * H // G
    PARTS = ((0, 0), (0, 1), (0, 2), (1, 0), (1, 1), (2, 0))
    NR = len(PARTS)
    ROWS = NR * DH
    SCALE = float(DH) ** -0.5
    STEPS = STILES * G
    PERB = QUARTERS // BATCH
    LEAST = -3.0e38
    with ExitStack() as ctx:
        ph = Phase(nc, ctx, "narrow")
        attended = ph.sb("attended", [P, GROUPS, STILES, G * DH])
        wo_hi, wo_lo = ph.sb("wo_hi", [P, D], F32R), ph.sb("wo_lo", [P, D], F32R)
        w_loaded, w_hi_ready, w_ready = ph.sem("w_loaded"), ph.sem("w_hi_ready"), ph.sem("w_ready")
        values = ph.sb("values", [P, GROUPS, STILES, G, DH])

        K_ROWS = 96
        qs = ph.sb("qs", [K_ROWS, BATCH * H * SEQ], BF16)
        ks = ph.sb("ks", [K_ROWS, BATCH * H * SEQ], BF16)
        stacks_cleared = ph.sem("stacks_cleared")

        parts_dram = nc.dram_tensor("narrow_parts_scratch", [2, 3, P, TOK], BF16, kind="Internal").ap()
        max_dram = nc.dram_tensor("narrow_max_scratch", [GROUPS, 2 * G * STILES, P], BF16, kind="Internal").ap()
        ones_row, ones_ready = ph.sb("ones_row", [2, SEQ], BF16), ph.sem("ones_ready")
        stacked = [ph.sem(f"stacked{i}") for i in range(3)]

        def clear_stack(pool, stack, b):
            half = H * SEQ
            pool.memset(stack[:, b * half:(b + 1) * half].bitcast(F32), 0.0).then_inc(stacks_cleared, 1)

        def load_stacks(sp, piece, g0, g1):
            b, heads = g0 * G // H, (g1 - g0) * G
            h0 = g0 * G - b * H
            cols = slice(g0 * G * SEQ, g1 * G * SEQ)
            for r, (qp, kp) in enumerate(PARTS):
                for st, m, s in ((ks, 1, kp), (qs, 0, qp)):
                    sp.dma_start(st[r * DH:(r + 1) * DH, cols].rearrange("d (h t) -> d h t", t=SEQ),
                                 parts_dram[m, s][h0 * DH:(h0 + heads) * DH, b * SEQ:(b + 1) * SEQ]
                                 .rearrange("(h d) t -> d h t", d=DH)).then_inc(stacked[piece], 16)
            sp.dma_start(ks[ROWS:ROWS + 2, cols].rearrange("r (h t) -> r h t", t=SEQ),
                         ones_row[:, :].unsqueeze(1).to_broadcast([2, heads, SEQ])).then_inc(stacked[piece], 16)

        with ExitStack() as ctx1:
            ph1 = Phase(nc, ctx1, "narrow_in")
            U = attended[:, :, :, :].rearrange("p a t d -> p (a t d)").rearrange("p (t d) -> p t d", d=D)
            UH, UL = ph1.sb("UH", [P, TOK], F32R), ph1.sb("UL", [P, TOK], F32R)
            w_raw = ph1.sb("w_raw", [P, 4 * D])
            w_hi, w_lo = ph1.sb("w_hi", [P, 3 * D], F32R), ph1.sb("w_lo", [P, 3 * D], F32R)
            part = ph1.sb("part", [P, 2, 3, TOK], BF16)
            rest = ph1.sb("rest", [P, 2, BANK])
            norm = Norm(ph1, "norm", X, U)
            turn = Turn(ph1, "turn", psum, C["ident"], lambda t: U[:, t, :], UH, UL,
                        lambda pe, q: pe.wait_ge(norm.normed, (q + 1) * PER_Q))
            projected = ph1.sem("projected")
            hi_taken = ph1.sem("hi_taken")
            rest_ready = ph1.sem("rest_ready")
            mid_taken = ph1.sem("mid_taken")
            low_taken = ph1.sem("low_taken")
            v_done = ph1.sem("v_done")
            v_copied = ph1.sem("v_copied")
            parts_stored = ph1.sem("parts_stored")
            block = ctx1.enter_context(nc.Block())

            @block.sync
            def _(sp):
                sp.dma_start(w_raw[:, 0:3 * D], io["L1_attn_w_qkv"]).then_inc(w_loaded, 16)
                sp.dma_start(w_raw[:, 3 * D:], io["L1_attn_w_out"]).then_inc(w_loaded, 16)
                for b in range(BATCH):
                    sp.wait_ge(low_taken, 2 * PERB * (b + 1))
                    cols = slice(b * SEQ, (b + 1) * SEQ)
                    for m in range(2):
                        sp.dma_start(parts_dram[m, :, :, cols].rearrange("s p t -> p s t"), part[:, m, :, cols]).then_inc(parts_stored, 16)
                    sp.wait_ge(parts_stored, 32 * (b + 1))
                    if b == 0:
                        sp.wait_ge(stacks_cleared, 2)
                        sp.wait_ge(ones_ready, 1)
                        load_stacks(sp, 0, 0, 1)

            @block.gpsimd
            def _(pool):
                pool.memset(ones_row[:, :], 1.0).then_inc(ones_ready, 1)
                clear_stack(pool, ks, 0)
                split_weights(pool, [(w_raw[:, 0:3 * D], w_hi[:, :], w_lo[:, :], 32),
                                     (w_raw[:, 3 * D:], wo_hi[:, :], wo_lo[:, :], 32)], w_loaded, w_hi_ready, w_ready)
                clear_stack(pool, qs, 0)

            @block.tensor
            def _(pe):
                turn.tensor(pe)
                pe.wait_ge(w_ready, 1)
                for q in range(QUARTERS):
                    pe.wait_ge(turn.lo_ready, q + 1)
                    for m in range(2):
                        k = 2 * q + m
                        if k >= 4:
                            pe.wait_ge(rest_ready, k - 3)
                        split_product(pe, psum[:, 4 + k % 4, :], w_hi[:, tile(m)], w_lo[:, tile(m)],
                                      UH[:, quarter(q)], UL[:, quarter(q)]).then_inc(projected, 1)
                for q in range(QUARTERS):
                    for i in range(PER_Q):
                        t = q * PER_Q + i
                        last = split_product(pe, psum[:, q, tile(i)], UH[:, tile(t)], UL[:, tile(t)],
                                             w_hi[:, tile(2)], w_lo[:, tile(2)])
                    last.then_inc(v_done, 1)

            @block.scalar
            def _(act):
                norm_and_turn_scalar(act, norm, turn)
                for q in range(QUARTERS):
                    for m in range(2):
                        k = 2 * q + m
                        act.wait_ge(projected, k + 1)
                        act.activation(part[:, m, 0, quarter(q)], psum[:, 4 + k % 4, :], ACT.Copy).then_inc(hi_taken, 1)
                        act.wait_ge(rest_ready, k + 1)
                        act.activation(part[:, m, 1, quarter(q)], rest[:, k % 2, :], ACT.Copy).then_inc(mid_taken, 1)
                for q in range(QUARTERS):
                    act.wait_ge(v_done, q + 1)
                    b, s0 = q * PER_Q // STILES, q * PER_Q % STILES
                    last = None
                    for i in range(PER_Q):
                        last = act.activation(values[:, b * G:(b + 1) * G, s0 + i, :, :],
                                              psum[:, q, tile(i)].rearrange("p (a g d) -> p a g d", a=G, g=G),
                                              ACT.Copy)
                    last.then_inc(v_copied, 1)

            @block.vector
            def _(dve):
                norm_and_turn_vector(dve, norm, turn)
                for q in range(QUARTERS):
                    for m in range(2):
                        k = 2 * q + m
                        dve.wait_ge(hi_taken, k + 1)
                        if k >= 2:
                            dve.wait_ge(mid_taken, k - 1)
                            dve.wait_ge(low_taken, k - 1)
                        dve.tensor_tensor(rest[:, k % 2, :], psum[:, 4 + k % 4, :], part[:, m, 0, quarter(q)],
                                          ALU.subtract).then_inc(rest_ready, 1)
                        dve.wait_ge(mid_taken, k + 1)
                        dve.tensor_tensor(part[:, m, 2, quarter(q)], rest[:, k % 2, :], part[:, m, 1, quarter(q)],
                                          ALU.subtract).then_inc(low_taken, 1)

        with ExitStack() as ctx2:
            ph2 = Phase(nc, ctx2, "narrow_att")
            probs = ph2.sb("probs", [P, 2, G, SEQ])
            v_ones = ph2.sb("v_ones", [P, 2, STILES, G, 32])
            maxima = ph2.sb("maxima", [P, 2, 2, STEPS])
            top = ph2.sb("top", [P, STEPS])
            shift = ph2.sb("shift", [P, 2 * STEPS], BF16)
            shift_t = ph2.sb("shift_t", [2 * STEPS, P], BF16)
            sums = ph2.sb("sums", [P, SEQ])
            inv = ph2.sb("inv", [P, 4 * G])
            half = ph2.sb("half", [P, 2, BANK])
            running = ph2.sb("running", [P, 2, BANK], BF16)
            v_zero = ph2.sem("v_zero")
            v_base = ph2.sem("v_base")
            v_ready = ph2.sem("v_ready")
            chunk_done = ph2.sem("chunk_done")
            chunk_used = ph2.sem("chunk_used")
            top_ready = ph2.sem("top_ready")
            shift_hi = ph2.sem("shift_hi")
            shift_ready = ph2.sem("shift_ready")
            shift_copied = ph2.sem("shift_copied")
            shift_stored = ph2.sem("shift_stored")
            shift_loaded = ph2.sem("shift_loaded")
            half_copied = ph2.sem("half_copied")
            kept = ph2.sem("kept")
            scored = ph2.sem("scored")
            exped = ph2.sem("exped")
            mixed = ph2.sem("mixed")
            sums_copied = ph2.sem("sums_copied")
            inv_ready = ph2.sem("inv_ready")
            block = ctx2.enter_context(nc.Block())

            UNITS = 2 * STEPS
            EARLY = 8
            queue = []
            for g in range(GROUPS):
                queue += [("max", g, s, x) for s in range(STEPS) for x in range(2)] + [("shift", g)]
            n_lead = UNITS + 1 + EARLY
            lead, queue = queue[:n_lead], queue[n_lead:]
            plan = []
            for k in range(GROUPS * UNITS):
                n, u = k // UNITS, k % UNITS
                now = [("out", n - 1, (u - 16) // 4)] if n >= 1 and u in (16, 20) else []
                a, b = (min(len(queue), i * (UNITS + 1) // UNITS) for i in (k, k + 1))
                plan.append(now + queue[a:b])
            tail = [("out", GROUPS - 1, 0), ("out", GROUPS - 1, 1)]
            order = lead + [c for now in plan for c in now] + tail
            number = {c: i for i, c in enumerate(order)}
            paired = [c[1:3] for i, c in enumerate(order) if c[0] == "max" and c[3] == 0
                      and i + 1 < n_lead]
            pair_index = {step: i for i, step in enumerate(paired)}

            def copied_half(c):
                return c[0] == "max" and c[3] == 0 and c[1:3] in pair_index

            def scan_number(n):
                return number[("max",) + paired[n] + (1,)]

            def bank_of(i):
                return i % 8 if i < n_lead else 5 + i % 3

            def held_before(i):
                return next((p for p in range(i - 1, max(i - 16, -1), -1) if bank_of(p) == bank_of(i)), None)

            def head_tok(g, s):
                return (g * G + s % G) * SEQ

            @block.sync
            def _(sp):
                load_stacks(sp, 1, 1, GROUPS // BATCH)
                sp.wait_ge(stacks_cleared, 4)
                load_stacks(sp, 2, GROUPS // BATCH, GROUPS)
                for g in range(GROUPS):
                    sp.wait_ge(shift_copied, g + 1)
                    sp.dma_start(max_dram[g], shift_t[:, :]).then_inc(shift_stored, 16)
                    sp.wait_ge(shift_stored, 16 * (g + 1))
                    sp.dma_start(qs[ROWS:ROWS + 2, g * G * SEQ:(g + 1) * G * SEQ],
                                 max_dram[g].rearrange("(r x) y -> r (x y)", r=2)).then_inc(shift_loaded, 16)

            @block.gpsimd
            def _(pool):
                pool.memset(v_ones[:, :, :, :, :], 0.0).then_inc(v_zero, 1)
                pool.wait_ge(v_zero, 1)
                pool.memset(v_ones[:, :, :, :, DH:DH + 1], 1.0).then_inc(v_base, 1)
                for stack in (ks, qs):
                    clear_stack(pool, stack, 1)
                pool.wait_ge(v_base, 1)
                for n in range(GROUPS):
                    if n >= 2:
                        pool.wait_ge(mixed, (n - 1) * STILES * 2)
                    pool.tensor_copy(v_ones[:, n % 2, :, :, 0:DH], values[:, n, :, :, :]).then_inc(v_ready, 1)

            @block.tensor
            def _(pe):
                def wait_free(p):
                    if p is None:
                        return
                    if copied_half(order[p]):
                        pe.wait_ge(half_copied, pair_index[order[p][1:3]] + 1)
                    else:
                        pe.wait_ge(chunk_used, p + 1)

                def chunk(c):
                    i = number[c]
                    bank = bank_of(i)
                    wait_free(held_before(i))
                    if c[0] == "max":
                        _, g, s, x = c
                        if s == 0 and x == 0 and g in (0, 1, GROUPS // BATCH):
                            pe.wait_ge(stacked[(0, 1, GROUPS // BATCH).index(g)], 16 * (2 * NR + 1))
                        at = head_tok(g, s)
                        last = pe.matmul(psum[:, bank, :], qs[:, at + s // G * P:at + s // G * P + P],
                                         ks[:, at + x * BANK:at + (x + 1) * BANK], start=True, stop=True,
                                         skip_group_check=True)
                    elif c[0] == "shift":
                        pe.wait_ge(shift_ready, c[1] + 1)
                        last = pe.transpose(psum[:, bank, :].bitcast(BF16)[0:2 * STEPS, 0:P], shift[:, :], C["ident_bf"])
                    else:
                        _, g, x = c
                        pe.wait_ge(sums_copied, g + 1)
                        for i2 in range(4):
                            last = pe.transpose(psum[:, bank, tile(i2)], sums[:, tile(4 * x + i2)], C["ident"])
                    last.then_inc(chunk_done, 1)

                def mix(n, kt, x):
                    if x == 0:
                        pe.wait_ge(exped, 2 * (n * STEPS + (kt + 1) * G))
                        if kt == 0:
                            pe.wait_ge(v_ready, n + 1)
                            if n >= 1:
                                pe.wait_ge(sums_copied, n)
                    for j in range(G):
                        last = pe.matmul(psum[32 * j:32 * j + 32, 3 + x, :], v_ones[:, n % 2, kt, j, :],
                                         probs[:, kt % 2, j, x * BANK:(x + 1) * BANK],
                                         start=(kt == 0), stop=(kt == STILES - 1), skip_group_check=True)
                    last.then_inc(mixed, 1)

                for c in lead:
                    chunk(c)
                for p in range(n_lead - 8, n_lead):
                    if bank_of(p) < 5:
                        wait_free(p)
                for n in range(GROUPS):
                    for u in range(UNITS):
                        k = n * UNITS + u
                        kt, j, x = u // (2 * G), u // 2 % G, u % 2
                        if u == 0:
                            pe.wait_ge(shift_loaded, 16 * (n + 1))
                        if k >= 3:
                            pe.wait_ge(exped, k - 2)
                        at = head_tok(n, j)
                        pe.matmul(psum[:, k % 3, :], ks[:, at + kt * P:at + kt * P + P],
                                  qs[:, at + x * BANK:at + (x + 1) * BANK], start=True, stop=True,
                                  skip_group_check=True).then_inc(scored, 1)
                        for c in plan[k]:
                            chunk(c)
                        if u % (2 * G) in (2, 6) and k >= 2 * G:
                            before = (k - 2 * G) // (2 * G)
                            mix(before // STILES, before % STILES, u % (2 * G) // 4)
                mix(GROUPS - 1, STILES - 1, 0)
                mix(GROUPS - 1, STILES - 1, 1)
                for c in tail:
                    chunk(c)

            def evacuate(act, n):
                act.wait_ge(mixed, 2 * STILES * (n + 1))
                if n >= 1:
                    act.wait_ge(chunk_done, number[("out", n - 1, 1)] + 1)
                act.activation(sums[:, :], psum[:, 3:5, :].rearrange("p a b -> p (a b)"), ACT.Copy).then_inc(sums_copied, 1)

            @block.scalar
            def _(act):
                def copy_half(c):
                    n = pair_index[c[1:3]]
                    act.wait_ge(chunk_done, number[c] + 1)
                    if n >= 2:
                        act.wait_ge(chunk_used, scan_number(n - 2) + 1)
                    act.activation(half[:, n % 2, :], psum[:, bank_of(number[c]), :], ACT.Copy).then_inc(half_copied, 1)

                for c in lead:
                    if copied_half(c):
                        copy_half(c)
                for n in range(GROUPS):
                    for u in range(UNITS):
                        k = n * UNITS + u
                        kt, j, x = u // (2 * G), u // 2 % G, u % 2
                        act.wait_ge(scored, k + 1)
                        if n * STILES + kt >= 2 and j == x == 0:
                            act.wait_ge(mixed, 2 * (n * STILES + kt - 1))
                        act.activation(probs[:, kt % 2, j, x * BANK:(x + 1) * BANK], psum[:, k % 3, :],
                                       ACT.Exp, scale=SCALE).then_inc(exped, 1)
                        if u == 8 and n >= 1:
                            evacuate(act, n - 1)
                evacuate(act, GROUPS - 1)

            @block.vector
            def _(dve):
                def column(s):
                    return slice((s % G) * STILES + s // G, (s % G) * STILES + s // G + 1)

                def keep(n):
                    g, s = paired[n]
                    dve.wait_ge(chunk_used, scan_number(n) + 1)
                    dve.tensor_copy(maxima[:, g % 2, :, column(s)],
                                    running[:, n % 2, BANK - 1:BANK].unsqueeze(1).to_broadcast([P, 2, 1])).then_inc(kept, 1)

                to_keep = []
                for i, c in enumerate(order):
                    bank = bank_of(i)
                    if copied_half(c):
                        continue
                    if c[0] == "max":
                        _, g, s, x = c
                        dve.wait_ge(chunk_done, i + 1)
                        if s == 0 and g >= 2:
                            dve.wait_ge(top_ready, g - 1)
                        if c[1:3] in pair_index:
                            n = pair_index[c[1:3]]
                            dve.wait_ge(half_copied, n + 1)
                            if n >= 2:
                                dve.wait_ge(kept, n - 1)
                            dve.tensor_tensor_scan(running[:, n % 2, :], psum[:, bank, :], half[:, n % 2, :], LEAST,
                                                   ALU.max, ALU.max).then_inc(chunk_used, 2)
                            to_keep.append(n)
                            if len(to_keep) == 2:
                                keep(to_keep.pop(0))
                        else:
                            dve.tensor_reduce(maxima[:, g % 2, x, column(s)], psum[:, bank, :], AX.X,
                                              ALU.max).then_inc(chunk_used, 1)
                        if s == STEPS - 1 and x == 1:
                            while to_keep:
                                keep(to_keep.pop(0))
                            dve.wait_ge(chunk_used, i + 1)
                            dve.wait_ge(kept, sum(p[0] <= g for p in paired))
                            dve.tensor_tensor(top[:, :], maxima[:, g % 2, 0, :], maxima[:, g % 2, 1, :], ALU.max).then_inc(top_ready, 1)
                            dve.wait_ge(top_ready, g + 1)
                            if g >= 1:
                                dve.wait_ge(chunk_done, number[("shift", g - 1)] + 1)
                            dve.tensor_scalar(shift[:, 0:STEPS], top[:, :], -1.0, None, ALU.mult).then_inc(shift_hi, 1)
                            dve.wait_ge(shift_hi, g + 1)
                            dve.scalar_tensor_tensor(shift[:, STEPS:], top[:, :], -1.0, shift[:, 0:STEPS],
                                                     ALU.mult, ALU.subtract).then_inc(shift_ready, 1)
                    elif c[0] == "shift":
                        g = c[1]
                        dve.wait_ge(chunk_done, i + 1)
                        if g >= 1:
                            dve.wait_ge(shift_stored, 16 * g)
                        dve.tensor_copy(shift_t[:, :], psum[:, bank, :].bitcast(BF16)[0:2 * STEPS, 0:P]).then_inc(chunk_used, 1)
                        dve.wait_ge(chunk_used, i + 1)
                        dve.sem_inc(shift_copied, 1)
                    else:
                        _, g, x = c
                        dve.wait_ge(chunk_done, i + 1)
                        dve.wait_ge(chunk_used, i)
                        view = psum[:, bank, :].rearrange("p (t j d) -> p t j d", t=4, j=G)
                        dve.reciprocal(inv[:, :].rearrange("p (t j) -> p t j", j=G), view[:, :, :, DH]).then_inc(inv_ready, 1)
                        dve.wait_ge(inv_ready, 2 * g + x + 1)
                        dve.tensor_tensor(attended[:, g, 4 * x:4 * x + 4, :].rearrange("p t (j d) -> p t j d", d=DH),
                                          view[:, :, :, 0:DH],
                                          inv[:, :].rearrange("p (t j) -> p t j", j=G).unsqueeze(3).to_broadcast([P, 4, G, DH]),
                                          ALU.mult).then_inc(chunk_used, 1)

        with ExitStack() as ctx3:
            ph3 = Phase(nc, ctx3, "narrow_out")
            UH, UL = ph3.sb("AH", [P, TOK], F32R), ph3.sb("AL", [P, TOK], F32R)
            gathered = ph3.sb("gathered", [P, TILES, D])
            gathered_ready = ph3.sem("gathered_ready")
            turn = Turn(ph3, "turn", psum, C["ident"], lambda t: gathered[:, t, :], UH, UL,
                        lambda pe, q: pe.wait_ge(gathered_ready, q + 1))
            project_and_add(nc, ctx3, ph3, psum, turn, X, [(UH, UL, wo_hi[:, :], wo_lo[:, :])],
                            gather=(gathered, attended, gathered_ready, G))


def experts_phase(nc, psum, X, C, io, out, stored):
    E, TOPK, HID = 8, 2, io["L1_ffn_up_w"].shape[2]
    FB = HID // P
    ALLE = E + 1
    with ExitStack() as ctx:
        ph = Phase(nc, ctx, "moe")
        U = ph.sb("U", [P, TILES, D])
        UH, UL = ph.sb("UH", [P, TOK], F32R), ph.sb("UL", [P, TOK], F32R)
        raw_up = ph.sb("raw_up", [P, 2, HID])
        raw_down = ph.sb("raw_down", [P, 2, FB, D])
        up_hi = ph.sb("up_hi", [P, 2, HID], F32R)
        up_lo = ph.sb("up_lo", [P, 2, HID], F32R)
        down_hi = ph.sb("down_hi", [P, 2, FB, D], F32R)
        down_lo = ph.sb("down_lo", [P, 2, FB, D], F32R)
        up_bias = ph.sb("up_bias", [P, ALLE, FB])
        down_bias = ph.sb("down_bias", [P, ALLE])
        gate_raw = ph.sb("gate_raw", [P, E])
        gate_hi = ph.sb("gate_hi", [P, E], F32R)
        gate_lo = ph.sb("gate_lo", [P, E], F32R)
        gate_bias = ph.sb("gate_bias", [P, E])
        logits = ph.sb("logits", [P, TILES, E])
        scores = ph.sb("scores", [P, TILES, E])
        rank = ph.sb("rank", [P, TILES, E])
        beats = ph.sb("beats", [P, TILES, E, E])
        ties = ph.sb("ties", [P, TILES, E, E])
        chosen = ph.sb("chosen", [P, TILES, E])
        total = ph.sb("total", [P, TILES])
        share = ph.sb("share", [P, TILES])
        mixw = ph.sb("mixw", [P, TILES, E])
        mixw_t = ph.sb("mixw_t", [P, P])
        mixb = ph.sb("mixb", [P, 2, TOK])
        hidden = ph.sb("hidden", [P, 2, FB, BANK])
        hidden_hi = ph.sb("hidden_hi", [P, 2, FB, BANK], F32R)
        hidden_lo = ph.sb("hidden_lo", [P, 2, FB, BANK], F32R)
        term = ph.sb("term", [P, 2, BANK])
        acc = ph.sb("acc", [P, TOK])
        least = ph.sb("least", [P, TILES])
        peak = ph.sb("peak", [P, TILES])
        peak_eps = ph.sb("peak_eps", [P, TILES])
        inv_peak = ph.sb("inv_peak", [P, TILES])
        scr = nc.dram_tensor("moe_mix_scratch", [P, P], F32, kind="Internal").ap()

        norm = Norm(ph, "norm", X, U)
        turn = Turn(ph, "turn", psum, C["ident"], lambda t: U[:, t, :], UH, UL,
                    lambda pe, q: pe.wait_ge(norm.normed, (q + 1) * PER_Q))
        small_loaded = ph.sem("small_loaded")
        up_loaded = [ph.sem(f"up_loaded{i}") for i in range(2)]
        down_loaded = [ph.sem(f"down_loaded{i}") for i in range(2)]
        gate_hi_ready = ph.sem("gate_hi_ready")
        gate_ready = ph.sem("gate_ready")
        up_hi_ready = ph.sem("up_hi_ready")
        up_ready = ph.sem("up_ready")
        down_hi_ready = ph.sem("down_hi_ready")
        down_ready = ph.sem("down_ready")
        hidden_hi_ready = ph.sem("hidden_hi_ready")
        hidden_lo_ready = ph.sem("hidden_lo_ready")
        logits_done = ph.sem("logits_done")
        logits_ready = ph.sem("logits_ready")
        scores_ready = ph.sem("scores_ready")
        gate_step = ph.sem("gate_step")
        mix_turned = ph.sem("mix_turned")
        mix_copied = ph.sem("mix_copied")
        mix_stored = ph.sem("mix_stored")
        mixb_loaded = [ph.sem(f"mixb_loaded{i}") for i in range(2)]
        up_done = ph.sem("up_done")
        hidden_ready = ph.sem("hidden_ready")
        down_done = ph.sem("down_done")
        term_ready = ph.sem("term_ready")
        acc_ready = ph.sem("acc_ready")
        acc_turned = ph.sem("acc_turned")
        peak_step = ph.sem("peak_step")
        result_ready = ph.sem("result_ready")
        GATE_STEPS = 10

        def up_src(e):
            return io["L1_ffn_up_w"][e] if e < E else io["L1_ffn_sw_up"]

        def down_src(e):
            w = io["L1_ffn_down_w"][e] if e < E else io["L1_ffn_sw_down"]
            return w.rearrange("(a p) n -> p a n", p=P)

        out_v = out.rearrange("b (t p) d -> p (b t) d", p=P)
        block = ctx.enter_context(nc.Block())

        def mixb_load(sp, n):
            if n >= 3:
                sp.wait_ge(term_ready, (n - 1) * QUARTERS)
            src = scr.rearrange("(t e) p -> e t p", e=E)[n - 1]
            sp.dma_start(mixb[:, n % 2, :].rearrange("p (t k) -> p t k", k=P),
                         src.partition_broadcast(P)).then_inc(mixb_loaded[n % 2], 16)

        @block.sync
        def _(sp):
            with nc.allow_non_contiguous_dma(reason="small bias columns"):
                sp.dma_start(gate_raw[:, :], io["L1_ffn_gate_w"]).then_inc(small_loaded, 16)
                sp.dma_start(gate_bias[:, :], io["L1_ffn_bias"].partition_broadcast(P)).then_inc(small_loaded, 16)
                sp.dma_start(up_bias[:, 0:E, :], io["L1_ffn_up_b"].rearrange("e (a p) -> p e a", p=P)).then_inc(small_loaded, 16)
                sp.dma_start(up_bias[:, E, :], io["L1_ffn_sb_up"].rearrange("(a p) -> p a", p=P)).then_inc(small_loaded, 16)
                sp.dma_start(down_bias[:, 0:E], io["L1_ffn_down_b"].rearrange("e p -> p e")).then_inc(small_loaded, 16)
                sp.dma_start(down_bias[:, E:E + 1], io["L1_ffn_sb_down"].rearrange("(p a) -> p a", a=1)).then_inc(small_loaded, 16)
            for n in range(ALLE):
                e = (n + E) % ALLE
                if n >= 2:
                    sp.wait_ge(up_ready, n - 1)
                    sp.wait_ge(down_ready, n - 1)
                sp.dma_start(raw_up[:, n % 2, :], up_src(e)).then_inc(up_loaded[n % 2], 16)
                sp.dma_start(raw_down[:, n % 2, :, :], down_src(e)).then_inc(down_loaded[n % 2], 16)
                if n == 1:
                    sp.wait_ge(mix_copied, 1)
                    sp.dma_start(scr, mixw_t[:, :]).then_inc(mix_stored, 16)
                    sp.wait_ge(mix_stored, 16)
                if n >= 1:
                    mixb_load(sp, n)
            for q in range(QUARTERS):
                sp.wait_ge(result_ready, q + 1)
                sp.dma_start(out_v[:, q * PER_Q:(q + 1) * PER_Q, :],
                             X[:, q * PER_Q:(q + 1) * PER_Q, :]).then_inc(stored, 16)
            sp.wait_ge(stored, 16 * QUARTERS)

        @block.gpsimd
        def _(pool):
            pool.wait_ge(small_loaded, 16 * 6)
            pool.tensor_copy(gate_hi[:, :], gate_raw[:, :]).then_inc(gate_hi_ready, 1)
            pool.wait_ge(gate_hi_ready, 1)
            pool.tensor_tensor(gate_lo[:, :], gate_raw[:, :], f32(gate_hi[:, :]), ALU.subtract).then_inc(gate_ready, 1)
            for n in range(ALLE):
                pool.wait_ge(up_loaded[n % 2], 16 * (n // 2 + 1))
                if n >= 2:
                    pool.wait_ge(up_done, (n - 1) * QUARTERS * FB)
                pool.tensor_copy(up_hi[:, n % 2, :], raw_up[:, n % 2, :]).then_inc(up_hi_ready, 1)
                pool.wait_ge(up_hi_ready, n + 1)
                pool.tensor_tensor(up_lo[:, n % 2, :], raw_up[:, n % 2, :], f32(up_hi[:, n % 2, :]),
                                   ALU.subtract).then_inc(up_ready, 1)
                pool.wait_ge(down_loaded[n % 2], 16 * (n // 2 + 1))
                if n >= 2:
                    pool.wait_ge(down_done, (n - 1) * QUARTERS)
                pool.tensor_copy(down_hi[:, n % 2, :, :], raw_down[:, n % 2, :, :]).then_inc(down_hi_ready, 1)
                pool.wait_ge(down_hi_ready, n + 1)
                pool.tensor_tensor(down_lo[:, n % 2, :, :], raw_down[:, n % 2, :, :], f32(down_hi[:, n % 2, :, :]),
                                   ALU.subtract).then_inc(down_ready, 1)

        @block.tensor
        def _(pe):
            def gate_logits(q):
                if q == 0:
                    pe.wait_ge(gate_ready, 1)
                for t in range(q * PER_Q, (q + 1) * PER_Q):
                    last = split_product(pe, psum[:, 4, t * E:(t + 1) * E], UH[:, tile(t)], UL[:, tile(t)],
                                         gate_hi[:, :], gate_lo[:, :])
                last.then_inc(logits_done, 1)

            turn.tensor(pe, gate_logits)

            def up(n, q):
                if q == 0:
                    pe.wait_ge(up_ready, n + 1)
                for a in range(FB):
                    k = (n * QUARTERS + q) * FB + a
                    if k >= 4:
                        pe.wait_ge(hidden_ready, k - 3)
                    split_product(pe, psum[:, a, :], up_hi[:, n % 2, tile(a)], up_lo[:, n % 2, tile(a)],
                                  UH[:, quarter(q)], UL[:, quarter(q)]).then_inc(up_done, 1)

            def down(n, q):
                k = n * QUARTERS + q
                if q == 0:
                    pe.wait_ge(down_ready, n + 1)
                if k == 0:
                    pe.wait_ge(mix_copied, 1)
                if k >= 2:
                    pe.wait_ge(term_ready, k - 1)
                for a in range(FB):
                    pe.wait_ge(hidden_lo_ready, k * FB + a + 1)
                    last = split_product(pe, psum[:, 6 + k % 2, :], down_hi[:, n % 2, a, :], down_lo[:, n % 2, a, :],
                                         hidden_hi[:, k % 2, a, :], hidden_lo[:, k % 2, a, :],
                                         start=(a == 0), stop=(a == FB - 1))
                last.then_inc(down_done, 1)

            steps = [(n, q) for n in range(ALLE) for q in range(QUARTERS)]
            for k, (n, q) in enumerate(steps):
                up(n, q)
                if k == 0:
                    pe.wait_ge(gate_step, GATE_STEPS)
                    pe.transpose(psum[:, 5, 0:P], mixw[:, :, :].rearrange("p t e -> p (t e)"),
                                 C["ident"]).then_inc(mix_turned, 1)
                if k >= 1:
                    down(*steps[k - 1])
            down(*steps[-1])
            for q in range(QUARTERS):
                pe.wait_ge(acc_ready, (ALLE - 2) * QUARTERS + q + 1)
                if q == 0:
                    pe.wait_ge(hidden_ready, ALLE * QUARTERS * FB)
                for i in range(PER_Q):
                    last = pe.transpose(psum[:, q, tile(i)], acc[:, tile(q * PER_Q + i)], C["ident"])
                last.then_inc(acc_turned, 1)

        @block.scalar
        def _(act):
            norm_and_turn_scalar(act, norm, turn)
            act.wait_ge(logits_ready, 1)
            act.activation(scores[:, :, :], logits[:, :, :], ACT.Sigmoid).then_inc(scores_ready, 1)
            for n in range(ALLE):
                e = (n + E) % ALLE
                for q in range(QUARTERS):
                    k = n * QUARTERS + q
                    if k >= 2:
                        act.wait_ge(hidden_lo_ready, (k - 1) * FB)
                        act.wait_ge(down_done, k - 1)
                    for a in range(FB + 1):
                        if a < FB:
                            act.wait_ge(up_done, k * FB + a + 1)
                            act.activation(hidden[:, k % 2, a, :], psum[:, a, :], ACT.Gelu,
                                           bias=up_bias[:, e, a:a + 1]).then_inc(hidden_ready, 1)
                        if a >= 1:
                            act.wait_ge(hidden_ready, k * FB + a)
                            act.activation(hidden_hi[:, k % 2, a - 1, :], hidden[:, k % 2, a - 1, :],
                                           ACT.Copy).then_inc(hidden_hi_ready, 1)
                    if k == 0:
                        act.wait_ge(mix_turned, 1)
                        act.activation(mixw_t[:, :], psum[:, 5, 0:P], ACT.Copy).then_inc(mix_copied, 1)

        @block.vector
        def _(dve):
            norm_and_turn_vector(dve, norm, turn)
            dve.wait_ge(small_loaded, 16 * 6)
            dve.wait_ge(logits_done, QUARTERS)
            dve.tensor_tensor(logits[:, :, :], psum[:, 4, 0:TILES * E].rearrange("p (t e) -> p t e", e=E),
                              gate_bias[:, :].unsqueeze(1).to_broadcast([P, TILES, E]),
                              ALU.add).then_inc(logits_ready, 1)
            dve.wait_ge(scores_ready, 1)
            choose(dve, scores, beats, ties, rank, chosen, C["before"], E, TOPK, gate_step)
            dve.wait_ge(gate_step, 6)
            dve.tensor_reduce(total[:, :], chosen[:, :, :], AX.X, ALU.add).then_inc(gate_step, 1)
            dve.wait_ge(gate_step, 7)
            dve.tensor_scalar(share[:, :], total[:, :], 1e-6, 10.0, ALU.add, ALU.mult).then_inc(gate_step, 1)
            dve.wait_ge(gate_step, 8)
            dve.reciprocal(total[:, :], share[:, :]).then_inc(gate_step, 1)
            dve.wait_ge(gate_step, 9)
            dve.tensor_tensor(mixw[:, :, :], chosen[:, :, :],
                              total[:, :].unsqueeze(2).to_broadcast([P, TILES, E]), ALU.mult).then_inc(gate_step, 1)
            def low_parts(k):
                for a in range(FB):
                    dve.wait_ge(hidden_hi_ready, k * FB + a + 1)
                    if k >= 2:
                        dve.wait_ge(down_done, k - 1)
                    dve.tensor_tensor(hidden_lo[:, k % 2, a, :], hidden[:, k % 2, a, :], f32(hidden_hi[:, k % 2, a, :]),
                                      ALU.subtract).then_inc(hidden_lo_ready, 1)

            def add_term(k):
                n, q = k // QUARTERS, k % QUARTERS
                e = (n + E) % ALLE
                dve.wait_ge(down_done, k + 1)
                if n == 0:
                    dve.tensor_scalar(acc[:, quarter(q)], psum[:, 6 + k % 2, :], down_bias[:, e:e + 1],
                                      0.1, ALU.add, ALU.mult).then_inc(term_ready, 1)
                    return
                if q == 0:
                    dve.wait_ge(mixb_loaded[n % 2], 16 * ((n + 1) // 2))
                if n >= 2:
                    dve.wait_ge(acc_ready, (n - 2) * QUARTERS + q + 1)
                dve.scalar_tensor_tensor(term[:, k % 2, :], psum[:, 6 + k % 2, :], down_bias[:, e:e + 1],
                                         mixb[:, n % 2, quarter(q)], ALU.add, ALU.mult).then_inc(term_ready, 1)
                dve.wait_ge(term_ready, k + 1)
                dve.tensor_tensor(acc[:, quarter(q)], acc[:, quarter(q)], term[:, k % 2, :],
                                  ALU.add).then_inc(acc_ready, 1)

            for k in range(ALLE * QUARTERS):
                low_parts(k)
                if k >= 1:
                    add_term(k - 1)
            add_term(ALLE * QUARTERS - 1)
            for q in range(QUARTERS):
                part = slice(q * PER_Q, (q + 1) * PER_Q)
                dve.wait_ge(acc_turned, q + 1)
                turned = psum[:, q, :].rearrange("p (t d) -> p t d", d=D)
                dve.tensor_reduce(peak[:, part], turned, AX.X, ALU.max).then_inc(peak_step, 1)
                dve.tensor_reduce(least[:, part], turned, AX.X, ALU.min).then_inc(peak_step, 1)
                dve.wait_ge(peak_step, 5 * q + 2)
                dve.scalar_tensor_tensor(peak_eps[:, part], least[:, part], -1.0, peak[:, part], ALU.mult,
                                         ALU.max).then_inc(peak_step, 1)
                dve.wait_ge(peak_step, 5 * q + 3)
                dve.tensor_scalar(peak[:, part], peak_eps[:, part], 1e-6, None, ALU.add).then_inc(peak_step, 1)
                dve.wait_ge(peak_step, 5 * q + 4)
                dve.reciprocal(inv_peak[:, part], peak[:, part]).then_inc(peak_step, 1)
                dve.wait_ge(peak_step, 5 * q + 5)
                for i in range(PER_Q):
                    t = q * PER_Q + i
                    last = dve.scalar_tensor_tensor(X[:, t, :], psum[:, q, tile(i)], inv_peak[:, t:t + 1],
                                                    X[:, t, :], ALU.mult, ALU.add)
                last.then_inc(result_ready, 1)


def program(nc, io, const, out):
    with ExitStack() as ctx:
        Phase.sems = []

        def sb(name, shape, dt=F32):
            return ctx.enter_context(nc.sbuf_tensor(name, shape, dt))

        psum = ctx.enter_context(nc.psum_tensor("psum", [P, 8, BANK], F32))
        X = sb("X", [P, TILES, D])
        ident = sb("ident", [P, P])
        ident_bf = sb("ident_bf", [P, P], BF16)
        before = sb("before", [P, 8, 8])
        C = {"ident": ident[:, :], "ident_bf": ident_bf[:, :], "before": before[:, :, :]}
        stored = ctx.enter_context(nc.semaphore("stored"))
        loaded = ctx.enter_context(nc.semaphore("loaded"))
        with nc.Block() as block:
            @block.sync
            def _(sp):
                src = io["L0_attn_inputs"].rearrange("b (t p) d -> p (b t) d", p=P)
                for q in range(QUARTERS):
                    sp.dma_start(X[:, q * PER_Q:(q + 1) * PER_Q, :], src[:, q * PER_Q:(q + 1) * PER_Q, :]).then_inc(loaded, 16)
                sp.dma_start(ident[:, :], const["ident"]).then_inc(loaded, 16)
                sp.dma_start(before[:, :, :], const["before"].partition_broadcast(P)).then_inc(loaded, 16)
                sp.wait_ge(loaded, 16 * 6)

            @block.vector
            def _(dve):
                dve.wait_ge(loaded, 16 * 6)
                dve.tensor_copy(ident_bf[:, :], ident[:, :])
        flow_phase(nc, psum, X, C, io, const)
        clear_semaphores(nc)
        gated_attention_phase(nc, psum, X, C, io)
        clear_semaphores(nc)
        narrow_attention_phase(nc, psum, X, C, io)
        clear_semaphores(nc)
        experts_phase(nc, psum, X, C, io, out, stored)


def constants():
    import numpy as np
    eye = np.eye(P, dtype=np.float32)
    row, col = np.arange(P)[:, None], np.arange(P)[None, :]
    row_head = np.where(row % 32 < 16, row % 32, -1)
    token = (row // 32) % 2 * BANK + np.arange(BANK)[None, :] + 1.0
    return {
        "sums_w": (row // 8 == np.arange(32)[None, :] % 16).astype(np.float32),
        "spread": (row_head == col // 8).astype(np.float32),
        "carry_w": ((row + 32 == col) & (row // 32 % 2 == 0)).astype(np.float32),
        "normal": token.astype(np.float32),
        "inv_normal": (1.0 / token).astype(np.float32),
        "causal": (row <= col).astype(np.float32),
        "blocks": (row // 8 == col // 8).astype(np.float32),
        "ident": eye,
        "before": np.tril(np.ones((8, 8), np.float32), -1),
    }


def kernel(**inputs):
    import numpy as _np
    import concourse.bacc as _bacc
    from concourse import mybir as _mybir
    from concourse.bass_utils import run_bass_kernel_spmd as _run

    nc = _bacc.Bacc("TRN2", target_bir_lowering=False, num_devices=1)
    arrays, io, const = {}, {}, {}
    for name, a in inputs.items():
        if name == "L0_attn_attn_mask":
            continue
        a = _np.ascontiguousarray(a)
        arrays[f"in_{name}"] = a
        io[name] = nc.dram_tensor(f"in_{name}", a.shape, _mybir.dt.from_np(a.dtype), kind="ExternalInput").ap()
    for name, a in constants().items():
        arrays[f"const_{name}"] = a
        const[name] = nc.dram_tensor(f"const_{name}", a.shape, _mybir.dt.from_np(a.dtype), kind="ExternalInput").ap()
    out = nc.dram_tensor("out_0", (BATCH, SEQ, D), _mybir.dt.float32, kind="ExternalOutput").ap()
    program(nc, io, const, out)
    r = _run(nc, [arrays], core_ids=[0])
    return r.results[0]["out_0"]
```
